# Optimizing a Trainium2 kernel written in Bass

```python
import numpy as np
import jax
import jax.numpy as jnp

def _softmax(x, axis=-1):
    return jax.nn.softmax(x, axis=axis)

def _gelu(x):
    return jax.nn.gelu(x, approximate=True)

def _silu(x):
    return jax.nn.silu(x)

def _sigmoid(x):
    return jax.nn.sigmoid(x)

def _layernorm(x, axis=-1, eps=1e-05):
    m = jnp.mean(x, axis=axis, keepdims=True)
    v = jnp.var(x, axis=axis, keepdims=True)
    return (x - m) / jnp.sqrt(v + eps)

def _scatter_add(tgt, idx, src, axis=0):
    return tgt.at[idx].add(src)

def _segment_sum(src, seg, n):
    return jax.ops.segment_sum(src, seg, n)
kernel_name = 'mk_xattn_ffn_d1_seqx_r4_7a5432'

def setup_inputs(seed: int=0):
    np.random.seed(seed)
    _w = jnp.asarray

    def _rec_inputs():
        import jax
        import jax.numpy as jnp
        _rk = jax.random.key(seed)
        x = -0.0003929 + 0.9999 * jax.random.normal(jax.random.fold_in(_rk, 1), (32, 112, 256), jnp.float32)
        _lenS = 112 - jax.random.randint(jax.random.fold_in(_rk, 7), (32,), 0, max(1, 112 // 4) + 1, jnp.int32)
        _lenS2 = 375 - jax.random.randint(jax.random.fold_in(_rk, 8), (32,), 0, max(1, 375 // 4) + 1, jnp.int32)
        _ctx_768P = jax.random.normal(jax.random.fold_in(_rk, 11), (32, 16, 192), jnp.float32)
        _ctx_768c = jax.random.dirichlet(jax.random.fold_in(_rk, 511), 0.3 * jnp.ones((16,), jnp.float32), (32, 375))
        _ctx_768t = jnp.einsum('bsk,bkd->bsd', _ctx_768c, _ctx_768P)
        _ctx_768t = _ctx_768t * jax.lax.rsqrt(jnp.mean(jnp.square(_ctx_768t)) + 1e-12) * 0.953939
        ctx_768 = -7.36909e-05 + 0.999899 * (_ctx_768t + 0.3 * jax.random.normal(jax.random.fold_in(_rk, 611), (32, 375, 192), jnp.float32))
        return (x, ctx_768)
    x, ctx_768 = _rec_inputs()

    def _L0_xattn_setup():
        import jax, jax.numpy as jnp
        import numpy as np
        EPS = 1e-05

        def layernorm(x, g, b):
            mu = jnp.mean(x, axis=-1, keepdims=True)
            var = jnp.mean(jnp.square(x - mu), axis=-1, keepdims=True)
            return (x - mu) * jax.lax.rsqrt(var + EPS) * g + b
        key = jax.random.key(seed)
        ks = jax.random.split(key, 12)
        B, L1, L2 = (8, 512, 512)
        D1, D2, E = (256, 192, 256)
        s1, s2, se = (D1 ** (-0.5), D2 ** (-0.5), E ** (-0.5))
        return {'modality1': jax.random.normal(ks[0], (B, L1, D1), jnp.float32), 'modality2': jax.random.normal(ks[1], (B, L2, D2), jnp.float32), 'ln1_g': jnp.ones((D1,), jnp.float32), 'ln1_b': jnp.zeros((D1,), jnp.float32), 'ln2_g': jnp.ones((D2,), jnp.float32), 'ln2_b': jnp.zeros((D2,), jnp.float32), 'Wq': jax.random.normal(ks[2], (D1, E), jnp.float32) * s1, 'bq': jax.random.normal(ks[3], (E,), jnp.float32) * 0.01, 'Wk': jax.random.normal(ks[4], (D2, E), jnp.float32) * s2, 'bk': jax.random.normal(ks[5], (E,), jnp.float32) * 0.01, 'Wv': jax.random.normal(ks[6], (D2, E), jnp.float32) * s2, 'bv': jax.random.normal(ks[7], (E,), jnp.float32) * 0.01, 'Wo': jax.random.normal(ks[8], (E, D1), jnp.float32) * se, 'bo': jax.random.normal(ks[9], (D1,), jnp.float32) * 0.01}
    _L0_xattn_all = _L0_xattn_setup()
    _L0_xattn_in = {k: v for k, v in _L0_xattn_all.items() if k in ('ln1_g', 'ln1_b', 'ln2_g', 'ln2_b', 'Wq', 'bq', 'Wk', 'bk', 'Wv', 'bv', 'Wo', 'bo')}
    del _L0_xattn_all

    def _L0_ffn_setup():
        import jax, jax.numpy as jnp
        import numpy as np
        H = 256
        I = 128
        E = 8
        K = 2
        SI = I * 2
        B, S = (2, 256)

        def _mlp(x, gw, uw, dw):
            return jax.nn.silu(x @ gw.T) * (x @ uw.T) @ dw.T
        key = jax.random.key(seed)
        ks = jax.random.split(key, 9)
        s = 0.02
        return {'x': jax.random.normal(ks[0], (B, S, H), jnp.float32), 'gate_w': jax.random.normal(ks[1], (E, H), jnp.float32) * s, 'lb_bias': jnp.zeros((E,), jnp.float32), 'expert_gate_w': jax.random.normal(ks[2], (E, I, H), jnp.float32) * s, 'expert_up_w': jax.random.normal(ks[3], (E, I, H), jnp.float32) * s, 'expert_down_w': jax.random.normal(ks[4], (E, H, I), jnp.float32) * s, 'shared_gate_w': jax.random.normal(ks[5], (SI, H), jnp.float32) * s, 'shared_up_w': jax.random.normal(ks[6], (SI, H), jnp.float32) * s, 'shared_down_w': jax.random.normal(ks[7], (H, SI), jnp.float32) * s}
    _L0_ffn_all = _L0_ffn_setup()
    _L0_ffn_in = {k: v for k, v in _L0_ffn_all.items() if k in ('gate_w', 'lb_bias', 'expert_gate_w', 'expert_up_w', 'expert_down_w', 'shared_gate_w', 'shared_up_w', 'shared_down_w')}
    del _L0_ffn_all
    return {'x': x, 'ctx_768': ctx_768, 'L0_xattn_ln1_g': _L0_xattn_in['ln1_g'], 'L0_xattn_ln1_b': _L0_xattn_in['ln1_b'], 'L0_xattn_ln2_g': _L0_xattn_in['ln2_g'], 'L0_xattn_ln2_b': _L0_xattn_in['ln2_b'], 'L0_xattn_Wq': _L0_xattn_in['Wq'], 'L0_xattn_bq': _L0_xattn_in['bq'], 'L0_xattn_Wk': _L0_xattn_in['Wk'], 'L0_xattn_bk': _L0_xattn_in['bk'], 'L0_xattn_Wv': _L0_xattn_in['Wv'], 'L0_xattn_bv': _L0_xattn_in['bv'], 'L0_xattn_Wo': _L0_xattn_in['Wo'], 'L0_xattn_bo': _L0_xattn_in['bo'], 'L0_ffn_gate_w': _L0_ffn_in['gate_w'], 'L0_ffn_lb_bias': _L0_ffn_in['lb_bias'], 'L0_ffn_expert_gate_w': _L0_ffn_in['expert_gate_w'], 'L0_ffn_expert_up_w': _L0_ffn_in['expert_up_w'], 'L0_ffn_expert_down_w': _L0_ffn_in['expert_down_w'], 'L0_ffn_shared_gate_w': _L0_ffn_in['shared_gate_w'], 'L0_ffn_shared_up_w': _L0_ffn_in['shared_up_w'], 'L0_ffn_shared_down_w': _L0_ffn_in['shared_down_w']}

def reference(x, ctx_768, L0_xattn_ln1_g, L0_xattn_ln1_b, L0_xattn_ln2_g, L0_xattn_ln2_b, L0_xattn_Wq, L0_xattn_bq, L0_xattn_Wk, L0_xattn_bk, L0_xattn_Wv, L0_xattn_bv, L0_xattn_Wo, L0_xattn_bo, L0_ffn_gate_w, L0_ffn_lb_bias, L0_ffn_expert_gate_w, L0_ffn_expert_up_w, L0_ffn_expert_down_w, L0_ffn_shared_gate_w, L0_ffn_shared_up_w, L0_ffn_shared_down_w):
    import jax
    import jax.numpy as jnp

    def _L0_xattn_ref(modality1, modality2, ln1_g, ln1_b, ln2_g, ln2_b, Wq, bq, Wk, bk, Wv, bv, Wo, bo):
        import jax, jax.numpy as jnp
        import numpy as np
        EPS = 1e-05

        def layernorm(x, g, b):
            mu = jnp.mean(x, axis=-1, keepdims=True)
            var = jnp.mean(jnp.square(x - mu), axis=-1, keepdims=True)
            return (x - mu) * jax.lax.rsqrt(var + EPS) * g + b
        E = Wq.shape[1]
        scaling = E ** (-0.5)
        x1 = layernorm(modality1, ln1_g, ln1_b)
        x2 = layernorm(modality2, ln2_g, ln2_b)
        q = x1 @ Wq + bq
        k = x2 @ Wk + bk
        v = x2 @ Wv + bv
        scores = jnp.einsum('bqe,bke->bqk', q, k) * scaling
        attn = jax.nn.softmax(scores, axis=-1)
        ctx = jnp.einsum('bqk,bke->bqe', attn, v)
        return ctx @ Wo + bo

    def _L0_ffn_ref(x, gate_w, lb_bias, expert_gate_w, expert_up_w, expert_down_w, shared_gate_w, shared_up_w, shared_down_w):
        import jax, jax.numpy as jnp
        import numpy as np
        H = 256
        I = 128
        E = 8
        K = 2
        SI = I * 2
        B, S = (2, 256)

        def _mlp(x, gw, uw, dw):
            return jax.nn.silu(x @ gw.T) * (x @ uw.T) @ dw.T
        b, s, h = x.shape
        xf = x.reshape(-1, h)
        logits = xf @ gate_w.T + lb_bias
        scores = jax.nn.sigmoid(logits.astype(jnp.float32))
        topw, topi = jax.lax.top_k(scores, K)
        topw = (topw / (topw.sum(-1, keepdims=True) + 1e-08)).astype(x.dtype)
        out = jnp.zeros_like(xf)
        for e in range(E):
            m = topi == e
            sel = m.any(axis=-1)
            cnt = m.sum()
            wmean = (topw * m).sum() / jnp.maximum(cnt, 1).astype(topw.dtype)
            y = _mlp(xf, expert_gate_w[e], expert_up_w[e], expert_down_w[e])
            out = out + jnp.where(sel[:, None], y * wmean, jnp.zeros((), x.dtype))
        out = out.reshape(b, s, h)
        out = out + _mlp(x, shared_gate_w, shared_up_w, shared_down_w)
        return out
    x = x + _L0_xattn_ref(_layernorm(x, axis=-1), ctx_768, L0_xattn_ln1_g, L0_xattn_ln1_b, L0_xattn_ln2_g, L0_xattn_ln2_b, L0_xattn_Wq, L0_xattn_bq, L0_xattn_Wk, L0_xattn_bk, L0_xattn_Wv, L0_xattn_bv, L0_xattn_Wo, L0_xattn_bo)
    x = x + _L0_ffn_ref(_layernorm(x, axis=-1), L0_ffn_gate_w, L0_ffn_lb_bias, L0_ffn_expert_gate_w, L0_ffn_expert_up_w, L0_ffn_expert_down_w, L0_ffn_shared_gate_w, L0_ffn_shared_up_w, L0_ffn_shared_down_w)
    return x

_drawn_inputs = setup_inputs


def setup_inputs(seed=0):
    import zlib

    import numpy as np

    out = dict(_drawn_inputs(seed))
    spreads = {'L0_xattn_ln1_g': (1.0, 0.2),
     'L0_xattn_ln1_b': (0.0, 0.428),
     'L0_xattn_ln2_g': (1.0, 0.2),
     'L0_xattn_ln2_b': (0.0, 0.1),
     'L0_ffn_lb_bias': (0.0, 0.8)}
    factors = {'L0_xattn_bq': 8.0,
     'L0_xattn_bk': 8.0,
     'L0_xattn_bv': 6.719,
     'L0_xattn_bo': 6.341,
     'L0_ffn_gate_w': 8.0,
     'L0_ffn_expert_gate_w': 7.834,
     'L0_ffn_expert_up_w': 7.705,
     'L0_ffn_expert_down_w': 7.742,
     'L0_ffn_shared_gate_w': 3.915,
     'L0_ffn_shared_up_w': 3.888,
     'L0_ffn_shared_down_w': 3.87}
    for name, (base, spread) in spreads.items():
        noise = np.random.default_rng([zlib.crc32(name.encode()), seed]).standard_normal(out[name].shape)
        drawn = base * np.exp(spread * noise) if base else spread * noise
        out[name] = jnp.asarray(drawn.astype(out[name].dtype))
    for name, factor in factors.items():
        out[name] = (out[name] * factor).astype(out[name].dtype)
    return out
```

```python
from contextlib import ExitStack

import concourse.bass as bass
from concourse import mybir

F32 = mybir.dt.float32
F32R = mybir.dt.float32r
BF16 = mybir.dt.bfloat16
ALU = mybir.AluOpType
ACT = mybir.ActivationFunctionType
AX = mybir.AxisListType

EPS = 1e-5
OFF = -(2.0 ** 64)

GROUP = 4
LEAD = 10


def attention_and_experts(nc, x, ctx_in, wq_t, wq, wk_t, wk, wv_t, wv, wo, g2_rows, columns, b2_columns,
                          bo, gate_w_t, lb_rows, gate_up_t, down_t, out):
    B, T, D = x.shape
    K, DC = ctx_in.shape[1:]
    KT = 3
    KP = K // KT
    DT = D // 128
    FA = DC + 2
    FH = FA // 2
    E = lb_rows.shape[1]
    UNITS = down_t.shape[1]
    SHARED = UNITS - E
    BLOCK = GROUP * T
    NB = B // GROUP
    TURNS = NB - 4
    LAST = 42
    SCALE = float(D) ** -0.5
    CHUNKS = 8
    CHUNK = gate_up_t.shape[1] // CHUNKS
    assert T * GROUP == BLOCK and KP * KT == K and LEAD + GROUP * TURNS + 5 <= B

    x_rows = x.rearrange("b t d -> t b d")
    out_rows = out.rearrange("b t d -> t b d")
    ctx_rows = ctx_in.rearrange("b (p t) d -> p b t d", t=KT)

    top = ExitStack()
    with top:
        def sb(name, shape, dt=F32, where=top):
            return where.enter_context(nc.sbuf_tensor(name, shape, dt))

        def sem(name):
            return top.enter_context(nc.semaphore(name))

        X = sb("x_sb", [T, B, D])
        XH = sb("xn_hi", [128, DT, B * T], F32R)
        XL = sb("xn_lo", [128, DT, B * T], F32R)
        GUH = sb("gate_up_hi", [128, 2 * DT * UNITS, 128], F32R)
        GUL = sb("gate_up_lo", [128, 2 * DT * UNITS, 128], F32R)
        ROUTE = sb("route", [T, 2, B, E])
        OFFT = sb("off_tokens", [128, B * T], BF16)
        OFFSEL = sb("off_select", [128, E, 128], BF16)
        ONES = sb("ones", [T, 128])

        one = ExitStack()
        with one:
            def s1(name, shape, dt=F32):
                return sb(name, shape, dt, one)

            G2 = s1("g2_sb", [128, DC])
            COL = s1("columns_sb", [128, 5, DT])
            B2C = s1("b2_columns_sb", [DC // 2, 2])
            LBR = s1("lb_rows_sb", [T, E])
            GW = s1("gate_w_sb", [128, DT, E])
            WKA = s1("wk_aug", [128, DT, FA])
            WVA = s1("wv_aug", [128, DT, FA])
            G1S = s1("g1_scaled", [128, DT])
            TQ = s1("q_bias", [128, DT])
            A = s1("a_sb", [128, DT, FA])
            C = s1("c_sb", [FH, 2])
            VO = s1("vo_sb", [FH, 2, D])
            ID = s1("identity", [128, 128])
            IDB = s1("identity_bf", [T, T], BF16)
            BEFORE = s1("before", [T, E, E])
            HALF = s1("minus_half", [128, 5])
            STG = s1("stage", [128, 2, CHUNK])

            RAW = s1("ctx_raw", [KP, 4, KT, DC])
            X2N = s1("ctx_norm", [KP, 4, KT, FA])
            N1 = s1("x_norm", [T, 4, D])
            X1T = s1("x_norm_t", [128, DT, 2 * T])
            QT = s1("q_t", [FH, 2, 2, 2 * T])
            X2T = s1("ctx_norm_t", [FH, 2, 2, K])
            P = s1("probs", [T, 2, K])
            PT = s1("probs_t", [KP, 2, KT, T])
            CT = s1("context_t", [FH, 2, 2, T])
            XN = s1("x2_norm", [T, 2, D])
            XNS = s1("xn_t", [128, DT, BLOCK])
            ST = s1("stats", [128, 5, 6])
            MV = s1("mean_var", [128, 4, 5, 2])
            VE = s1("var_eps", [128, 4, 5])
            RS = s1("rstd", [128, 4, 5])
            NM = s1("minus_mean_rstd", [128, 4, 5])
            NMAX = s1("minus_max", [T, 4])
            L = s1("row_sum", [T, 4])
            RL = s1("row_sum_inv", [T, 4])
            LG = s1("logits_sb", [T, GROUP, E])
            EX = s1("exp_minus", [T, GROUP, E])
            EX1 = s1("one_plus_exp", [T, GROUP, E])
            SC = s1("route_scores", [T, GROUP, E])
            GT = s1("greater", [T, GROUP, E, E])
            GE = s1("greater_equal", [T, GROUP, E, E])
            EQ = s1("equal", [T, GROUP, E, E])
            EQB = s1("equal_before", [T, GROUP, E, E])
            AHEAD = s1("is_ahead", [T, GROUP, E, E])
            SUM4 = s1("ahead_sum4", [T, GROUP, E, 4])
            SUM2 = s1("ahead_sum2", [T, GROUP, E, 2])
            RK = s1("rank", [T, GROUP, E])
            OFFB = s1("off_bf", [T, GROUP, 128], BF16)
            SS = s1("selected_scores", [T, GROUP, E])
            SM = s1("score_sum", [T, GROUP])
            SE = s1("score_sum_eps", [T, GROUP])
            SI = s1("score_sum_inv", [T, GROUP])

            spare = XNS[:, :, :].rearrange("p a b -> p (a b)")
            WQT = spare[:, 0:DT * D].rearrange("p (t n) -> p t n", t=DT)
            WKT = spare[:, DT * D:DT * (D + DC)].rearrange("p (t n) -> p t n", t=DT)
            WVT = X1T[:, :, :].rearrange("p a b -> p (a b)")[:, 0:DT * DC].rearrange("p (t n) -> p t n", t=DT)
            WQ = STG[:, 0, 0:DT * D].rearrange("p (t n) -> p t n", t=DT)
            WO = STG[:, 1, 0:DT * D].rearrange("p (t n) -> p t n", t=DT)
            WK = N1[0:DC // 2, 0:2, :]
            WV = N1[0:DC // 2, 2:4, :]

            x2t_ps = one.enter_context(nc.psum_tensor("x2t_ps", [128, 2, 512], F32))
            s_ps = one.enter_context(nc.psum_tensor("s_ps", [128, 512], F32))
            pt_ps = one.enter_context(nc.psum_tensor("pt_ps", [128, 512], F32))
            ct_ps = one.enter_context(nc.psum_tensor("ct_ps", [128, 512], F32))
            o_ps = one.enter_context(nc.psum_tensor("o_ps", [128, 512], F32))
            tr_ps = one.enter_context(nc.psum_tensor("tr_ps", [128, 512], F32))
            q_ps = one.enter_context(nc.psum_tensor("q_ps", [128, 512], F32))
            LOGITS = 2 * 2 * T

            setup_full = sem("setup_full")
            bo_full = sem("bo_full")
            x_first = sem("x_first")
            x_rest = sem("x_rest")
            raw_full = [sem(f"raw_full{j}") for j in range(4)]
            stage_full = [sem(f"stage_full{j}") for j in range(2)]
            made = sem("made_by_pool")
            cleared = sem("cleared")
            bias_done = sem("bias_done")
            aug_done = sem("aug_done")
            fold_done = sem("fold_done")
            folded = sem("folded")
            vo_ready = sem("vo_ready")
            vec_made = sem("made_by_vector")
            ctx_stats = sem("ctx_stats")
            ctx_mv = sem("ctx_mv")
            x_stats = sem("x_stats")
            x_mv = sem("x_mv")
            x2_stats = sem("x2_stats")
            x2_mv = sem("x2_mv")
            var_ready = sem("var_ready")
            rstd_ready = sem("rstd_ready")
            nm_ready = sem("nm_ready")
            ctx_ready = sem("ctx_norm_ready")
            n1_ready = sem("n1_ready")
            x1t_done = sem("x1t_done")
            x1t_ready = sem("x1t_ready")
            q_done = sem("q_done")
            q_ready = sem("q_ready")
            x2t_done = sem("x2t_done")
            x2t_ready = sem("x2t_ready")
            s_done = sem("s_done")
            max_ready = sem("max_ready")
            exp_ready = sem("exp_ready")
            inv_ready = sem("inv_ready")
            pt_done = sem("pt_done")
            pt_ready = sem("pt_ready")
            ct_done = sem("ct_done")
            ct_ready = sem("ct_ready")
            o_done = sem("o_done")
            xmid_ready = sem("xmid_ready")
            xn_ready = sem("xn_ready")
            xnt_done = sem("xnt_done")
            xnt_ready = sem("xnt_ready")
            xlo_ready = sem("xlo_ready")
            lg_done = sem("lg_done")
            lg_ready = sem("lg_ready")
            negexp_ready = sem("negexp_ready")
            denominator = sem("sigmoid_denominator")
            scored = sem("scored")
            compared = sem("compared")
            ranking = sem("ranking")
            ranked = sem("ranked")
            routing = sem("routing")
            route_ready = sem("route_ready")
            off_done = sem("off_done")
            off_ready = sem("off_ready")
            whi_ready = sem("whi_ready")
            wlo_ready = sem("wlo_ready")
            passed = sem("passed_a_wait")

            def need(eng, s, n, r, top_value, per=GROUP, apart=False):
                if isinstance(r, int):
                    n = min(n, top_value)
                    if n > 0:
                        eng.wait_ge(s, n)
                elif apart:
                    assert n > 0
                    eng.wait_ge(s, n + per * r)
                    eng.sem_inc(passed, 1)
                else:
                    assert n > 0
                    eng.wait_ge(s, n + per * r)

            def valid(b):
                return 0 <= b < B

            def steps(eng, step):
                for i in range(-5, LEAD):
                    step(i, 0)
                with eng.Fori(0, TURNS) as r:
                    for i in range(LEAD, LEAD + GROUP):
                        step(i, r)
                for i in range(LEAD + GROUP * TURNS, LAST):
                    step(i, 0)

            N_SETUP = 12
            block = one.enter_context(nc.Block())

            @block.sync
            def _(sp):
                sp.dma_start(X[:, 0:GROUP, :], x_rows[:, 0:GROUP, :]).then_inc(x_first, 16)
                for j in range(4):
                    sp.dma_start(RAW[:, j, :, :], ctx_rows[:, j, :, :]).then_inc(raw_full[j], 16)
                two = lambda a: a.rearrange("(t p) n -> p t n", t=2)
                for dst, src in ((WQT[:, :, :], two(wq_t)), (WQ[:, :, :], two(wq)), (WKT[:, :, :], two(wk_t)),
                                 (WVT[:, :, :], two(wv_t)), (WK[:, :, :], two(wk)), (WV[:, :, :], two(wv)),
                                 (WO[:, :, :], two(wo)), (G2[:, :], g2_rows), (COL[:, :, :], columns),
                                 (B2C[:, :], b2_columns), (LBR[:, :], lb_rows), (GW[:, :, :], two(gate_w_t))):
                    sp.dma_start(dst, src).then_inc(setup_full, 16)
                sp.dma_start(X[:, GROUP:B, :], x_rows[:, GROUP:B, :]).then_inc(x_rest, 16)
                sp.wait_ge(vo_ready, 2)
                sp.dma_start(VO[FH - 1:FH, 1, :], bo).then_inc(bo_full, 16)
                for k in range(CHUNKS):
                    sp.wait_ge(ctx_ready, KT * (k + 1))
                    sp.dma_start(RAW[:, k % 4, :, :], ctx_rows[:, GROUP + k, :, :]).then_inc(raw_full[k % 4], 16)
                    if k >= 2:
                        sp.wait_ge(wlo_ready, k - 1)
                    sp.dma_start(STG[:, k % 2, :], gate_up_t[:, k * CHUNK:(k + 1) * CHUNK])\
                        .then_inc(stage_full[k % 2], 16)
                with sp.Fori(0, NB - 3) as r:
                    for j in range(GROUP):
                        sp.wait_ge(ctx_ready, KT * (CHUNKS + 1 + j) + KT * GROUP * r)
                        sp.dma_start(RAW[:, j, :, :], ctx_rows[:, GROUP + CHUNKS + j + GROUP * r, :, :])\
                            .then_inc(raw_full[j], 16)
                sp.wait_ge(bo_full, 16)

            @block.gpsimd
            def _(pool):
                nc.gpsimd.memset(ID[:, :], 0.0).then_inc(cleared, 1)
                nc.gpsimd.memset(BEFORE[:, :, :], 1.0).then_inc(cleared, 1)
                nc.gpsimd.memset(OFFSEL[:, :, :], 0.0).then_inc(cleared, 1)
                nc.gpsimd.memset(HALF[:, :], -0.5).then_inc(made, 1)
                pool.wait_ge(cleared, 3)
                nc.gpsimd.affine_select(out=ID[:, :], in_=ID[:, :], compare_op=ALU.not_equal, fill=1.0, base=0,
                                        pattern=[[-1, 128]], channel_multiplier=1).then_inc(made, 1)
                nc.gpsimd.affine_select(out=BEFORE[:, :, :], in_=BEFORE[:, :, :], compare_op=ALU.is_gt, fill=0.0,
                                        base=0, pattern=[[1, E], [-1, E]], channel_multiplier=0).then_inc(made, 1)
                nc.gpsimd.affine_select(out=OFFSEL[:, :, :], in_=OFFSEL[:, :, :], compare_op=ALU.not_equal, fill=OFF,
                                        base=0, pattern=[[-1, E], [0, 128]], channel_multiplier=1).then_inc(made, 1)
                pool.wait_ge(made, 4)

                pool.sem_inc(ranked, 1)

                def rank(s, r):
                    def then(k):
                        need(pool, ranking, 5 * s + k, r, 10 ** 6, 5)

                    need(pool, compared, 2 * s + 2, r, 2 * NB, 2)
                    nc.gpsimd.tensor_tensor(EQ[:, :, :, :], GE[:, :, :, :], GT[:, :, :, :], ALU.subtract)\
                        .then_inc(ranking, 1)
                    then(1)
                    nc.gpsimd.tensor_tensor(EQB[:, :, :, :], EQ[:, :, :, :],
                                            BEFORE[:, :, :].unsqueeze(1).broadcast_to([T, GROUP, E, E]),
                                            ALU.mult).then_inc(ranking, 1)
                    then(2)
                    nc.gpsimd.tensor_tensor(AHEAD[:, :, :, :], GT[:, :, :, :], EQB[:, :, :, :], ALU.add)\
                        .then_inc(ranking, 1)
                    then(3)
                    nc.gpsimd.tensor_tensor(SUM4[:, :, :, :], AHEAD[:, :, :, 0:4], AHEAD[:, :, :, 4:8], ALU.add)\
                        .then_inc(ranking, 1)
                    then(4)
                    nc.gpsimd.tensor_tensor(SUM2[:, :, :, :], SUM4[:, :, :, 0:2], SUM4[:, :, :, 2:4], ALU.add)\
                        .then_inc(ranking, 1)
                    then(5)
                    nc.gpsimd.tensor_tensor(RK[:, :, :], SUM2[:, :, :, 0], SUM2[:, :, :, 1], ALU.add)\
                        .then_inc(ranked, 1)

                def step(i, r):
                    j = i % 4
                    if -4 <= i <= B + 2:
                        need(pool, var_ready, 2 * (i + 5), r, 10 ** 6, 2 * GROUP)
                        need(pool, n1_ready, i + 1, r, B)
                        need(pool, xn_ready, i - 6, r, B)
                        nc.gpsimd.tensor_tensor(RS[:, j, :], VE[:, j, :], HALF[:, :], ALU.pow).then_inc(rstd_ready, 1)
                    if valid(i + 3):
                        need(pool, nm_ready, i + 5, r, 10 ** 6)
                        need(pool, ct_done, i, r, B)
                        need(pool, raw_full[(i + 3) % 4], 16 * ((i + 3) // 4 + 1), r, 10 ** 6, 16, apart=True)
                        for t in range(KT):
                            nc.gpsimd.tensor_scalar(X2N[:, (i + 3) % 4, t, 0:DC], RAW[:, (i + 3) % 4, t, :],
                                                    RS[0:KP, j, t:t + 1], NM[0:KP, j, t:t + 1],
                                                    ALU.mult, ALU.add).then_inc(ctx_ready, 1)
                    if isinstance(r, int) and 0 <= i < CHUNKS:
                        pool.wait_ge(whi_ready, i + 1)
                        n = CHUNK // 128
                        nc.gpsimd.tensor_tensor(GUL[:, i * n:(i + 1) * n, :],
                                                STG[:, i % 2, :].rearrange("p (a b) -> p a b", b=128),
                                                GUH[:, i * n:(i + 1) * n, :].bitcast(F32),
                                                ALU.subtract).then_inc(wlo_ready, 1)
                    if valid(i - 5):
                        b = i - 5
                        need(pool, xnt_ready, 2 * (b + 1), r, 2 * B, 2 * GROUP)
                        at = bass.ds(b * T + r * BLOCK, T)
                        nc.gpsimd.tensor_tensor(XL[:, :, at], XNS[:, :, (b % 4) * T:(b % 4 + 1) * T],
                                                XH[:, :, at].bitcast(F32), ALU.subtract).then_inc(xlo_ready, 1)

                    if i % 4 == 3 and 11 <= i < 11 + B:
                        rank((i - 11) // 4, r)

                steps(pool, step)

            @block.vector
            def _(dve):
                nc.vector.memset(ONES[:, :], 1.0).then_inc(vec_made, 1)
                nc.vector.memset(MV[:, :, :, :], 1.0).then_inc(vec_made, 1)
                nc.vector.memset(OFFB[:, :, :], 0.0).then_inc(vec_made, 1)
                nc.vector.memset(WVA[:, :, FA - 1:FA], 0.0).then_inc(vec_made, 1)
                nc.vector.memset(WKA[:, :, FA - 1:FA], 0.0).then_inc(vec_made, 1)
                nc.vector.memset(X2N[:, :, :, DC:FA], 1.0).then_inc(vec_made, 1)
                dve.wait_ge(made, 4)
                nc.vector.tensor_copy(IDB[:, :], ID[0:T, 0:T]).then_inc(vec_made, 1)
                dve.wait_ge(vec_made, 7)

                def norms(i, r):
                    m = (i + 1) % 4
                    if valid(i + 4):
                        need(dve, raw_full[(i + 4) % 4], 16 * ((i + 4) // 4 + 1), r, 10 ** 6, 16)
                        for t in range(KT):
                            nc.vector.bn_stats(ST[0:KP, t, :], RAW[:, (i + 4) % 4, t, :]).then_inc(ctx_stats, 1)
                    if valid(i + 5):
                        if i + 5 < GROUP:
                            dve.wait_ge(x_first, 16)
                        else:
                            dve.wait_ge(x_rest, 16)
                        nc.vector.bn_stats(ST[0:T, 4, :], X[:, i + 5 + GROUP * r, :]).then_inc(x_stats, 1)
                    if valid(i - 2):
                        need(dve, xmid_ready, i - 1, r, B, apart=True)
                        nc.vector.bn_stats(ST[0:T, 3, :], X[:, i - 2 + GROUP * r, :]).then_inc(x2_stats, 1)
                    if valid(i + 4):
                        need(dve, ctx_stats, KT * (i + 5), r, KT * B, KT * GROUP, apart=True)
                        for t in range(KT):
                            nc.vector.bn_aggr(MV[0:KP, m, t, :], ST[0:KP, t, :]).then_inc(ctx_mv, 1)
                    if valid(i + 5):
                        need(dve, x_stats, i + 6, r, B, apart=True)
                        nc.vector.bn_aggr(MV[0:T, m, 4, :], ST[0:T, 4, :]).then_inc(x_mv, 1)
                    if valid(i - 2):
                        need(dve, x2_stats, i - 1, r, B, apart=True)
                        nc.vector.bn_aggr(MV[0:T, m, 3, :], ST[0:T, 3, :]).then_inc(x2_mv, 1)
                    if -4 <= i + 1 <= B + 2:
                        need(dve, ctx_mv, KT * (i + 5), r, KT * B, KT * GROUP)
                        need(dve, x_mv, i + 6, r, B)
                        need(dve, x2_mv, i - 1, r, B)
                        need(dve, rstd_ready, i + 2, r, 10 ** 6)
                        nc.vector.tensor_scalar(VE[:, m, 0:4], MV[:, m, 0:4, 1], EPS, None, ALU.add)\
                            .then_inc(var_ready, 1)
                        nc.vector.tensor_scalar(VE[:, m, 4:5], MV[:, m, 4:5, 1], 1.0 + EPS, EPS * EPS, ALU.mult,
                                                ALU.add).then_inc(var_ready, 1)

                dve.sem_inc(off_ready, 1)
                dve.wait_ge(setup_full, 16 * N_SETUP)
                g2b = G2[:, :].unsqueeze(1).broadcast_to([128, DT, DC])
                nc.vector.tensor_tensor(WKA[:, :, 0:DC], WKT[:, :, :], g2b, ALU.mult).then_inc(aug_done, 1)
                nc.vector.tensor_tensor(WVA[:, :, 0:DC], WVT[:, :, :], g2b, ALU.mult).then_inc(aug_done, 1)
                nc.vector.tensor_scalar(G1S[:, :], COL[:, 0, :], SCALE, None, ALU.mult).then_inc(aug_done, 1)
                dve.wait_ge(bias_done, 1)
                nc.vector.tensor_tensor(TQ[:, :], tr_ps[:, 0:2], COL[:, 2, :], ALU.add).then_inc(aug_done, 1)
                nc.vector.tensor_tensor(WKA[:, :, DC], tr_ps[:, 2:4], COL[:, 3, :], ALU.add).then_inc(aug_done, 1)
                nc.vector.tensor_tensor(WVA[:, :, DC], tr_ps[:, 4:6], COL[:, 4, :], ALU.add).then_inc(aug_done, 1)
                dve.wait_ge(fold_done, 1)
                dve.wait_ge(aug_done, 6)
                for dt in range(DT):
                    nc.vector.tensor_scalar(A[:, dt, :], x2t_ps[:, dt, 0:FA], G1S[:, dt:dt + 1], None, ALU.mult)\
                        .then_inc(folded, 1)
                nc.vector.tensor_scalar(C[:, :], q_ps[0:FH, 0:2], SCALE, None, ALU.mult).then_inc(folded, 1)
                nc.vector.tensor_copy(VO[:, 0, :], ct_ps[0:FH, 0:D]).then_inc(vo_ready, 1)
                nc.vector.tensor_copy(VO[:, 1, :], o_ps[0:FH, 0:D]).then_inc(vo_ready, 1)
                dve.sem_inc(off_ready, 1)
                def score(s, r):
                    need(dve, negexp_ready, s + 2, r, NB + 1, 1)
                    nc.vector.tensor_scalar(EX1[:, :, :], EX[:, :, :], 1.0, None, ALU.add).then_inc(denominator, 1)
                    need(dve, denominator, s + 1, r, NB, 1)
                    need(dve, ranked, s + 1, r, NB + 1, 1)
                    nc.vector.reciprocal(SC[:, :, :], EX1[:, :, :]).then_inc(scored, 1)
                    need(dve, scored, s + 1, r, NB, 1)
                    of_j = SC[:, :, :].unsqueeze(2).broadcast_to([T, GROUP, E, E])
                    of_e = SC[:, :, :].unsqueeze(3).broadcast_to([T, GROUP, E, E])
                    nc.vector.tensor_tensor(GT[:, :, :, :], of_j, of_e, ALU.is_gt).then_inc(compared, 1)
                    nc.vector.tensor_tensor(GE[:, :, :, :], of_j, of_e, ALU.is_ge).then_inc(compared, 1)

                R = 3

                def route(s, r):
                    def then(k):
                        need(dve, routing, R * s + k, r, 10 ** 6, R)

                    need(dve, ranked, s + 2, r, NB + 1, 1)
                    need(dve, off_done, s + 1, r, NB + 1, 1)
                    blk = bass.ds(s * GROUP + r * GROUP, GROUP)
                    nc.vector.tensor_scalar(OFFB[:, :, 0:E], RK[:, :, :], 1.5, None, ALU.is_gt)\
                        .then_inc(route_ready, 1)
                    nc.vector.scalar_tensor_tensor(out=SS[:, :, :], in0=RK[:, :, :], scalar=1.5, in1=SC[:, :, :],
                                                   op0=ALU.is_lt, op1=ALU.mult).then_inc(routing, 1)
                    nc.vector.tensor_scalar(ROUTE[:, 1, blk, :], RK[:, :, :], 1.5, None, ALU.is_lt)\
                        .then_inc(route_ready, 1)
                    then(1)
                    nc.vector.tensor_reduce(SM[:, :], SS[:, :, :], AX.X, ALU.add).then_inc(routing, 1)
                    then(2)
                    nc.vector.tensor_scalar(SE[:, :], SM[:, :], 1e-8, None, ALU.add).then_inc(routing, 1)
                    then(3)
                    nc.vector.reciprocal(SI[:, :], SE[:, :]).then_inc(route_ready, 1)
                    need(dve, route_ready, 4 * s + 3, r, 10 ** 6, 4)
                    nc.vector.tensor_tensor(ROUTE[:, 0, blk, :], SS[:, :, :],
                                            SI[:, :].unsqueeze(2).broadcast_to([T, GROUP, E]), ALU.mult)\
                        .then_inc(route_ready, 1)

                def step(i, r):
                    if i % 2 == 0 and valid(i - 8):
                        p = (i - 8) // 2
                        need(dve, lg_done, p + 1, r, B // 2, 2)
                        need(dve, negexp_ready, p // 2 + 1, r, NB + 1, 1)
                        nc.vector.tensor_tensor(LG[:, 2 * (p % 2):2 * (p % 2) + 2, :],
                                                q_ps[0:T, LOGITS:LOGITS + 2 * E].rearrange("p (a e) -> p a e", e=E),
                                                LBR[:, :].unsqueeze(1).broadcast_to([T, 2, E]), ALU.add)\
                            .then_inc(lg_ready, 1)
                    if valid(i - 2):
                        need(dve, exp_ready, i - 1, r, B)
                        nc.vector.reciprocal(RL[:, (i - 2) % 4:(i - 2) % 4 + 1], L[:, (i - 2) % 4:(i - 2) % 4 + 1])\
                            .then_inc(inv_ready, 1)
                    if valid(i + 1):
                        need(dve, s_done, i + 2, r, B)
                        nc.vector.tensor_reduce(NMAX[:, (i + 1) % 4:(i + 1) % 4 + 1], s_ps[0:T, 0:K], AX.X, ALU.max,
                                                negate=True).then_inc(max_ready, 1)
                    if -4 <= i <= B + 2:
                        need(dve, rstd_ready, i + 5, r, 10 ** 6)
                        need(dve, n1_ready, i + 1, r, B)
                        need(dve, xn_ready, i - 6, r, B)
                        need(dve, ctx_ready, KT * i, r, KT * B, KT * GROUP)
                        nc.vector.scalar_tensor_tensor(out=NM[:, i % 4, :], in0=MV[:, i % 4, :, 0], scalar=-1.0,
                                                       in1=RS[:, i % 4, :], op0=ALU.mult, op1=ALU.mult)\
                            .then_inc(nm_ready, 1)
                    if valid(i):
                        need(dve, pt_done, i + 1, r, B)
                        need(dve, ct_done, i - 1, r, B)
                        nc.vector.tensor_copy(PT[:, i % 2, :, :].rearrange("p a b -> p (a b)"), pt_ps[0:KP, 0:KT * T])\
                            .then_inc(pt_ready, 1)
                    if valid(i - 2):
                        b = i - 2
                        need(dve, inv_ready, b + 1, r, B)
                        need(dve, o_done, b + 1, r, B)
                        nc.vector.scalar_tensor_tensor(out=X[:, b + GROUP * r, :], in0=o_ps[0:T, 0:D],
                                                       scalar=RL[:, b % 4:b % 4 + 1], in1=X[:, b + GROUP * r, :],
                                                       op0=ALU.mult, op1=ALU.add).then_inc(xmid_ready, 1)
                    norms(i, r)
                    if i % 4 == 2 and 10 <= i < 10 + B:
                        score((i - 10) // 4, r)
                    if i % 4 == 0 and 12 <= i < 12 + B:
                        route((i - 12) // 4, r)
                    if i % 4 == 1 and 13 <= i < 13 + B:
                        s = (i - 13) // 4
                        need(dve, off_done, s + 2, r, NB + 1, 1)
                        nc.vector.tensor_copy(OFFT[:, bass.ds(s * BLOCK + r * BLOCK, BLOCK)], q_ps[:, 0:BLOCK])\
                            .then_inc(off_ready, 1)

                steps(dve, step)

            @block.scalar
            def _(act):
                def step(i, r):
                    j = i % 4
                    if i % 2 == 0 and valid(i + 2):
                        p = (i + 2) // 2
                        need(act, x1t_done, p + 1, r, B // 2, 2)
                        need(act, q_done, p, r, B // 2, 2)
                        nc.scalar.activation(X1T[:, :, :].rearrange("p a b -> p (a b)"), tr_ps[:, 0:4 * T], ACT.Copy)\
                            .then_inc(x1t_ready, 1)
                    if valid(i + 2):
                        need(act, x2t_done, i + 3, r, B)
                        need(act, s_done, i + 1, r, B)
                        nc.scalar.activation(X2T[:, i % 2, :, :], x2t_ps[0:FH, :, 0:K], ACT.Copy)\
                            .then_inc(x2t_ready, 1)
                    if i % 2 == 0 and valid(i + 2):
                        p = (i + 2) // 2
                        need(act, q_done, p + 1, r, B // 2, 2)
                        need(act, s_done, i, r, B)
                        for h in range(2):
                            nc.scalar.activation(QT[:, p % 2, h, :], q_ps[0:FH, h * 2 * T:(h + 1) * 2 * T],
                                                 ACT.Identity, bias=C[:, h:h + 1]).then_inc(q_ready, 1)
                    if valid(i - 4):
                        b = i - 4
                        need(act, xnt_done, b + 1, r, B)
                        need(act, xlo_ready, b - 3, r, B)
                        need(act, lg_done, (b - 4) // 2 + 1, r, B // 2, 2)
                        nc.scalar.activation(XH[:, :, bass.ds(b * T + r * BLOCK, T)],
                                             tr_ps[:, 0:2 * T].rearrange("p (a b) -> p a b", b=T), ACT.Copy)\
                            .then_inc(xnt_ready, 1)
                        nc.scalar.activation(XNS[:, :, (b % 4) * T:(b % 4 + 1) * T],
                                             tr_ps[:, 0:2 * T].rearrange("p (a b) -> p a b", b=T), ACT.Copy)\
                            .then_inc(xnt_ready, 1)
                    if valid(i + 1):
                        need(act, max_ready, i + 2, r, B)
                        need(act, pt_done, i, r, B)
                        need(act, inv_ready, i - 2, r, B)
                        nc.scalar.activation(P[:, (i + 1) % 2, :], s_ps[0:T, 0:K], ACT.Exp,
                                             bias=NMAX[:, (i + 1) % 4:(i + 1) % 4 + 1],
                                             accum_out=L[:, (i + 1) % 4:(i + 1) % 4 + 1]).then_inc(exp_ready, 1)
                    if i % 4 == 2 and 10 <= i < 10 + B:
                        s = (i - 10) // 4
                        need(act, lg_ready, 2 * s + 2, r, B // 2, 2)
                        nc.scalar.activation(EX[:, :, :], LG[:, :, :], ACT.Exp, scale=-1.0).then_inc(negexp_ready, 1)
                    if valid(i + 4):
                        b = i + 4
                        need(act, nm_ready, i + 5, r, 10 ** 6)
                        need(act, x1t_done, b // 2 - 1, r, B // 2, 2)
                        nc.scalar.activation(N1[:, b % 4, :], X[:, b + GROUP * r, :], ACT.Identity,
                                             bias=NM[0:T, j, 4:5], scale=RS[0:T, j, 4:5]).then_inc(n1_ready, 1)
                    if valid(i - 3):
                        b = i - 3
                        need(act, nm_ready, i + 5, r, 10 ** 6)
                        need(act, xnt_done, b - 1, r, B)
                        nc.scalar.activation(XN[:, b % 2, :], X[:, b + GROUP * r, :], ACT.Identity,
                                             bias=NM[0:T, j, 3:4], scale=RS[0:T, j, 3:4]).then_inc(xn_ready, 1)
                    if isinstance(r, int) and 0 <= i < CHUNKS:
                        act.wait_ge(stage_full[i % 2], 16 * (i // 2 + 1))
                        n = CHUNK // 128
                        nc.scalar.activation(GUH[:, i * n:(i + 1) * n, :],
                                             STG[:, i % 2, :].rearrange("p (a b) -> p a b", b=128), ACT.Copy)\
                            .then_inc(whi_ready, 1)
                    if valid(i - 1):
                        b = i - 1
                        need(act, ct_done, b + 1, r, B)
                        need(act, o_done, b - 1, r, B)
                        nc.scalar.activation(CT[:, b % 2, :, :].rearrange("p a b -> p (a b)"), ct_ps[0:FH, 0:2 * T],
                                             ACT.Copy).then_inc(ct_ready, 1)

                act.sem_inc(negexp_ready, 1)
                act.wait_ge(folded, 3)
                steps(act, step)

            @block.tensor
            def _(pe):
                pe.sem_inc(off_done, 1)
                pe.wait_ge(setup_full, 16 * N_SETUP)
                for et in range(DT):
                    for dt in range(DT):
                        nc.tensor.matmul(tr_ps[:, et:et + 1], WQ[:, dt, et * 128:(et + 1) * 128], COL[:, 1, dt:dt + 1],
                                         start=dt == 0, stop=dt == DT - 1)
                for at, w in ((2, WK), (4, WV)):
                    for et in range(DT):
                        for ft in range(2):
                            last = nc.tensor.matmul(tr_ps[:, at + et:at + et + 1], w[:, ft, et * 128:(et + 1) * 128],
                                                    B2C[:, ft:ft + 1], start=ft == 0, stop=ft == 1)
                last.then_inc(bias_done, 1)
                pe.wait_ge(aug_done, 6)
                pe.wait_ge(vec_made, 7)
                for dt in range(DT):
                    for et in range(DT):
                        nc.tensor.matmul(x2t_ps[:, dt, 0:FA], WQT[:, et, dt * 128:(dt + 1) * 128], WKA[:, et, :],
                                         start=et == 0, stop=et == DT - 1)
                for h, ps in ((0, ct_ps), (1, o_ps)):
                    for et in range(DT):
                        nc.tensor.matmul(q_ps[0:FH, h:h + 1], WKA[:, et, h * FH:(h + 1) * FH], TQ[:, et:et + 1],
                                         start=et == 0, stop=et == DT - 1)
                    for et in range(DT):
                        last = nc.tensor.matmul(ps[0:FH, 0:D], WVA[:, et, h * FH:(h + 1) * FH], WO[:, et, :],
                                                start=et == 0, stop=et == DT - 1)
                last.then_inc(fold_done, 1)
                pe.wait_ge(folded, 3)
                pe.wait_ge(vo_ready, 2)
                pe.wait_ge(made, 4)

                def step(i, r):
                    if i % 2 == 0 and valid(i + 2):
                        need(pe, n1_ready, i + 4, r, B)
                        need(pe, xnt_ready, 2 * (i - 4), r, 2 * B, 2 * GROUP)
                        for kt in range(DT):
                            for jj in range(2):
                                last = nc.tensor.transpose(tr_ps[:, (2 * kt + jj) * T:(2 * kt + jj + 1) * T],
                                                           N1[:, (i + 2 + jj) % 4, kt * 128:(kt + 1) * 128],
                                                           ID[0:T, 0:T])
                        last.then_inc(x1t_done, 1)
                    if valid(i + 1):
                        b = i + 1
                        need(pe, x2t_ready, b + 1, r, B)
                        need(pe, q_ready, 2 * (b // 2 + 1), r, B, GROUP)
                        need(pe, exp_ready, b, r, B)
                        for h in range(2):
                            last = nc.tensor.matmul(s_ps[0:T, 0:K], QT[:, (b // 2) % 2, h, (b % 2) * T:(b % 2 + 1) * T],
                                                    X2T[:, b % 2, h, :], start=h == 0, stop=h == 1)
                        last.then_inc(s_done, 1)
                    if valid(i + 2):
                        b = i + 2
                        need(pe, ctx_ready, KT * (b + 1), r, KT * B, KT * GROUP)
                        need(pe, x2t_ready, b, r, B)
                        for h in range(2):
                            for t in range(KT):
                                last = nc.tensor.transpose(x2t_ps[0:FH, h, t * KP:(t + 1) * KP],
                                                           X2N[:, b % 4, t, h * FH:(h + 1) * FH], ID[0:KP, 0:KP])
                        last.then_inc(x2t_done, 1)
                    if i % 2 == 0 and valid(i + 2):
                        p = (i + 2) // 2
                        need(pe, x1t_ready, p + 1, r, B // 2, 2)
                        need(pe, q_ready, 2 * p, r, B, GROUP)
                        need(pe, lg_ready, (i - 8) // 2 + 1, r, B // 2, 2)
                        need(pe, off_ready, (i - 10) // 4 + 1, r, NB + 1, 1)
                        for h in range(2):
                            for kt in range(DT):
                                last = nc.tensor.matmul(q_ps[0:FH, h * 2 * T:(h + 1) * 2 * T],
                                                        A[:, kt, h * FH:(h + 1) * FH], X1T[:, kt, :],
                                                        start=kt == 0, stop=kt == DT - 1)
                        last.then_inc(q_done, 1)
                    if valid(i - 4):
                        b = i - 4
                        need(pe, xn_ready, b + 1, r, B)
                        need(pe, xnt_ready, 2 * b, r, 2 * B, 2 * GROUP)
                        if i % 2 == 0:
                            need(pe, x1t_ready, (i + 2) // 2 + 1, r, B // 2, 2)
                        for kt in range(DT):
                            last = nc.tensor.transpose(tr_ps[:, kt * T:(kt + 1) * T],
                                                       XN[:, b % 2, kt * 128:(kt + 1) * 128], ID[0:T, 0:T])
                        last.then_inc(xnt_done, 1)
                    if valid(i):
                        need(pe, exp_ready, i + 1, r, B)
                        need(pe, pt_ready, i, r, B)
                        for t in range(KT):
                            last = nc.tensor.transpose(pt_ps[0:KP, t * T:(t + 1) * T],
                                                       P[:, i % 2, t * KP:(t + 1) * KP], ID[0:T, 0:T])
                        last.then_inc(pt_done, 1)
                    if valid(i - 1):
                        b = i - 1
                        need(pe, pt_ready, b + 1, r, B)
                        need(pe, ct_ready, b, r, B)
                        for h in range(2):
                            for t in range(KT):
                                last = nc.tensor.matmul(ct_ps[0:FH, h * T:(h + 1) * T],
                                                        X2N[:, b % 4, t, h * FH:(h + 1) * FH], PT[:, b % 2, t, :],
                                                        start=t == 0, stop=t == KT - 1)
                        last.then_inc(ct_done, 1)
                    if valid(i - 2):
                        b = i - 2
                        need(pe, ct_ready, b + 1, r, B)
                        need(pe, xmid_ready, b, r, B)
                        if b == 0:
                            pe.wait_ge(bo_full, 16)
                        for h in range(2):
                            last = nc.tensor.matmul(o_ps[0:T, 0:D], CT[:, b % 2, h, :], VO[:, h, :],
                                                    start=h == 0, stop=h == 1)
                        last.then_inc(o_done, 1)
                    if i % 2 == 1 and valid(i - 7):
                        p = (i - 7) // 2
                        need(pe, xnt_ready, 2 * (i - 5), r, 2 * B, 2 * GROUP)
                        need(pe, q_ready, 2 * ((i + 1) // 2 + 1), r, B, GROUP)
                        need(pe, lg_ready, p, r, B // 2, 2)
                        need(pe, off_ready, (i - 9) // 4 + 1, r, NB + 1, 1)
                        for jj in range(2):
                            b = i - 7 + jj
                            for kt in range(DT):
                                last = nc.tensor.matmul(q_ps[0:T, LOGITS + jj * E:LOGITS + (jj + 1) * E],
                                                        XNS[:, kt, (b % 4) * T:(b % 4 + 1) * T], GW[:, kt, :],
                                                        start=kt == 0, stop=kt == DT - 1)
                        last.then_inc(lg_done, 1)
                    if i % 4 == 1 and 13 <= i < 13 + B:
                        s = (i - 13) // 4
                        need(pe, route_ready, 4 * s + 1, r, 10 ** 6, 4)
                        need(pe, q_ready, 2 * ((i + 1) // 2 + 1), r, B, GROUP)
                        need(pe, off_ready, s + 1, r, NB, 1)
                        for jj in range(GROUP):
                            last = nc.tensor.matmul(q_ps[:, jj * T:(jj + 1) * T], OFFB[:, jj, :], IDB[:, :],
                                                    start=True, stop=True)
                        last.then_inc(off_done, 1)

                steps(pe, step)

        two = ExitStack()
        with two:
            def s2(name, shape, dt=F32):
                return sb(name, shape, dt, two)

            WD = s2("down", [128, UNITS, D])
            WDH = s2("down_hi", [128, UNITS, D], F32R)
            WDL = s2("down_lo", [128, UNITS, D], F32R)
            SG = s2("silu", [128, 2, BLOCK])
            HF = s2("hidden", [128, 2, BLOCK])
            HH = s2("hidden_hi", [128, 2, BLOCK], F32R)
            HL = s2("hidden_lo", [128, 2, BLOCK], F32R)
            TOT = s2("totals", [128, 2, E])
            CNT = s2("counts", [128, E])
            INV = s2("counts_inv", [128, E])
            WM = s2("mean_weight", [128, E])

            g_ps = two.enter_context(nc.psum_tensor("g_ps", [128, 2, 512], F32))
            u_ps = two.enter_context(nc.psum_tensor("u_ps", [128, 2, 512], F32))
            d_ps = two.enter_context(nc.psum_tensor("d_ps", [128, GROUP, 512], F32))

            down_full = sem("down_full")
            tot_done = sem("tot_done")
            tot_ready = sem("tot_ready")
            mean_chain = sem("mean_chain")
            mean_ready = sem("mean_ready")
            dhi_ready = sem("dhi_ready")
            dlo_ready = sem("dlo_ready")
            g_done = sem("g_done")
            u_done = sem("u_done")
            silu_ready = sem("silu_ready")
            h_ready = sem("h_ready")
            hhi_ready = sem("hhi_ready")
            hlo_ready = sem("hlo_ready")
            d_done = sem("d_done")
            fin_ready = sem("fin_ready")
            stored = sem("stored")

            def units(eng, unit):
                for u in range(UNITS):
                    unit(u, 0, True)
                with eng.Fori(0, NB - 1) as r:
                    for u in range(UNITS):
                        unit(u, r, False)

            def after(eng, s, n, r, per):
                if not isinstance(r, int):
                    eng.wait_ge(s, n + per + per * r)
                elif n > 0:
                    eng.wait_ge(s, n)

            block2 = two.enter_context(nc.Block())

            @block2.sync
            def _(sp):
                sp.dma_start(WD[:, :, :], down_t).then_inc(down_full, 16)
                with sp.Fori(0, NB) as r:
                    sp.wait_ge(fin_ready, GROUP + GROUP * r)
                    rows = bass.ds(GROUP * r, GROUP)
                    sp.dma_start(out_rows[:, rows, :], X[:, rows, :]).then_inc(stored, 16)
                sp.wait_ge(stored, 16 * NB)

            @block2.scalar
            def _(act):
                def unit(u, r, first):
                    after(act, g_done, u + 1, r, UNITS)
                    after(act, h_ready, u - 1, r, UNITS)
                    nc.scalar.activation(SG[:, u % 2, :], g_ps[:, u % 2, 0:BLOCK], ACT.Silu).then_inc(silu_ready, 1)
                    if first:
                        if u == 0:
                            act.wait_ge(down_full, 16)
                        if u < SHARED:
                            nc.scalar.activation(WDH[:, u, :], WD[:, u, :], ACT.Copy).then_inc(dhi_ready, 1)
                        else:
                            act.wait_ge(mean_ready, 1)
                            nc.scalar.activation(WDH[:, u, :], WD[:, u, :], ACT.Copy,
                                                 scale=WM[:, u - SHARED:u - SHARED + 1]).then_inc(dhi_ready, 1)
                    after(act, h_ready, u + 1, r, UNITS)
                    after(act, d_done, u - 1, r, UNITS)
                    nc.scalar.activation(HH[:, u % 2, :], HF[:, u % 2, :], ACT.Copy).then_inc(hhi_ready, 1)

                units(act, unit)

            @block2.vector
            def _(dve):
                def finish(r, n):
                    if isinstance(r, int):
                        dve.wait_ge(d_done, n * UNITS)
                    else:
                        dve.wait_ge(d_done, UNITS + UNITS * r)
                    for j in range(GROUP):
                        row = (n - 1) * GROUP + j if isinstance(r, int) else GROUP * r + j
                        nc.vector.tensor_tensor(X[:, row, :], d_ps[0:T, j, 0:D], X[:, row, :], ALU.add)\
                            .then_inc(fin_ready, 1)

                def unit(u, r, first):
                    after(dve, u_done, u + 1, r, UNITS)
                    after(dve, silu_ready, u + 1, r, UNITS)
                    after(dve, hlo_ready, u - 1, r, UNITS)
                    after(dve, hhi_ready, u - 1, r, UNITS)
                    nc.vector.tensor_tensor(HF[:, u % 2, :], u_ps[:, u % 2, 0:BLOCK], SG[:, u % 2, :], ALU.mult)\
                        .then_inc(h_ready, 1)
                    if first:
                        dve.wait_ge(dhi_ready, u + 1)
                        if u < SHARED:
                            nc.vector.tensor_tensor(WDL[:, u, :], WD[:, u, :], WDH[:, u, :].bitcast(F32),
                                                    ALU.subtract).then_inc(dlo_ready, 1)
                        else:
                            nc.vector.scalar_tensor_tensor(out=WDL[:, u, :], in0=WD[:, u, :],
                                                           scalar=WM[:, u - SHARED:u - SHARED + 1],
                                                           in1=WDH[:, u, :].bitcast(F32), op0=ALU.mult,
                                                           op1=ALU.subtract).then_inc(dlo_ready, 1)
                    after(dve, hhi_ready, u + 1, r, UNITS)
                    after(dve, d_done, u - 1, r, UNITS)
                    nc.vector.tensor_tensor(HL[:, u % 2, :], HF[:, u % 2, :], HH[:, u % 2, :].bitcast(F32),
                                            ALU.subtract).then_inc(hlo_ready, 1)
                    if not first and u == 0:
                        finish(r, 0)

                dve.wait_ge(tot_done, 1)
                nc.vector.tensor_reduce(TOT[:, :, :], d_ps[:, 0, :].rearrange("p (w b e) -> p w e b", w=2, e=E),
                                        AX.X, ALU.add).then_inc(tot_ready, 1)
                dve.wait_ge(tot_ready, 1)
                nc.vector.tensor_scalar(CNT[:, :], TOT[:, 1, :], 1.0, None, ALU.max).then_inc(mean_chain, 1)
                dve.wait_ge(mean_chain, 1)
                nc.vector.reciprocal(INV[:, :], CNT[:, :]).then_inc(mean_chain, 1)
                dve.wait_ge(mean_chain, 2)
                nc.vector.tensor_tensor(WM[:, :], TOT[:, 0, :], INV[:, :], ALU.mult).then_inc(mean_ready, 1)
                dve.wait_ge(mean_ready, 1)
                units(dve, unit)
                finish(0, NB)

            @block2.tensor
            def _(pe):
                def gate_up(u, r, first):
                    tokens = bass.ds(0 if first else BLOCK + BLOCK * r, BLOCK)
                    for g, ps, free, done in ((0, g_ps, silu_ready, g_done), (1, u_ps, h_ready, u_done)):
                        after(pe, free, u - 1, r, UNITS)
                        out_ps = ps[:, u % 2, 0:BLOCK]
                        if g == 0 and u >= SHARED:
                            nc.tensor.matmul(out_ps, OFFSEL[:, u - SHARED, :], OFFT[:, tokens], start=True, stop=False)
                        n = 0
                        for kt in range(DT):
                            at = (u * 2 + g) * DT + kt
                            for w, v in ((GUH, XH), (GUH, XL), (GUL, XH)):
                                last = nc.tensor.matmul(out_ps, w[:, at, :], v[:, kt, tokens],
                                                        start=n == 0 and not (g == 0 and u >= SHARED),
                                                        stop=n == 3 * DT - 1)
                                n += 1
                        last.then_inc(done, 1)

                def down(u, r, late):
                    if isinstance(r, int):
                        n = u + 1 + late * UNITS
                        pe.wait_ge(hlo_ready, n)
                        pe.wait_ge(hhi_ready, n)
                    else:
                        n = u + 1 + (0 if late else UNITS)
                        pe.wait_ge(hlo_ready, n + UNITS * r)
                        pe.wait_ge(hhi_ready, n + UNITS * r)
                    if isinstance(r, int) and not late:
                        pe.wait_ge(dlo_ready, u + 1)
                        if u == 0:
                            pe.wait_ge(tot_ready, 1)
                    if not isinstance(r, int) and not late and u == 0:
                        pe.wait_ge(fin_ready, GROUP + GROUP * r)
                    for j in range(GROUP):
                        k = 0
                        for h, w in ((HH, WDH), (HH, WDL), (HL, WDH)):
                            last = nc.tensor.matmul(d_ps[0:T, j, 0:D], h[:, u % 2, j * T:(j + 1) * T], w[:, u, :],
                                                    start=u == 0 and k == 0, stop=u == UNITS - 1 and k == 2)
                            k += 1
                    last.then_inc(d_done, 1)

                nc.tensor.matmul(d_ps[:, 0, :], ONES[:, :], ROUTE[:, :, :, :].rearrange("p w b e -> p (w b e)"),
                                 start=True, stop=True).then_inc(tot_done, 1)

                def unit(u, r, first):
                    gate_up(u, r, first)
                    if u > 0:
                        down(u - 1, r, 0)
                    elif not first:
                        down(UNITS - 1, r, 1)

                units(pe, unit)
                down(UNITS - 1, 0, NB - 1)


def kernel(x, ctx_768, L0_xattn_ln1_g, L0_xattn_ln1_b, L0_xattn_ln2_g, L0_xattn_ln2_b, L0_xattn_Wq, L0_xattn_bq,
           L0_xattn_Wk, L0_xattn_bk, L0_xattn_Wv, L0_xattn_bv, L0_xattn_Wo, L0_xattn_bo, L0_ffn_gate_w,
           L0_ffn_lb_bias, L0_ffn_expert_gate_w, L0_ffn_expert_up_w, L0_ffn_expert_down_w, L0_ffn_shared_gate_w,
           L0_ffn_shared_up_w, L0_ffn_shared_down_w):
    import numpy as np
    import concourse.bacc as bacc
    from concourse.bass_utils import run_bass_kernel_spmd

    a = np.asarray
    T = x.shape[1]
    cols = lambda v: a(v).reshape(2, 128).T
    halves = lambda w: a(w).reshape(-1, 128, a(w).shape[-1])
    gate = np.concatenate([halves(L0_ffn_shared_gate_w), a(L0_ffn_expert_gate_w)])
    up = np.concatenate([halves(L0_ffn_shared_up_w), a(L0_ffn_expert_up_w)])
    gate_up = np.stack([gate, up], axis=1).reshape(-1, 2, 128, 2, 128).transpose(4, 0, 1, 3, 2).reshape(128, -1)
    shared_down = a(L0_ffn_shared_down_w).T.reshape(2, 128, -1)
    down = np.concatenate([shared_down, a(L0_ffn_expert_down_w).transpose(0, 2, 1)]).transpose(1, 0, 2)
    ins = {
        "x": a(x), "ctx_in": a(ctx_768),
        "wq_t": a(L0_xattn_Wq).T, "wq": a(L0_xattn_Wq), "wk_t": a(L0_xattn_Wk).T, "wk": a(L0_xattn_Wk),
        "wv_t": a(L0_xattn_Wv).T, "wv": a(L0_xattn_Wv), "wo": a(L0_xattn_Wo),
        "g2_rows": np.broadcast_to(a(L0_xattn_ln2_g), (128, 192)),
        "columns": np.stack([cols(v) for v in (L0_xattn_ln1_g, L0_xattn_ln1_b, L0_xattn_bq, L0_xattn_bk,
                                               L0_xattn_bv)], axis=1),
        "b2_columns": a(L0_xattn_ln2_b).reshape(2, 96).T,
        "bo": a(L0_xattn_bo).reshape(1, -1),
        "gate_w_t": a(L0_ffn_gate_w).T,
        "lb_rows": np.broadcast_to(a(L0_ffn_lb_bias), (T, 8)),
        "gate_up_t": gate_up, "down_t": down,
    }
    nc = bacc.Bacc("TRN2", target_bir_lowering=False, num_devices=1)
    arrays, args = {}, {}
    for name, v in ins.items():
        v = np.ascontiguousarray(v)
        arrays[f"in_{name}"] = v
        args[name] = nc.dram_tensor(f"in_{name}", v.shape, mybir.dt.from_np(v.dtype), kind="ExternalInput").ap()
    out = nc.dram_tensor("out_0", x.shape, F32, kind="ExternalOutput").ap()
    attention_and_experts(nc, **args, out=out)
    r = run_bass_kernel_spmd(nc, [arrays], core_ids=[0])
    return r.results[0]["out_0"]
```

```python
from contextlib import ExitStack

import concourse.bass as bass
from concourse import mybir

F32 = mybir.dt.float32
F32R = mybir.dt.float32r
BF16 = mybir.dt.bfloat16
I32 = mybir.dt.int32
ALU = mybir.AluOpType
ACT = mybir.ActivationFunctionType
AX = mybir.AxisListType

EPS = 1e-5
NOWHERE = float(2 ** 20)
GROUP = 4
LEAD = 15
TILE = 128


def attention_and_experts(nc, x, ctx_in, wq_t, wq, wk_t, wk, wv_t, wv, wo, g2_rows, columns, b2_columns,
                          bo, gate_w_t, lb_rows, gate_up_t, down_t, region_rows, expert_ids, tile_ids, tile_starts,
                          token_ids, row_ids,
                          expert_rows, token_rows, out):
    B, T, D = x.shape
    K, DC = ctx_in.shape[1:]
    KT = 3
    KP = K // KT
    DT = D // 128
    FA = DC + 2
    FH = FA // 2
    E = lb_rows.shape[1]
    UNITS = down_t.shape[1]
    SHARED = UNITS - E
    BLOCK = GROUP * T
    NB = B // GROUP
    TURNS = NB - 5
    R = B * T
    NT = tile_ids.shape[1]
    NK = tile_starts.shape[1]
    SW = token_rows.shape[1]
    LAST = 42
    SCALE = float(D) ** -0.5
    CHUNKS = 8
    CHUNK = gate_up_t.shape[1] // CHUNKS
    assert T * GROUP == BLOCK and KP * KT == K and LEAD + GROUP * TURNS + 5 <= B

    x_rows = x.rearrange("b t d -> t b d")
    out_rows = out.rearrange("b t d -> t b d")
    ctx_rows = ctx_in.rearrange("b (p t) d -> p b t d", t=KT)

    top = ExitStack()
    with top:
        def sb(name, shape, dt=F32, where=top):
            return where.enter_context(nc.sbuf_tensor(name, shape, dt))

        def sem(name):
            return top.enter_context(nc.semaphore(name))

        X = sb("x_sb", [T, B, D])
        XNT = sb("xn_t_all", [128, DT, B * T])
        GUH = sb("gate_up_hi", [128, 2 * DT * UNITS, 128], F32R)
        GUL = sb("gate_up_lo", [128, 2 * DT * UNITS, 128], F32R)
        ROUTE = sb("route", [T, 2, B, E])
        ID = sb("identity", [128, 128])
        ER = sb("region_first", [128, E])
        BEFORE = sb("before", [128, E, E])
        SEND = sb("send", [128, GROUP, SW])
        TOKEN = sb("token_ids_sb", [T, B])
        SLOT = sb("send_rows", [T, GROUP, 2], I32)
        ONES = sb("ones", [T, 128])

        send_full = [sem(f"send_full{j}") for j in range(GROUP)]
        sent = [sem(f"sent{j}") for j in range(GROUP)]
        slot_ready = sem("slot_ready")
        down_full = sem("down_full")

        def send(j):
            for k in range(2):
                nc.gpsimd.indirect_dma_start(token_rows, bass.IndirectOffsetOnAxis(ap=SLOT[:, j, k:k + 1], axis=0),
                                             SEND[0:T, j, :], None, bounds_check=E * R - 1, oob_is_err=False)\
                    .then_inc(sent[j], 16)

        one = ExitStack()
        with one:
            def s1(name, shape, dt=F32):
                return sb(name, shape, dt, one)

            G2 = s1("g2_sb", [128, DC])
            COL = s1("columns_sb", [128, 5, DT])
            B2C = s1("b2_columns_sb", [DC // 2, 2])
            LBR = s1("lb_rows_sb", [T, E])
            GW = s1("gate_w_sb", [128, DT, E])
            WKA = s1("wk_aug", [128, DT, FA])
            WVA = s1("wv_aug", [128, DT, FA])
            G1S = s1("g1_scaled", [128, DT])
            TQ = s1("q_bias", [128, DT])
            A = s1("a_sb", [128, DT, FA])
            C = s1("c_sb", [FH, 2])
            VO = s1("vo_sb", [FH, 2, D])
            ONESB = s1("ones_bf", [T, T], BF16)
            TRIB = s1("earlier_bf", [T, T], BF16)
            HALF = s1("minus_half", [128, 5])
            STG = s1("stage", [128, 2, CHUNK])

            RAW = s1("ctx_raw", [KP, 4, KT, DC])
            X2N = s1("ctx_norm", [KP, 4, KT, FA])
            N1 = s1("x_norm", [T, 4, D])
            X1T = s1("x_norm_t", [128, DT, 2 * T])
            QT = s1("q_t", [FH, 2, 2, 2 * T])
            X2T = s1("ctx_norm_t", [FH, 2, 2, K])
            P = s1("probs", [T, 2, K])
            PT = s1("probs_t", [KP, 2, KT, T])
            CT = s1("context_t", [FH, 2, 2, T])
            XN = s1("x2_norm", [T, 2, D])
            XNS = s1("xn_t", [128, DT, BLOCK])
            XNA = s1("x2_norm_all", [T, B, D])
            ST = s1("stats", [128, 5, 6])
            MV = s1("mean_var", [128, 4, 5, 2])
            VE = s1("var_eps", [128, 4, 5])
            RS = s1("rstd", [128, 4, 5])
            NM = s1("minus_mean_rstd", [128, 4, 5])
            NMAX = s1("minus_max", [T, 4])
            L = s1("row_sum", [T, 4])
            RL = s1("row_sum_inv", [T, 4])
            LG = s1("logits_sb", [T, GROUP, E])
            EX = s1("exp_minus", [T, GROUP, E])
            EX1 = s1("one_plus_exp", [T, GROUP, E])
            SC = s1("route_scores", [T, GROUP, E])
            GT = s1("greater", [T, GROUP, E, E])
            GE = s1("greater_equal", [T, GROUP, E, E])
            EQ = s1("equal", [T, GROUP, E, E])
            EQB = s1("equal_before", [T, GROUP, E, E])
            AHEAD = s1("is_ahead", [T, GROUP, E, E])
            SUM4 = s1("ahead_sum4", [T, GROUP, E, 4])
            SUM2 = s1("ahead_sum2", [T, GROUP, E, 2])
            RK = s1("rank", [T, GROUP, E])
            SELB = s1("selected_bf", [T, GROUP, E], BF16)
            BASE = s1("region_next", [T, E])
            ROWS = s1("region_rows_group", [T, GROUP, E])
            CH = s1("chosen_rows", [T, GROUP, E])
            CMAX = s1("chosen_max", [T, GROUP])
            CSUM = s1("chosen_sum", [T, GROUP])
            SS = s1("selected_scores", [T, GROUP, E])
            SM = s1("score_sum", [T, GROUP])
            SE = s1("score_sum_eps", [T, GROUP])
            SI = s1("score_sum_inv", [T, GROUP])

            spare = XNS[:, :, :].rearrange("p a b -> p (a b)")
            WQT = spare[:, 0:DT * D].rearrange("p (t n) -> p t n", t=DT)
            WKT = spare[:, DT * D:DT * (D + DC)].rearrange("p (t n) -> p t n", t=DT)
            WVT = X1T[:, :, :].rearrange("p a b -> p (a b)")[:, 0:DT * DC].rearrange("p (t n) -> p t n", t=DT)
            WQ = STG[:, 0, 0:DT * D].rearrange("p (t n) -> p t n", t=DT)
            WO = STG[:, 1, 0:DT * D].rearrange("p (t n) -> p t n", t=DT)
            WK = N1[0:DC // 2, 0:2, :]
            WV = N1[0:DC // 2, 2:4, :]

            x2t_ps = one.enter_context(nc.psum_tensor("x2t_ps", [128, 2, 512], F32))
            s_ps = one.enter_context(nc.psum_tensor("s_ps", [128, 512], F32))
            pt_ps = one.enter_context(nc.psum_tensor("pt_ps", [128, 512], F32))
            ct_ps = one.enter_context(nc.psum_tensor("ct_ps", [128, 512], F32))
            o_ps = one.enter_context(nc.psum_tensor("o_ps", [128, 512], F32))
            tr_ps = one.enter_context(nc.psum_tensor("tr_ps", [128, 512], F32))
            q_ps = one.enter_context(nc.psum_tensor("q_ps", [128, 512], F32))
            LOGITS = 2 * 2 * T

            setup_full = sem("setup_full")
            bo_full = sem("bo_full")
            x_first = sem("x_first")
            x_rest = sem("x_rest")
            raw_full = [sem(f"raw_full{j}") for j in range(4)]
            stage_full = [sem(f"stage_full{j}") for j in range(2)]
            made = sem("made_by_pool")
            cleared = sem("cleared")
            bias_done = sem("bias_done")
            aug_done = sem("aug_done")
            fold_done = sem("fold_done")
            folded = sem("folded")
            vo_ready = sem("vo_ready")
            vec_made = sem("made_by_vector")
            ctx_stats = sem("ctx_stats")
            ctx_mv = sem("ctx_mv")
            x_stats = sem("x_stats")
            x_mv = sem("x_mv")
            x2_stats = sem("x2_stats")
            x2_mv = sem("x2_mv")
            var_ready = sem("var_ready")
            rstd_ready = sem("rstd_ready")
            nm_ready = sem("nm_ready")
            ctx_ready = sem("ctx_norm_ready")
            n1_ready = sem("n1_ready")
            x1t_done = sem("x1t_done")
            x1t_ready = sem("x1t_ready")
            q_done = sem("q_done")
            q_ready = sem("q_ready")
            x2t_done = sem("x2t_done")
            x2t_ready = sem("x2t_ready")
            s_done = sem("s_done")
            max_ready = sem("max_ready")
            exp_ready = sem("exp_ready")
            inv_ready = sem("inv_ready")
            pt_done = sem("pt_done")
            pt_ready = sem("pt_ready")
            ct_done = sem("ct_done")
            ct_ready = sem("ct_ready")
            o_done = sem("o_done")
            xmid_ready = sem("xmid_ready")
            xn_ready = sem("xn_ready")
            xnt_done = sem("xnt_done")
            xnt_ready = sem("xnt_ready")
            xna_full = [sem(f"xna_full{j}") for j in range(2)]
            base_ready = sem("base_ready")
            rows_ready = sem("rows_ready")
            choosing = sem("choosing")
            zeroed = sem("zeroed")
            lg_done = sem("lg_done")
            lg_ready = sem("lg_ready")
            negexp_ready = sem("negexp_ready")
            denominator = sem("sigmoid_denominator")
            scored = sem("scored")
            compared = sem("compared")
            ranking = sem("ranking")
            ranked = sem("ranked")
            routing = sem("routing")
            route_ready = sem("route_ready")
            off_done = sem("off_done")
            off_ready = sem("off_ready")
            whi_ready = sem("whi_ready")
            wlo_ready = sem("wlo_ready")
            passed = sem("passed_a_wait")

            def need(eng, s, n, r, top_value, per=GROUP, apart=False):
                if isinstance(r, int):
                    n = min(n, top_value)
                    if n > 0:
                        eng.wait_ge(s, n)
                elif apart:
                    assert n > 0
                    eng.wait_ge(s, n + per * r)
                    eng.sem_inc(passed, 1)
                else:
                    assert n > 0
                    eng.wait_ge(s, n + per * r)

            def valid(b):
                return 0 <= b < B

            def steps(eng, step):
                for i in range(-5, LEAD):
                    step(i, 0)
                with eng.Fori(0, TURNS) as r:
                    for i in range(LEAD, LEAD + GROUP):
                        step(i, r)
                for i in range(LEAD + GROUP * TURNS, LAST):
                    step(i, 0)

            N_SETUP = 14
            block = one.enter_context(nc.Block())

            @block.sync
            def _(sp):
                sp.dma_start(X[:, 0:GROUP, :], x_rows[:, 0:GROUP, :]).then_inc(x_first, 16)
                for j in range(4):
                    sp.dma_start(RAW[:, j, :, :], ctx_rows[:, j, :, :]).then_inc(raw_full[j], 16)
                two = lambda a: a.rearrange("(t p) n -> p t n", t=2)
                for dst, src in ((WQT[:, :, :], two(wq_t)), (WQ[:, :, :], two(wq)), (WKT[:, :, :], two(wk_t)),
                                 (WVT[:, :, :], two(wv_t)), (WK[:, :, :], two(wk)), (WV[:, :, :], two(wv)),
                                 (WO[:, :, :], two(wo)), (G2[:, :], g2_rows), (COL[:, :, :], columns),
                                 (B2C[:, :], b2_columns), (LBR[:, :], lb_rows), (GW[:, :, :], two(gate_w_t)),
                                 (ER[:, :], region_rows), (TOKEN[:, :], token_ids)):
                    sp.dma_start(dst, src).then_inc(setup_full, 16)
                sp.dma_start(X[:, GROUP:B, :], x_rows[:, GROUP:B, :]).then_inc(x_rest, 16)
                sp.wait_ge(vo_ready, 2)
                sp.dma_start(VO[FH - 1:FH, 1, :], bo).then_inc(bo_full, 16)
                sp.wait_ge(cleared, 5)
                for e in range(E):
                    sp.dma_start(token_rows[e * R:e * R + TILE, :], SEND[:, 0, :]).then_inc(zeroed, 16)

                def step(i, r):
                    if valid(i + 5) and i + 5 >= GROUP:
                        b = i + 5
                        need(sp, ctx_ready, KT * (b - 3), r, KT * B, KT * GROUP)
                        sp.dma_start(RAW[:, b % 4, :, :], ctx_rows[:, b + GROUP * r, :, :])\
                            .then_inc(raw_full[b % 4], 16)
                    if isinstance(r, int) and 0 <= i + 2 < CHUNKS:
                        k = i + 2
                        if k >= 2:
                            sp.wait_ge(wlo_ready, k - 1)
                        sp.dma_start(STG[:, k % 2, :], gate_up_t[:, k * CHUNK:(k + 1) * CHUNK])\
                            .then_inc(stage_full[k % 2], 16)
                    if valid(i - 3):
                        b = i - 3
                        need(sp, xn_ready, b + 1, r, B)
                        sp.dma_start(XNA[:, b + GROUP * r, :], XN[:, b % 2, :]).then_inc(xna_full[b % 2], 16)
                    if valid(i - 11):
                        b = i - 11
                        need(sp, xna_full[b % 2], 16 * (b // 2 + 1), r, 16 * B // 2, 32, apart=True)
                        if b < GROUP and isinstance(r, int):
                            sp.wait_ge(zeroed, 16 * E)
                        need(sp, sent[b % 4], 32 * (b // 4), r, 10 ** 6, 32)
                        sp.dma_start(SEND[0:T, b % 4, 0:D], XNA[:, b + GROUP * r, :]).then_inc(send_full[b % 4], 16)

                steps(sp, step)
                for i in range(LAST, B + 11):
                    step(i, 0)
                sp.wait_ge(bo_full, 16)
                for j in range(GROUP):
                    sp.wait_ge(send_full[j], 16 * NB)

            @block.gpsimd
            def _(pool):
                nc.gpsimd.memset(ID[:, :], 0.0).then_inc(cleared, 1)
                nc.gpsimd.memset(BEFORE[:, :, :], 1.0).then_inc(cleared, 1)
                nc.gpsimd.memset(SEND[:, 0, 0:D], 0.0).then_inc(cleared, 1)
                nc.gpsimd.memset(SEND[:, 0, D:SW], NOWHERE).then_inc(cleared, 1)
                nc.gpsimd.memset(P[:, 0, 0:T], 1.0).then_inc(cleared, 1)
                nc.gpsimd.memset(HALF[:, :], -0.5).then_inc(made, 1)
                pool.wait_ge(cleared, 5)
                nc.gpsimd.affine_select(out=ID[:, :], in_=ID[:, :], compare_op=ALU.not_equal, fill=1.0, base=0,
                                        pattern=[[-1, 128]], channel_multiplier=1).then_inc(made, 1)
                nc.gpsimd.affine_select(out=BEFORE[:, :, :], in_=BEFORE[:, :, :], compare_op=ALU.is_gt, fill=0.0,
                                        base=0, pattern=[[1, E], [-1, E]], channel_multiplier=0).then_inc(made, 1)
                nc.gpsimd.affine_select(out=P[:, 0, 0:T], in_=P[:, 0, 0:T], compare_op=ALU.is_gt, fill=0.0,
                                        base=0, pattern=[[1, T]], channel_multiplier=-1).then_inc(made, 1)
                pool.wait_ge(made, 4)

                pool.sem_inc(ranked, 1)

                def rank(s, r):
                    def then(k):
                        need(pool, ranking, 5 * s + k, r, 10 ** 6, 5)

                    need(pool, compared, 2 * s + 2, r, 2 * NB, 2)
                    nc.gpsimd.tensor_tensor(EQ[:, :, :, :], GE[:, :, :, :], GT[:, :, :, :], ALU.subtract)\
                        .then_inc(ranking, 1)
                    then(1)
                    nc.gpsimd.tensor_tensor(EQB[:, :, :, :], EQ[:, :, :, :],
                                            BEFORE[0:T, :, :].unsqueeze(1).broadcast_to([T, GROUP, E, E]),
                                            ALU.mult).then_inc(ranking, 1)
                    then(2)
                    nc.gpsimd.tensor_tensor(AHEAD[:, :, :, :], GT[:, :, :, :], EQB[:, :, :, :], ALU.add)\
                        .then_inc(ranking, 1)
                    then(3)
                    nc.gpsimd.tensor_tensor(SUM4[:, :, :, :], AHEAD[:, :, :, 0:4], AHEAD[:, :, :, 4:8], ALU.add)\
                        .then_inc(ranking, 1)
                    then(4)
                    nc.gpsimd.tensor_tensor(SUM2[:, :, :, :], SUM4[:, :, :, 0:2], SUM4[:, :, :, 2:4], ALU.add)\
                        .then_inc(ranking, 1)
                    then(5)
                    nc.gpsimd.tensor_tensor(RK[:, :, :], SUM2[:, :, :, 0], SUM2[:, :, :, 1], ALU.add)\
                        .then_inc(ranked, 1)

                def step(i, r):
                    j = i % 4
                    if -4 <= i <= B + 2:
                        need(pool, var_ready, 2 * (i + 5), r, 10 ** 6, 2 * GROUP)
                        need(pool, n1_ready, i + 1, r, B)
                        need(pool, xn_ready, i - 6, r, B)
                        nc.gpsimd.tensor_tensor(RS[:, j, :], VE[:, j, :], HALF[:, :], ALU.pow).then_inc(rstd_ready, 1)
                    if valid(i + 3):
                        need(pool, nm_ready, i + 5, r, 10 ** 6)
                        need(pool, ct_done, i, r, B)
                        need(pool, raw_full[(i + 3) % 4], 16 * ((i + 3) // 4 + 1), r, 10 ** 6, 16, apart=True)
                        for t in range(KT):
                            nc.gpsimd.tensor_scalar(X2N[:, (i + 3) % 4, t, 0:DC], RAW[:, (i + 3) % 4, t, :],
                                                    RS[0:KP, j, t:t + 1], NM[0:KP, j, t:t + 1],
                                                    ALU.mult, ALU.add).then_inc(ctx_ready, 1)
                    if isinstance(r, int) and 0 <= i < CHUNKS:
                        pool.wait_ge(whi_ready, i + 1)
                        n = CHUNK // 128
                        nc.gpsimd.tensor_tensor(GUL[:, i * n:(i + 1) * n, :],
                                                STG[:, i % 2, :].rearrange("p (a b) -> p a b", b=128),
                                                GUH[:, i * n:(i + 1) * n, :].bitcast(F32),
                                                ALU.subtract).then_inc(wlo_ready, 1)
                    if i % 4 == 3 and 11 <= i < 11 + B:
                        rank((i - 11) // 4, r)
                    for first, js in ((14, (0, 1)), (15, (2,)), (16, (3,))):
                        s = (i - first) // 4
                        if i % 4 == first % 4 and 0 <= s < NB - 1:
                            for j in js:
                                need(pool, slot_ready, 4 * (s + 1), r, 4 * NB, 4, apart=True)
                                need(pool, send_full[j], 16 * (s + 1), r, 16 * NB, 16, apart=True)
                                send(j)

                steps(pool, step)

            @block.vector
            def _(dve):
                nc.vector.memset(ONES[:, :], 1.0).then_inc(vec_made, 1)
                nc.vector.memset(MV[:, :, :, :], 1.0).then_inc(vec_made, 1)
                nc.vector.memset(WVA[:, :, FA - 1:FA], 0.0).then_inc(vec_made, 1)
                nc.vector.memset(WKA[:, :, FA - 1:FA], 0.0).then_inc(vec_made, 1)
                nc.vector.memset(X2N[:, :, :, DC:FA], 1.0).then_inc(vec_made, 1)
                dve.wait_ge(made, 4)
                nc.vector.tensor_copy(TRIB[:, :], P[:, 0, 0:T]).then_inc(vec_made, 1)
                nc.vector.memset(ONESB[:, :], 1.0).then_inc(vec_made, 1)
                dve.wait_ge(vec_made, 7)

                def norms(i, r):
                    m = (i + 1) % 4
                    if valid(i + 4):
                        need(dve, raw_full[(i + 4) % 4], 16 * ((i + 4) // 4 + 1), r, 10 ** 6, 16)
                        for t in range(KT):
                            nc.vector.bn_stats(ST[0:KP, t, :], RAW[:, (i + 4) % 4, t, :]).then_inc(ctx_stats, 1)
                    if valid(i + 5):
                        if i + 5 < GROUP:
                            dve.wait_ge(x_first, 16)
                        else:
                            dve.wait_ge(x_rest, 16)
                        nc.vector.bn_stats(ST[0:T, 4, :], X[:, i + 5 + GROUP * r, :]).then_inc(x_stats, 1)
                    if valid(i - 2):
                        need(dve, xmid_ready, i - 1, r, B, apart=True)
                        nc.vector.bn_stats(ST[0:T, 3, :], X[:, i - 2 + GROUP * r, :]).then_inc(x2_stats, 1)
                    if valid(i + 4):
                        need(dve, ctx_stats, KT * (i + 5), r, KT * B, KT * GROUP, apart=True)
                        for t in range(KT):
                            nc.vector.bn_aggr(MV[0:KP, m, t, :], ST[0:KP, t, :]).then_inc(ctx_mv, 1)
                    if valid(i + 5):
                        need(dve, x_stats, i + 6, r, B, apart=True)
                        nc.vector.bn_aggr(MV[0:T, m, 4, :], ST[0:T, 4, :]).then_inc(x_mv, 1)
                    if valid(i - 2):
                        need(dve, x2_stats, i - 1, r, B, apart=True)
                        nc.vector.bn_aggr(MV[0:T, m, 3, :], ST[0:T, 3, :]).then_inc(x2_mv, 1)
                    if -4 <= i + 1 <= B + 2:
                        need(dve, ctx_mv, KT * (i + 5), r, KT * B, KT * GROUP)
                        need(dve, x_mv, i + 6, r, B)
                        need(dve, x2_mv, i - 1, r, B)
                        need(dve, rstd_ready, i + 2, r, 10 ** 6)
                        nc.vector.tensor_scalar(VE[:, m, 0:4], MV[:, m, 0:4, 1], EPS, None, ALU.add)\
                            .then_inc(var_ready, 1)
                        nc.vector.tensor_scalar(VE[:, m, 4:5], MV[:, m, 4:5, 1], 1.0 + EPS, EPS * EPS, ALU.mult,
                                                ALU.add).then_inc(var_ready, 1)

                dve.sem_inc(off_ready, 1)
                dve.wait_ge(setup_full, 16 * N_SETUP)
                g2b = G2[:, :].unsqueeze(1).broadcast_to([128, DT, DC])
                nc.vector.tensor_tensor(WKA[:, :, 0:DC], WKT[:, :, :], g2b, ALU.mult).then_inc(aug_done, 1)
                nc.vector.tensor_tensor(WVA[:, :, 0:DC], WVT[:, :, :], g2b, ALU.mult).then_inc(aug_done, 1)
                nc.vector.tensor_scalar(G1S[:, :], COL[:, 0, :], SCALE, None, ALU.mult).then_inc(aug_done, 1)
                nc.vector.tensor_copy(BASE[:, :], ER[0:T, :]).then_inc(base_ready, 1)
                dve.wait_ge(bias_done, 1)
                nc.vector.tensor_tensor(TQ[:, :], tr_ps[:, 0:2], COL[:, 2, :], ALU.add).then_inc(aug_done, 1)
                nc.vector.tensor_tensor(WKA[:, :, DC], tr_ps[:, 2:4], COL[:, 3, :], ALU.add).then_inc(aug_done, 1)
                nc.vector.tensor_tensor(WVA[:, :, DC], tr_ps[:, 4:6], COL[:, 4, :], ALU.add).then_inc(aug_done, 1)
                dve.wait_ge(fold_done, 1)
                dve.wait_ge(aug_done, 6)
                for dt in range(DT):
                    nc.vector.tensor_scalar(A[:, dt, :], x2t_ps[:, dt, 0:FA], G1S[:, dt:dt + 1], None, ALU.mult)\
                        .then_inc(folded, 1)
                nc.vector.tensor_scalar(C[:, :], q_ps[0:FH, 0:2], SCALE, None, ALU.mult).then_inc(folded, 1)
                nc.vector.tensor_copy(VO[:, 0, :], ct_ps[0:FH, 0:D]).then_inc(vo_ready, 1)
                nc.vector.tensor_copy(VO[:, 1, :], o_ps[0:FH, 0:D]).then_inc(vo_ready, 1)
                dve.wait_ge(base_ready, 1)

                def score(s, r):
                    need(dve, negexp_ready, s + 2, r, NB + 1, 1)
                    nc.vector.tensor_scalar(EX1[:, :, :], EX[:, :, :], 1.0, None, ALU.add).then_inc(denominator, 1)
                    need(dve, denominator, s + 1, r, NB, 1)
                    need(dve, ranked, s + 1, r, NB + 1, 1)
                    nc.vector.reciprocal(SC[:, :, :], EX1[:, :, :]).then_inc(scored, 1)
                    need(dve, scored, s + 1, r, NB, 1)
                    of_j = SC[:, :, :].unsqueeze(2).broadcast_to([T, GROUP, E, E])
                    of_e = SC[:, :, :].unsqueeze(3).broadcast_to([T, GROUP, E, E])
                    nc.vector.tensor_tensor(GT[:, :, :, :], of_j, of_e, ALU.is_gt).then_inc(compared, 1)
                    nc.vector.tensor_tensor(GE[:, :, :, :], of_j, of_e, ALU.is_ge).then_inc(compared, 1)

                RC = 3

                def route(s, r):
                    def then(k):
                        need(dve, routing, RC * s + k, r, 10 ** 6, RC)

                    need(dve, ranked, s + 2, r, NB + 1, 1)
                    need(dve, off_done, s + 1, r, NB + 1, 1)
                    blk = bass.ds(s * GROUP + r * GROUP, GROUP)
                    nc.vector.tensor_scalar(SELB[:, :, :], RK[:, :, :], 1.5, None, ALU.is_lt)\
                        .then_inc(route_ready, 1)
                    nc.vector.scalar_tensor_tensor(out=SS[:, :, :], in0=RK[:, :, :], scalar=1.5, in1=SC[:, :, :],
                                                   op0=ALU.is_lt, op1=ALU.mult).then_inc(routing, 1)
                    nc.vector.tensor_scalar(ROUTE[:, 1, blk, :], RK[:, :, :], 1.5, None, ALU.is_lt)\
                        .then_inc(route_ready, 1)
                    then(1)
                    nc.vector.tensor_reduce(SM[:, :], SS[:, :, :], AX.X, ALU.add).then_inc(routing, 1)
                    then(2)
                    nc.vector.tensor_scalar(SE[:, :], SM[:, :], 1e-8, None, ALU.add).then_inc(routing, 1)
                    then(3)
                    nc.vector.reciprocal(SI[:, :], SE[:, :]).then_inc(route_ready, 1)
                    need(dve, route_ready, 4 * s + 3, r, 10 ** 6, 4)
                    nc.vector.tensor_tensor(ROUTE[:, 0, blk, :], SS[:, :, :],
                                            SI[:, :].unsqueeze(2).broadcast_to([T, GROUP, E]), ALU.mult)\
                        .then_inc(route_ready, 1)

                def step(i, r):
                    if i % 2 == 0 and valid(i - 8):
                        p = (i - 8) // 2
                        need(dve, lg_done, p + 1, r, B // 2, 2)
                        need(dve, negexp_ready, p // 2 + 1, r, NB + 1, 1)
                        nc.vector.tensor_tensor(LG[:, 2 * (p % 2):2 * (p % 2) + 2, :],
                                                q_ps[0:T, LOGITS:LOGITS + 2 * E].rearrange("p (a e) -> p a e", e=E),
                                                LBR[:, :].unsqueeze(1).broadcast_to([T, 2, E]), ALU.add)\
                            .then_inc(lg_ready, 1)
                    if valid(i - 2):
                        need(dve, exp_ready, i - 1, r, B)
                        nc.vector.reciprocal(RL[:, (i - 2) % 4:(i - 2) % 4 + 1], L[:, (i - 2) % 4:(i - 2) % 4 + 1])\
                            .then_inc(inv_ready, 1)
                    if valid(i + 1):
                        need(dve, s_done, i + 2, r, B)
                        nc.vector.tensor_reduce(NMAX[:, (i + 1) % 4:(i + 1) % 4 + 1], s_ps[0:T, 0:K], AX.X, ALU.max,
                                                negate=True).then_inc(max_ready, 1)
                    if -4 <= i <= B + 2:
                        need(dve, rstd_ready, i + 5, r, 10 ** 6)
                        need(dve, n1_ready, i + 1, r, B)
                        need(dve, xn_ready, i - 6, r, B)
                        need(dve, ctx_ready, KT * i, r, KT * B, KT * GROUP)
                        nc.vector.scalar_tensor_tensor(out=NM[:, i % 4, :], in0=MV[:, i % 4, :, 0], scalar=-1.0,
                                                       in1=RS[:, i % 4, :], op0=ALU.mult, op1=ALU.mult)\
                            .then_inc(nm_ready, 1)
                    if valid(i):
                        need(dve, pt_done, i + 1, r, B)
                        need(dve, ct_done, i - 1, r, B)
                        nc.vector.tensor_copy(PT[:, i % 2, :, :].rearrange("p a b -> p (a b)"), pt_ps[0:KP, 0:KT * T])\
                            .then_inc(pt_ready, 1)
                    if valid(i - 2):
                        b = i - 2
                        need(dve, inv_ready, b + 1, r, B)
                        need(dve, o_done, b + 1, r, B)
                        nc.vector.scalar_tensor_tensor(out=X[:, b + GROUP * r, :], in0=o_ps[0:T, 0:D],
                                                       scalar=RL[:, b % 4:b % 4 + 1], in1=X[:, b + GROUP * r, :],
                                                       op0=ALU.mult, op1=ALU.add).then_inc(xmid_ready, 1)
                    norms(i, r)
                    if i % 4 == 2 and 10 <= i < 10 + B:
                        score((i - 10) // 4, r)
                    if i % 4 == 0 and 12 <= i < 12 + B:
                        route((i - 12) // 4, r)
                    if i % 4 == 1 and 13 <= i < 13 + B:
                        s = (i - 13) // 4
                        need(dve, off_done, s + 2, r, NB + 1, 1)
                        need(dve, off_ready, s + 1, r, NB + 1, 1)
                        blk = bass.ds(s * GROUP + r * GROUP, GROUP)
                        nc.vector.tensor_tensor(ROWS[:, :, :],
                                                q_ps[0:T, 0:GROUP * E].rearrange("p (a e) -> p a e", e=E),
                                                BASE[:, :].unsqueeze(1).broadcast_to([T, GROUP, E]), ALU.add)\
                            .then_inc(rows_ready, 1)
                        need(dve, rows_ready, s + 1, r, NB, 1)
                        nc.vector.tensor_tensor(BASE[:, :], q_ps[0:T, GROUP * E:(GROUP + 1) * E], BASE[:, :], ALU.add)\
                            .then_inc(off_ready, 1)
                        nc.vector.tensor_tensor(CH[:, :, :], ROWS[:, :, :], ROUTE[:, 1, blk, :], ALU.mult)\
                            .then_inc(choosing, 1)
                        need(dve, choosing, 3 * s + 1, r, 10 ** 6, 3)
                        need(dve, slot_ready, 4 * s, r, 4 * NB, 4)
                        nc.vector.tensor_reduce(CMAX[:, :], CH[:, :, :], AX.X, ALU.max).then_inc(choosing, 1)
                        nc.vector.tensor_reduce(CSUM[:, :], CH[:, :, :], AX.X, ALU.add).then_inc(choosing, 1)
                        need(dve, choosing, 3 * s + 3, r, 10 ** 6, 3)
                        if s == 0:
                            dve.wait_ge(zeroed, 16 * E)
                        for j in range(GROUP):
                            need(dve, sent[j], 32 * s, r, 10 ** 6, 32)
                        nc.vector.tensor_copy(SLOT[:, :, 0], CMAX[:, :]).then_inc(slot_ready, 1)
                        nc.vector.tensor_copy(SEND[0:T, :, D], TOKEN[:, blk]).then_inc(slot_ready, 1)
                        nc.vector.tensor_copy(SEND[0:T, :, D + 1], CMAX[:, :]).then_inc(slot_ready, 1)
                        nc.vector.tensor_tensor(SLOT[:, :, 1], CSUM[:, :], CMAX[:, :], ALU.subtract)\
                            .then_inc(slot_ready, 1)

                steps(dve, step)

            @block.scalar
            def _(act):
                def step(i, r):
                    j = i % 4
                    if i % 2 == 0 and valid(i + 2):
                        p = (i + 2) // 2
                        need(act, x1t_done, p + 1, r, B // 2, 2)
                        need(act, q_done, p, r, B // 2, 2)
                        nc.scalar.activation(X1T[:, :, :].rearrange("p a b -> p (a b)"), tr_ps[:, 0:4 * T], ACT.Copy)\
                            .then_inc(x1t_ready, 1)
                    if valid(i + 2):
                        need(act, x2t_done, i + 3, r, B)
                        need(act, s_done, i + 1, r, B)
                        nc.scalar.activation(X2T[:, i % 2, :, :], x2t_ps[0:FH, :, 0:K], ACT.Copy)\
                            .then_inc(x2t_ready, 1)
                    if i % 2 == 0 and valid(i + 2):
                        p = (i + 2) // 2
                        need(act, q_done, p + 1, r, B // 2, 2)
                        need(act, s_done, i, r, B)
                        for h in range(2):
                            nc.scalar.activation(QT[:, p % 2, h, :], q_ps[0:FH, h * 2 * T:(h + 1) * 2 * T],
                                                 ACT.Identity, bias=C[:, h:h + 1]).then_inc(q_ready, 1)
                    if valid(i - 4):
                        b = i - 4
                        need(act, xnt_done, b + 1, r, B)
                        need(act, lg_done, (b - 4) // 2 + 1, r, B // 2, 2)
                        nc.scalar.activation(XNT[:, :, bass.ds(b * T + r * BLOCK, T)],
                                             tr_ps[:, 0:2 * T].rearrange("p (a b) -> p a b", b=T), ACT.Copy)\
                            .then_inc(xnt_ready, 1)
                        nc.scalar.activation(XNS[:, :, (b % 4) * T:(b % 4 + 1) * T],
                                             tr_ps[:, 0:2 * T].rearrange("p (a b) -> p a b", b=T), ACT.Copy)\
                            .then_inc(xnt_ready, 1)
                    if valid(i + 1):
                        need(act, max_ready, i + 2, r, B)
                        need(act, pt_done, i, r, B)
                        need(act, inv_ready, i - 2, r, B)
                        nc.scalar.activation(P[:, (i + 1) % 2, :], s_ps[0:T, 0:K], ACT.Exp,
                                             bias=NMAX[:, (i + 1) % 4:(i + 1) % 4 + 1],
                                             accum_out=L[:, (i + 1) % 4:(i + 1) % 4 + 1]).then_inc(exp_ready, 1)
                    if i % 4 == 2 and 10 <= i < 10 + B:
                        s = (i - 10) // 4
                        need(act, lg_ready, 2 * s + 2, r, B // 2, 2)
                        nc.scalar.activation(EX[:, :, :], LG[:, :, :], ACT.Exp, scale=-1.0).then_inc(negexp_ready, 1)
                    if valid(i + 4):
                        b = i + 4
                        need(act, nm_ready, i + 5, r, 10 ** 6)
                        need(act, x1t_done, b // 2 - 1, r, B // 2, 2)
                        nc.scalar.activation(N1[:, b % 4, :], X[:, b + GROUP * r, :], ACT.Identity,
                                             bias=NM[0:T, j, 4:5], scale=RS[0:T, j, 4:5]).then_inc(n1_ready, 1)
                    if valid(i - 3):
                        b = i - 3
                        need(act, nm_ready, i + 5, r, 10 ** 6)
                        need(act, xnt_done, b - 1, r, B)
                        need(act, xna_full[b % 2], 16 * (b // 2), r, 16 * B // 2, 32)
                        nc.scalar.activation(XN[:, b % 2, :], X[:, b + GROUP * r, :], ACT.Identity,
                                             bias=NM[0:T, j, 3:4], scale=RS[0:T, j, 3:4]).then_inc(xn_ready, 1)
                    if isinstance(r, int) and 0 <= i < CHUNKS:
                        act.wait_ge(stage_full[i % 2], 16 * (i // 2 + 1))
                        n = CHUNK // 128
                        nc.scalar.activation(GUH[:, i * n:(i + 1) * n, :],
                                             STG[:, i % 2, :].rearrange("p (a b) -> p a b", b=128), ACT.Copy)\
                            .then_inc(whi_ready, 1)
                    if valid(i - 1):
                        b = i - 1
                        need(act, ct_done, b + 1, r, B)
                        need(act, o_done, b - 1, r, B)
                        nc.scalar.activation(CT[:, b % 2, :, :].rearrange("p a b -> p (a b)"), ct_ps[0:FH, 0:2 * T],
                                             ACT.Copy).then_inc(ct_ready, 1)

                act.sem_inc(negexp_ready, 1)
                act.wait_ge(folded, 3)
                steps(act, step)

            @block.tensor
            def _(pe):
                pe.sem_inc(off_done, 1)
                pe.wait_ge(setup_full, 16 * N_SETUP)
                for et in range(DT):
                    for dt in range(DT):
                        nc.tensor.matmul(tr_ps[:, et:et + 1], WQ[:, dt, et * 128:(et + 1) * 128], COL[:, 1, dt:dt + 1],
                                         start=dt == 0, stop=dt == DT - 1)
                for at, w in ((2, WK), (4, WV)):
                    for et in range(DT):
                        for ft in range(2):
                            last = nc.tensor.matmul(tr_ps[:, at + et:at + et + 1], w[:, ft, et * 128:(et + 1) * 128],
                                                    B2C[:, ft:ft + 1], start=ft == 0, stop=ft == 1)
                last.then_inc(bias_done, 1)
                pe.wait_ge(aug_done, 6)
                pe.wait_ge(vec_made, 7)
                for dt in range(DT):
                    for et in range(DT):
                        nc.tensor.matmul(x2t_ps[:, dt, 0:FA], WQT[:, et, dt * 128:(dt + 1) * 128], WKA[:, et, :],
                                         start=et == 0, stop=et == DT - 1)
                for h, ps in ((0, ct_ps), (1, o_ps)):
                    for et in range(DT):
                        nc.tensor.matmul(q_ps[0:FH, h:h + 1], WKA[:, et, h * FH:(h + 1) * FH], TQ[:, et:et + 1],
                                         start=et == 0, stop=et == DT - 1)
                    for et in range(DT):
                        last = nc.tensor.matmul(ps[0:FH, 0:D], WVA[:, et, h * FH:(h + 1) * FH], WO[:, et, :],
                                                start=et == 0, stop=et == DT - 1)
                last.then_inc(fold_done, 1)
                pe.wait_ge(folded, 3)
                pe.wait_ge(vo_ready, 2)
                pe.wait_ge(made, 4)

                def step(i, r):
                    if i % 2 == 0 and valid(i + 2):
                        need(pe, n1_ready, i + 4, r, B)
                        need(pe, xnt_ready, 2 * (i - 4), r, 2 * B, 2 * GROUP)
                        for kt in range(DT):
                            for jj in range(2):
                                last = nc.tensor.transpose(tr_ps[:, (2 * kt + jj) * T:(2 * kt + jj + 1) * T],
                                                           N1[:, (i + 2 + jj) % 4, kt * 128:(kt + 1) * 128],
                                                           ID[0:T, 0:T])
                        last.then_inc(x1t_done, 1)
                    if valid(i + 1):
                        b = i + 1
                        need(pe, x2t_ready, b + 1, r, B)
                        need(pe, q_ready, 2 * (b // 2 + 1), r, B, GROUP)
                        need(pe, exp_ready, b, r, B)
                        for h in range(2):
                            last = nc.tensor.matmul(s_ps[0:T, 0:K], QT[:, (b // 2) % 2, h, (b % 2) * T:(b % 2 + 1) * T],
                                                    X2T[:, b % 2, h, :], start=h == 0, stop=h == 1)
                        last.then_inc(s_done, 1)
                    if valid(i + 2):
                        b = i + 2
                        need(pe, ctx_ready, KT * (b + 1), r, KT * B, KT * GROUP)
                        need(pe, x2t_ready, b, r, B)
                        for h in range(2):
                            for t in range(KT):
                                last = nc.tensor.transpose(x2t_ps[0:FH, h, t * KP:(t + 1) * KP],
                                                           X2N[:, b % 4, t, h * FH:(h + 1) * FH], ID[0:KP, 0:KP])
                        last.then_inc(x2t_done, 1)
                    if i % 2 == 0 and valid(i + 2):
                        p = (i + 2) // 2
                        need(pe, x1t_ready, p + 1, r, B // 2, 2)
                        need(pe, q_ready, 2 * p, r, B, GROUP)
                        need(pe, lg_ready, (i - 8) // 2 + 1, r, B // 2, 2)
                        need(pe, off_ready, (i - 10) // 4 + 1, r, NB + 1, 1)
                        for h in range(2):
                            for kt in range(DT):
                                last = nc.tensor.matmul(q_ps[0:FH, h * 2 * T:(h + 1) * 2 * T],
                                                        A[:, kt, h * FH:(h + 1) * FH], X1T[:, kt, :],
                                                        start=kt == 0, stop=kt == DT - 1)
                        last.then_inc(q_done, 1)
                    if valid(i - 4):
                        b = i - 4
                        need(pe, xn_ready, b + 1, r, B)
                        need(pe, xnt_ready, 2 * b, r, 2 * B, 2 * GROUP)
                        if i % 2 == 0:
                            need(pe, x1t_ready, (i + 2) // 2 + 1, r, B // 2, 2)
                        for kt in range(DT):
                            last = nc.tensor.transpose(tr_ps[:, kt * T:(kt + 1) * T],
                                                       XN[:, b % 2, kt * 128:(kt + 1) * 128], ID[0:T, 0:T])
                        last.then_inc(xnt_done, 1)
                    if valid(i):
                        need(pe, exp_ready, i + 1, r, B)
                        need(pe, pt_ready, i, r, B)
                        for t in range(KT):
                            last = nc.tensor.transpose(pt_ps[0:KP, t * T:(t + 1) * T],
                                                       P[:, i % 2, t * KP:(t + 1) * KP], ID[0:T, 0:T])
                        last.then_inc(pt_done, 1)
                    if valid(i - 1):
                        b = i - 1
                        need(pe, pt_ready, b + 1, r, B)
                        need(pe, ct_ready, b, r, B)
                        for h in range(2):
                            for t in range(KT):
                                last = nc.tensor.matmul(ct_ps[0:FH, h * T:(h + 1) * T],
                                                        X2N[:, b % 4, t, h * FH:(h + 1) * FH], PT[:, b % 2, t, :],
                                                        start=t == 0, stop=t == KT - 1)
                        last.then_inc(ct_done, 1)
                    if valid(i - 2):
                        b = i - 2
                        need(pe, ct_ready, b + 1, r, B)
                        need(pe, xmid_ready, b, r, B)
                        if b == 0:
                            pe.wait_ge(bo_full, 16)
                        for h in range(2):
                            last = nc.tensor.matmul(o_ps[0:T, 0:D], CT[:, b % 2, h, :], VO[:, h, :],
                                                    start=h == 0, stop=h == 1)
                        last.then_inc(o_done, 1)
                    if i % 2 == 1 and valid(i - 7):
                        p = (i - 7) // 2
                        need(pe, xnt_ready, 2 * (i - 5), r, 2 * B, 2 * GROUP)
                        need(pe, q_ready, 2 * ((i + 1) // 2 + 1), r, B, GROUP)
                        need(pe, lg_ready, p, r, B // 2, 2)
                        need(pe, off_ready, (i - 10) // 4 + 1, r, NB + 1, 1)
                        for jj in range(2):
                            b = i - 7 + jj
                            for kt in range(DT):
                                last = nc.tensor.matmul(q_ps[0:T, LOGITS + jj * E:LOGITS + (jj + 1) * E],
                                                        XNS[:, kt, (b % 4) * T:(b % 4 + 1) * T], GW[:, kt, :],
                                                        start=kt == 0, stop=kt == DT - 1)
                        last.then_inc(lg_done, 1)
                    if i % 4 == 1 and 13 <= i < 13 + B:
                        s = (i - 13) // 4
                        need(pe, route_ready, 4 * s + 1, r, 10 ** 6, 4)
                        need(pe, q_ready, 2 * ((i + 1) // 2 + 1), r, B, GROUP)
                        need(pe, off_ready, s + 1, r, NB, 1)
                        for to in range(GROUP + 1):
                            parts = [(ONESB, jj) for jj in range(to)] + [(TRIB, to)] * (to < GROUP)
                            for k, (w, jj) in enumerate(parts):
                                last = nc.tensor.matmul(q_ps[0:T, to * E:(to + 1) * E], w[:, :], SELB[:, jj, :],
                                                        start=k == 0, stop=k == len(parts) - 1)
                        last.then_inc(off_done, 1)

                steps(pe, step)

        two = ExitStack()
        with two:
            def s2(name, shape, dt=F32):
                return sb(name, shape, dt, two)

            PAIRS = NT // 2
            FIELD = 4
            GATE_UP = DT * 2 * 128
            DEPTH = 4

            WDH = s2("down_hi", [128, UNITS, D], F32R)
            WDL = s2("down_lo", [128, UNITS, D], F32R)
            WD = s2("down", [128, UNITS, D])
            XSH = s2("xn_hi", [128, 2, DT, BLOCK], F32R)
            XSL = s2("xn_lo", [128, 2, DT, BLOCK], F32R)
            SG = s2("silu", [128, 2, BLOCK])
            HF = s2("hidden", [128, 2, BLOCK])
            HH = s2("hidden_hi", [128, 2, BLOCK], F32R)
            HL = s2("hidden_lo", [128, 2, BLOCK], F32R)
            XTH = s2("tile_t_hi", [128, 2, 4 * TILE], F32R)
            XTL = s2("tile_t_lo", [128, 2, 4 * TILE], F32R)
            TH = s2("tile_hidden", [TILE, 2, 2, TILE])
            THH = s2("tile_hidden_t_hi", [128, 2, 2 * TILE], F32R)
            THL = s2("tile_hidden_t_lo", [128, 2, 2 * TILE], F32R)
            YR = s2("returned", [128, 2, 2, GROUP, D])
            TOT = s2("totals", [128, 2, E])
            CNT = s2("counts", [128, E])
            INV = s2("counts_inv", [128, E])
            WM = s2("mean_weight", [128, E])
            EI = s2("expert_ids_sb", [128, E])
            TI = s2("tile_ids_sb", [128, NT])
            TS = s2("tile_starts_sb", [128, NK])
            HAS = s2("has_tile", [128, E, NK])
            TC = s2("tile_counts", [128, E])
            TCB = s2("tile_counts_before", [128, E, E])
            TF = s2("tile_first", [128, E])
            TE = s2("tile_end", [128, E])
            FL = s2("full_start", [128, E])
            TX = s2("tile_expert", [128, NT])
            TROW = s2("tile_row", [128, NT], I32)
            PK = s2("pair_units", [128, PAIRS])
            TABF = s2("tile_table_f", [128, PAIRS + 3])
            TAB = s2("tile_table", [128, PAIRS + 3], I32)

            ROWI = s2("row_ids_sb", [128, 1])
            OVER = s2("tile_overlap", [128, NT])
            ROWF = s2("tile_row_f", [128, NT])
            SKIP = s2("tile_skip", [128, NT])
            MINE = s2("tile_row_ids", [128, NT])
            SECOND = s2("is_second", [128, 2, 2])
            DESTF = s2("row_to_f", [128, 2, 2])
            DEST = s2("row_to", [128, 4, 2], I32)

            PAST = s2("past_expert", [128, NT, E])
            flat = YR[:, :, :, :, :].rearrange("p n w a d -> p (n w a d)")
            at_yo, at_sg = 8 * SW, 8 * SW + 4 * D
            XT = flat[:, 0:at_yo].rearrange("p (s k d) -> p s k d", s=4, k=2)
            YO = flat[:, at_yo:at_sg].rearrange("p (s k d) -> p s k d", s=2, k=2)
            TSG = flat[:, at_sg:at_sg + 4 * TILE].rearrange("p (s k n) -> p s k n", s=2, k=2)
            A1, A2, OH = (a.rearrange("p a b -> p (a b)")[:, 0:NT * E].rearrange("p (j e) -> p j e", e=E)
                          for a in (SG[:, :, :], HF[:, :, :], TH[:, :, :, :].rearrange("p a b c -> p (a b) c")))

            g_ps = two.enter_context(nc.psum_tensor("g_ps", [128, 2, 512], F32))
            u_ps = two.enter_context(nc.psum_tensor("u_ps", [128, 2, 512], F32))
            d_ps = two.enter_context(nc.psum_tensor("d_ps", [128, GROUP, 512], F32))

            consts_full = sem("consts_full")
            tot_done = sem("tot_done")
            tot_ready = sem("tot_ready")
            mean_chain = sem("mean_chain")
            mean_ready = sem("mean_ready")
            plan = sem("plan")
            table_ready = sem("table_ready")
            dhi_ready = sem("dhi_ready")
            dlo_ready = sem("dlo_ready")
            xhi_ready = sem("xhi_ready")
            xlo_ready = sem("xlo_ready")
            g_done = sem("g_done")
            u_done = sem("u_done")
            silu_ready = sem("silu_ready")
            h_ready = sem("h_ready")
            hhi_ready = sem("hhi_ready")
            hlo_ready = sem("hlo_ready")
            d_done = sem("d_done")
            fin_ready = sem("fin_ready")
            tile_full = [sem(f"tile_full{j}") for j in range(4)]
            tt_done = sem("tile_t_done")
            tthi_ready = sem("tile_t_hi_ready")
            ttlo_ready = sem("tile_t_lo_ready")
            tg_done = sem("tile_gate_up_done")
            tsilu_ready = sem("tile_silu_ready")
            th_ready = sem("tile_hidden_ready")
            tht_done = sem("tile_hidden_t_done")
            thhi_ready = sem("tile_hidden_hi_ready")
            thlo_ready = sem("tile_hidden_lo_ready")
            ty_done = sem("tile_out_done")
            ty_ready = sem("tile_out_ready")
            ty_sent = [sem(f"tile_out_sent{j}") for j in range(2)]
            second_ready = sem("second_ready")
            destf_ready = sem("destf_ready")
            dest_ready = sem("dest_ready")
            returned = [sem(f"returned{j}") for j in range(2)]
            adding = sem("adding_returned")
            added = sem("added_returned")
            stored = sem("stored")
            passed2 = sem("passed_a_wait2")

            def need(eng, s, n, r, per, apart=False):
                if isinstance(r, int):
                    if n > 0:
                        eng.wait_ge(s, n)
                else:
                    assert n > 0
                    eng.wait_ge(s, n + per * r)
                    if apart:
                        eng.sem_inc(passed2, 1)

            def tiles(eng, step):
                first = 6
                turns = (PAIRS - 2 - first) // 4
                for i in range(first):
                    step(i, 0)
                with eng.Fori(0, turns) as r:
                    for i in range(first, first + 4):
                        step(i, r)
                for i in range(first + 4 * turns, PAIRS + DEPTH):
                    step(i, 0)

            def pair(p):
                return 0 <= p < PAIRS

            def blocks(eng, block_step):
                block_step(1, 0)
                with eng.Fori(0, (NB - 4) // 2) as r:
                    for n in (2, 3):
                        block_step(n, r)
                for n in (NB - 2, NB - 1):
                    block_step(n, 0)

            block2 = two.enter_context(nc.Block())

            @block2.sync
            def _(sp):
                sp.dma_start(WD[:, :, :], down_t).then_inc(down_full, 16)
                for dst, src in ((EI, expert_ids), (TI, tile_ids), (TS, tile_starts), (ROWI, row_ids)):
                    sp.dma_start(dst[:, :], src).then_inc(consts_full, 16)
                for j in range(GROUP):
                    sp.wait_ge(sent[j], 32 * NB)
                sp.wait_ge(table_ready, 1)

                def load(p, r):
                    need(sp, tt_done, p - 3, r, 4, apart=True)
                    need(sp, destf_ready, p - 3, r, 4, apart=True)
                    for k in range(2):
                        row = sp.value_load(TROW[0:1, bass.ds(2 * p + k + 8 * r, 1)], min_val=0,
                                            max_val=E * R - TILE)
                        sp.dma_start(XT[:, p % 4, k, :], token_rows[bass.ds(row, TILE), :])\
                            .then_inc(tile_full[p % 4], 16)

                def step(i, r):
                    if pair(i + 2):
                        load(i + 2, r)

                load(0, 0)
                load(1, 0)
                tiles(sp, step)
                for j in range(2):
                    sp.wait_ge(ty_sent[j], 32 * PAIRS // 2)
                back = expert_rows.rearrange("(w b t) d -> t w b d", w=2, t=T)

                def fetch(n, r):
                    need(sp, added, 2 * (n - 1), r, 4)
                    for w in range(2):
                        sp.dma_start(YR[0:T, n % 2, w, :, :], back[:, w, bass.ds(GROUP * n + 2 * GROUP * r, GROUP), :])\
                            .then_inc(returned[n % 2], 16)

                def store(n, r):
                    need(sp, added, 2 * (n + 1), r, 4, apart=True)
                    rows = bass.ds(GROUP * n + 2 * GROUP * r, GROUP)
                    sp.dma_start(out_rows[:, rows, :], X[:, rows, :]).then_inc(stored, 16)

                fetch(0, 0)
                fetch(1, 0)
                with sp.Fori(0, (NB - 2) // 2) as r:
                    for n in range(2):
                        store(n, r)
                        fetch(n + 2, r)
                store(NB - 2, 0)
                store(NB - 1, 0)
                sp.wait_ge(stored, 16 * NB)

            @block2.gpsimd
            def _(pool):
                pool.wait_ge(slot_ready, 4 * NB)
                for j in range(GROUP):
                    pool.wait_ge(send_full[j], 16 * NB)
                    send(j)

                def step(i, r):
                    if pair(i - 4):
                        p = i - 4
                        need(pool, ty_ready, p + 1, r, 4, apart=True)
                        need(pool, dest_ready, p + 1, r, 4, apart=True)
                        for k in range(2):
                            nc.gpsimd.indirect_dma_start(
                                expert_rows, bass.IndirectOffsetOnAxis(ap=DEST[:, p % 4, k:k + 1], axis=0),
                                YO[:, p % 2, k, :], None, bounds_check=2 * R - 1, oob_is_err=False)\
                                .then_inc(ty_sent[p % 2], 16)

                tiles(pool, step)

            @block2.scalar
            def _(act):
                def halves(n, r):
                    need(act, g_done, 2 * (n - 1), r, 4)
                    need(act, u_done, 2 * (n - 1), r, 4)
                    nc.scalar.activation(XSH[:, n % 2, :, :], XNT[:, :, bass.ds(n * BLOCK + 2 * BLOCK * r, BLOCK)],
                                         ACT.Copy).then_inc(xhi_ready, 1)

                def unit(n, u, r):
                    q = SHARED * n + u
                    need(act, g_done, q + 1, r, 4)
                    need(act, h_ready, q - 1, r, 4)
                    nc.scalar.activation(SG[:, u, :], g_ps[:, u, 0:BLOCK], ACT.Silu).then_inc(silu_ready, 1)
                    need(act, h_ready, q + 1, r, 4)
                    need(act, d_done, q - 1, r, 4)
                    nc.scalar.activation(HH[:, u, :], HF[:, u, :], ACT.Copy).then_inc(hhi_ready, 1)

                def block_step(n, r):
                    unit(n, 0, r)
                    if n < NB - 1:
                        halves(n + 1, r)
                    unit(n, 1, r)

                def step(i, r):
                    if pair(i):
                        need(act, tt_done, i + 1, r, 4)
                        need(act, tg_done, i - 1, r, 4)
                        nc.scalar.activation(XTH[:, i % 2, :], d_ps[:, i % 2, :], ACT.Copy).then_inc(tthi_ready, 1)
                    if pair(i - 2):
                        p = i - 2
                        need(act, tht_done, p + 1, r, 4)
                        need(act, ty_done, p - 1, r, 4)
                        nc.scalar.activation(THH[:, p % 2, :], d_ps[:, 2 + p % 2, 0:2 * TILE], ACT.Copy)\
                            .then_inc(thhi_ready, 1)
                    if pair(i - 1):
                        p = i - 1
                        need(act, tg_done, p + 1, r, 4)
                        need(act, th_ready, p - 1, r, 4)
                        nc.scalar.activation(TSG[:, p % 2, :, :],
                                             g_ps[:, p % 2, :].rearrange("p (k g n) -> p k g n", k=2, g=2)[:, :, 0, :],
                                             ACT.Silu).then_inc(tsilu_ready, 1)
                    if pair(i - 3):
                        p = i - 3
                        need(act, ty_done, p + 1, r, 4)
                        need(act, ty_sent[p % 2], 32 * (p // 2), r, 64)
                        nc.scalar.activation(YO[:, p % 2, :, :].rearrange("p k d -> p (k d)"), u_ps[:, p % 2, :],
                                             ACT.Copy).then_inc(ty_ready, 1)

                halves(0, 0)
                act.wait_ge(down_full, 16)
                for u in range(SHARED):
                    nc.scalar.activation(WDH[:, u, :], WD[:, u, :], ACT.Copy).then_inc(dhi_ready, 1)
                unit(0, 0, 0)
                unit(0, 1, 0)
                act.wait_ge(mean_ready, 1)
                for e in range(E):
                    nc.scalar.activation(WDH[:, SHARED + e, :], WD[:, SHARED + e, :], ACT.Copy,
                                         scale=WM[:, e:e + 1]).then_inc(dhi_ready, 1)
                halves(1, 0)
                tiles(act, step)
                blocks(act, block_step)

            @block2.vector
            def _(dve):
                def halves(n, r):
                    need(dve, xhi_ready, n + 1, r, 2)
                    nc.vector.tensor_tensor(XSL[:, n % 2, :, :], XNT[:, :, bass.ds(n * BLOCK + 2 * BLOCK * r, BLOCK)],
                                            XSH[:, n % 2, :, :].bitcast(F32), ALU.subtract).then_inc(xlo_ready, 1)

                def unit(n, u, r):
                    q = SHARED * n + u
                    need(dve, u_done, q + 1, r, 4)
                    need(dve, silu_ready, q + 1, r, 4)
                    need(dve, hlo_ready, q - 1, r, 4)
                    need(dve, hhi_ready, q - 1, r, 4)
                    nc.vector.tensor_tensor(HF[:, u, :], u_ps[:, u, 0:BLOCK], SG[:, u, :], ALU.mult)\
                        .then_inc(h_ready, 1)
                    need(dve, hhi_ready, q + 1, r, 4)
                    need(dve, d_done, q - 1, r, 4)
                    nc.vector.tensor_tensor(HL[:, u, :], HF[:, u, :], HH[:, u, :].bitcast(F32), ALU.subtract)\
                        .then_inc(hlo_ready, 1)

                def finish(n, r):
                    need(dve, d_done, SHARED * (n + 1), r, 4)
                    for j in range(GROUP):
                        row = GROUP * n + j + 2 * GROUP * r
                        nc.vector.tensor_tensor(X[:, row, :], d_ps[0:T, j, 0:D], X[:, row, :], ALU.add)\
                            .then_inc(fin_ready, 1)

                def add_returned(n, w, r):
                    rows = bass.ds(GROUP * n + 2 * GROUP * r, GROUP)
                    need(dve, fin_ready, GROUP * (n + 1), r, 2 * GROUP)
                    need(dve, added, 2 * n + w, r, 4)
                    need(dve, returned[n % 2], 32 * (n // 2 + 1), r, 32)
                    nc.vector.tensor_tensor(X[:, rows, :], YR[0:T, n % 2, w, :, :], X[:, rows, :], ALU.add)\
                        .then_inc(added, 1)

                def block_step(n, r):
                    unit(n, 0, r)
                    if n < NB - 1:
                        halves(n + 1, r)
                    if n > 1:
                        finish(n - 1, r)
                    add_returned(n - 1, 0, r)
                    unit(n, 1, r)
                    add_returned(n - 1, 1, r)

                def step(i, r):
                    if pair(i):
                        need(dve, tthi_ready, i + 1, r, 4)
                        need(dve, tg_done, i - 1, r, 4)
                        nc.vector.tensor_tensor(XTL[:, i % 2, :], d_ps[:, i % 2, :], XTH[:, i % 2, :].bitcast(F32),
                                                ALU.subtract).then_inc(ttlo_ready, 1)
                    if pair(i - 2):
                        p = i - 2
                        need(dve, thhi_ready, p + 1, r, 4)
                        need(dve, ty_done, p - 1, r, 4)
                        nc.vector.tensor_tensor(THL[:, p % 2, :], d_ps[:, 2 + p % 2, 0:2 * TILE],
                                                THH[:, p % 2, :].bitcast(F32), ALU.subtract).then_inc(thlo_ready, 1)
                    if pair(i - 1):
                        p = i - 1
                        need(dve, tsilu_ready, p + 1, r, 4)
                        need(dve, tht_done, p - 1, r, 4)
                        nc.vector.tensor_tensor(TH[:, p % 2, :, :],
                                                g_ps[:, p % 2, :].rearrange("p (k g n) -> p k g n", k=2, g=2)[:, :, 1, :],
                                                TSG[:, p % 2, :, :], ALU.mult).then_inc(th_ready, 1)
                    if pair(i):
                        at = bass.ds(2 * i + 8 * r, 2)
                        need(dve, tile_full[i % 4], 32 * (i // 4 + 1), r, 32)
                        need(dve, destf_ready, i - 1, r, 4)
                        nc.vector.tensor_tensor(SECOND[:, i % 2, :], XT[:, i % 4, :, D + 1], MINE[:, at], ALU.is_gt)\
                            .then_inc(second_ready, 1)
                    if pair(i - 1):
                        p = i - 1
                        need(dve, second_ready, p + 1, r, 4)
                        need(dve, dest_ready, p - 1, r, 4)
                        nc.vector.scalar_tensor_tensor(out=DESTF[:, p % 2, :], in0=SECOND[:, p % 2, :],
                                                       scalar=float(R), in1=XT[:, p % 4, :, D], op0=ALU.mult,
                                                       op1=ALU.add).then_inc(destf_ready, 1)
                    if pair(i - 2):
                        p = i - 2
                        need(dve, destf_ready, p + 1, r, 4)
                        need(dve, ty_sent[p % 2], 32 * (p // 2 - 1), r, 64)
                        nc.vector.tensor_tensor(DEST[:, p % 4, :], DESTF[:, p % 2, :],
                                                SKIP[:, bass.ds(2 * p + 8 * r, 2)], ALU.add).then_inc(dest_ready, 1)

                halves(0, 0)
                dve.wait_ge(tot_done, 1)
                nc.vector.tensor_reduce(TOT[:, :, :], d_ps[:, 0, :].rearrange("p (w b e) -> p w e b", w=2, e=E),
                                        AX.X, ALU.add).then_inc(tot_ready, 1)
                dve.wait_ge(tot_ready, 1)
                nc.vector.tensor_scalar(CNT[:, :], TOT[:, 1, :], 1.0, None, ALU.max).then_inc(mean_chain, 1)
                dve.wait_ge(mean_chain, 1)
                nc.vector.reciprocal(INV[:, :], CNT[:, :]).then_inc(mean_chain, 1)
                dve.wait_ge(mean_chain, 2)
                nc.vector.tensor_tensor(WM[:, :], TOT[:, 0, :], INV[:, :], ALU.mult).then_inc(mean_ready, 1)
                for u in range(SHARED):
                    dve.wait_ge(dhi_ready, u + 1)
                    nc.vector.tensor_tensor(WDL[:, u, :], WD[:, u, :], WDH[:, u, :].bitcast(F32),
                                            ALU.subtract).then_inc(dlo_ready, 1)
                unit(0, 0, 0)
                unit(0, 1, 0)

                def over_tiles(a):
                    return a.unsqueeze(1).broadcast_to([128, NT, E])

                count = TOT[:, 1, :]
                tile = TI[:, :].unsqueeze(2).broadcast_to([128, NT, E])
                dve.wait_ge(consts_full, 64)
                nc.vector.tensor_tensor(HAS[:, :, :], count.unsqueeze(2).broadcast_to([128, E, NK]),
                                        TS[:, :].unsqueeze(1).broadcast_to([128, E, NK]), ALU.is_gt).then_inc(plan, 1)
                nc.vector.tensor_scalar(FL[:, :], count, -float(TILE), None, ALU.add).then_inc(plan, 1)
                dve.wait_ge(plan, 2)
                nc.vector.tensor_reduce(TC[:, :], HAS[:, :, :], AX.X, ALU.add).then_inc(plan, 1)
                dve.wait_ge(plan, 3)
                nc.vector.tensor_tensor(TCB[:, :, :], BEFORE[:, :, :], TC[:, :].unsqueeze(1).broadcast_to([128, E, E]),
                                        ALU.mult).then_inc(plan, 1)
                dve.wait_ge(plan, 4)
                nc.vector.tensor_reduce(TF[:, :], TCB[:, :, :], AX.X, ALU.add).then_inc(plan, 1)
                dve.wait_ge(plan, 5)
                nc.vector.tensor_tensor(TE[:, :], TF[:, :], TC[:, :], ALU.add).then_inc(plan, 1)
                nc.vector.tensor_tensor(A1[:, :, :], tile, over_tiles(TF[:, :]), ALU.subtract).then_inc(plan, 1)
                dve.wait_ge(plan, 7)
                nc.vector.tensor_tensor(PAST[:, :, :], over_tiles(TE[:, :]), tile, ALU.is_le).then_inc(plan, 1)
                nc.vector.scalar_tensor_tensor(out=A2[:, :, :], in0=A1[:, :, :], scalar=float(TILE),
                                               in1=over_tiles(FL[:, :]), op0=ALU.mult, op1=ALU.min).then_inc(plan, 1)
                dve.wait_ge(plan, 9)
                nc.vector.tensor_reduce(TX[:, :], PAST[:, :, :], AX.X, ALU.add).then_inc(plan, 1)
                nc.vector.scalar_tensor_tensor(out=A1[:, :, :], in0=A2[:, :, :], scalar=0.0,
                                               in1=over_tiles(ER[:, :]), op0=ALU.max, op1=ALU.add).then_inc(plan, 1)
                dve.wait_ge(plan, 11)
                nc.vector.tensor_scalar(TX[:, :], TX[:, :], float(E - 1), None, ALU.min).then_inc(plan, 1)
                dve.wait_ge(plan, 12)
                nc.vector.tensor_tensor(OH[:, :, :], TX[:, :].unsqueeze(2).broadcast_to([128, NT, E]),
                                        over_tiles(EI[:, :]), ALU.is_equal).then_inc(plan, 1)
                nc.vector.memset(TABF[:, :], 0.0).then_inc(plan, 1)
                pairs = TX[:, :].rearrange("p (i k) -> p i k", k=2)
                nc.vector.scalar_tensor_tensor(out=PK[:, :], in0=pairs[:, :, 1], scalar=float(1 << FIELD),
                                               in1=pairs[:, :, 0], op0=ALU.mult, op1=ALU.add).then_inc(plan, 1)
                dve.wait_ge(plan, 15)
                nc.vector.tensor_tensor(A2[:, :, :], A1[:, :, :], OH[:, :, :], ALU.mult).then_inc(plan, 1)
                dve.wait_ge(plan, 16)
                nc.vector.tensor_reduce(PAST[:, :, 0], A2[:, :, :], AX.X, ALU.add).then_inc(plan, 1)
                units = float(SHARED + (SHARED << FIELD))
                nc.vector.tensor_scalar(PK[:, :], PK[:, :], units, None, ALU.add).then_inc(plan, 1)
                dve.wait_ge(plan, 18)
                nc.vector.tensor_copy(TROW[:, :], PAST[:, :, 0]).then_inc(table_ready, 1)
                nc.vector.tensor_scalar(MINE[:, :], PAST[:, :, 0], ROWI[:, 0:1], None, ALU.add).then_inc(table_ready, 1)
                nc.vector.tensor_scalar(TABF[:, 1:PAIRS + 1], PK[:, :], float(GATE_UP), None, ALU.mult)\
                    .then_inc(plan, 1)
                dve.wait_ge(plan, 19)
                nc.vector.scalar_tensor_tensor(out=TABF[:, 3:PAIRS + 3], in0=PK[:, :],
                                               scalar=float(GATE_UP << 2 * FIELD), in1=TABF[:, 3:PAIRS + 3],
                                               op0=ALU.mult, op1=ALU.add).then_inc(plan, 1)
                dve.wait_ge(plan, 20)
                nc.vector.tensor_copy(TAB[:, :], TABF[:, :]).then_inc(table_ready, 1)
                nc.vector.tensor_tensor(A1[:, :, :], tile, over_tiles(TF[:, :]), ALU.subtract).then_inc(plan, 1)
                dve.wait_ge(plan, 21)
                nc.vector.scalar_tensor_tensor(out=A2[:, :, :], in0=A1[:, :, :], scalar=float(TILE),
                                               in1=over_tiles(ER[:, :]), op0=ALU.mult, op1=ALU.add).then_inc(plan, 1)
                dve.wait_ge(plan, 22)
                nc.vector.tensor_tensor(A1[:, :, :], A2[:, :, :], OH[:, :, :], ALU.mult).then_inc(plan, 1)
                dve.wait_ge(plan, 23)
                nc.vector.tensor_reduce(ROWF[:, :], A1[:, :, :], AX.X, ALU.add).then_inc(plan, 1)
                dve.wait_ge(plan, 24)
                nc.vector.tensor_tensor(OVER[:, :], ROWF[:, :], PAST[:, :, 0], ALU.subtract).then_inc(plan, 1)
                dve.wait_ge(plan, 25)
                nc.vector.tensor_scalar(SKIP[:, :], OVER[:, :], ROWI[:, 0:1], NOWHERE, ALU.is_gt, ALU.mult)\
                    .then_inc(plan, 1)

                finish(0, 0)
                for e in range(E):
                    u = SHARED + e
                    dve.wait_ge(dhi_ready, u + 1)
                    nc.vector.scalar_tensor_tensor(out=WDL[:, u, :], in0=WD[:, u, :],
                                                   scalar=WM[:, e:e + 1], in1=WDH[:, u, :].bitcast(F32),
                                                   op0=ALU.mult, op1=ALU.subtract).then_inc(dlo_ready, 1)
                halves(1, 0)

                dve.wait_ge(table_ready, 3)
                dve.wait_ge(plan, 26)
                tiles(dve, step)

                blocks(dve, block_step)
                finish(NB - 1, 0)
                add_returned(NB - 1, 0, 0)
                add_returned(NB - 1, 1, 0)

            @block2.tensor
            def _(pe):
                def gate_up(n, u, r):
                    q = SHARED * n + u
                    if u == 0:
                        need(pe, xhi_ready, n + 1, r, 2)
                        need(pe, xlo_ready, n + 1, r, 2)
                    for g, ps, free, done in ((0, g_ps, silu_ready, g_done), (1, u_ps, h_ready, u_done)):
                        need(pe, free, q - 1, r, 4)
                        k = 0
                        for kt in range(DT):
                            at = (u * DT + kt) * 2 + g
                            for w, v in ((GUH, XSH), (GUH, XSL), (GUL, XSH)):
                                last = nc.tensor.matmul(ps[:, u, 0:BLOCK], w[:, at, :], v[:, n % 2, kt, :],
                                                        start=k == 0, stop=k == 3 * DT - 1)
                                k += 1
                        last.then_inc(done, 1)

                def down(n, u, r):
                    q = SHARED * n + u
                    need(pe, hlo_ready, q + 1, r, 4)
                    need(pe, hhi_ready, q + 1, r, 4)
                    if u == 0:
                        need(pe, fin_ready, GROUP * n, r, 2 * GROUP)
                    for j in range(GROUP):
                        k = 0
                        for h, w in ((HH, WDH), (HH, WDL), (HL, WDH)):
                            last = nc.tensor.matmul(d_ps[0:T, j, 0:D], h[:, u, j * T:(j + 1) * T], w[:, u, :],
                                                    start=u == 0 and k == 0, stop=u == 1 and k == 2)
                            k += 1
                    last.then_inc(d_done, 1)

                guh, gul, wdh, wdl = (w.rearrange("p a n -> p (a n)") for w in
                                      (GUH[:, :, :], GUL[:, :, :], WDH[:, :, :], WDL[:, :, :]))

                def offset(table, field, size):
                    shift = field * FIELD + (GATE_UP.bit_length() - size.bit_length())
                    return nc.s_assert_within((table >> shift if shift else table) & (15 * size), 0,
                                              (UNITS - 1) * size,
                                              skip_runtime_bounds_check_because="the table is made of units")

                def step(i, r):
                    if pair(i - 1) or pair(i - 3):
                        table = nc.values_load(TAB[0:1, bass.ds(i + 4 * r, 1)], engines=(pe.engine,), min_val=0,
                                               max_val=(GATE_UP << 4 * FIELD) - 1,
                                               skip_runtime_bounds_check_because="it has four fields")
                    if pair(i):
                        need(pe, tile_full[i % 4], 32 * (i // 4 + 1), r, 32)
                        need(pe, ttlo_ready, i - 1, r, 4)
                        for k in range(2):
                            for kt in range(DT):
                                last = nc.tensor.transpose(d_ps[:, i % 2, (k * DT + kt) * TILE:(k * DT + kt + 1) * TILE],
                                                           XT[:, i % 4, k, kt * 128:(kt + 1) * 128], ID[:, :])
                        last.then_inc(tt_done, 1)
                    if pair(i - 2):
                        p = i - 2
                        need(pe, th_ready, p + 1, r, 4)
                        need(pe, thlo_ready, p - 1, r, 4)
                        for k in range(2):
                            last = nc.tensor.transpose(d_ps[:, 2 + p % 2, k * TILE:(k + 1) * TILE],
                                                       TH[:, p % 2, k, :], ID[:, :])
                        last.then_inc(tht_done, 1)
                    if pair(i - 1):
                        p = i - 1
                        need(pe, tthi_ready, p + 1, r, 4)
                        need(pe, ttlo_ready, p + 1, r, 4)
                        need(pe, th_ready, p - 1, r, 4)
                        for k in range(2):
                            at = offset(table, k, GATE_UP)
                            n = 0
                            for kt in range(DT):
                                cols = slice((k * DT + kt) * TILE, (k * DT + kt + 1) * TILE)
                                for w, v in ((guh, XTH), (gul, XTH), (guh, XTL)):
                                    last = nc.tensor.matmul(g_ps[:, p % 2, k * 256:(k + 1) * 256], v[:, p % 2, cols],
                                                            w[:, bass.ds(at + kt * 2 * TILE, 2 * TILE)],
                                                            start=n == 0, stop=n == 3 * DT - 1)
                                    n += 1
                        last.then_inc(tg_done, 1)
                    if pair(i - 3):
                        p = i - 3
                        need(pe, thhi_ready, p + 1, r, 4)
                        need(pe, thlo_ready, p + 1, r, 4)
                        need(pe, ty_ready, p - 1, r, 4)
                        for k in range(2):
                            at = offset(table, 2 + k, D)
                            for n, (w, v) in enumerate(((wdh, THH), (wdl, THH), (wdh, THL))):
                                last = nc.tensor.matmul(u_ps[:, p % 2, k * D:(k + 1) * D],
                                                        v[:, p % 2, k * TILE:(k + 1) * TILE],
                                                        w[:, bass.ds(at, D)],
                                                        start=n == 0, stop=n == 2)
                        last.then_inc(ty_done, 1)

                nc.tensor.matmul(d_ps[:, 0, :], ONES[:, :], ROUTE[:, :, :, :].rearrange("p w b e -> p (w b e)"),
                                 start=True, stop=True).then_inc(tot_done, 1)
                gate_up(0, 0, 0)
                gate_up(0, 1, 0)
                pe.wait_ge(dlo_ready, SHARED)
                pe.wait_ge(tot_ready, 1)
                down(0, 0, 0)
                down(0, 1, 0)

                pe.wait_ge(fin_ready, GROUP)
                pe.wait_ge(h_ready, SHARED)
                pe.wait_ge(table_ready, 3)
                pe.wait_ge(dlo_ready, UNITS)
                tiles(pe, step)

                pe.wait_ge(th_ready, PAIRS)
                pe.wait_ge(ty_ready, PAIRS)

                def block_step(n, r):
                    gate_up(n, 0, r)
                    if n > 1:
                        down(n - 1, 1, r)
                    gate_up(n, 1, r)
                    down(n, 0, r)

                blocks(pe, block_step)
                down(NB - 1, 1, 0)


def kernel(x, ctx_768, L0_xattn_ln1_g, L0_xattn_ln1_b, L0_xattn_ln2_g, L0_xattn_ln2_b, L0_xattn_Wq, L0_xattn_bq,
           L0_xattn_Wk, L0_xattn_bk, L0_xattn_Wv, L0_xattn_bv, L0_xattn_Wo, L0_xattn_bo, L0_ffn_gate_w,
           L0_ffn_lb_bias, L0_ffn_expert_gate_w, L0_ffn_expert_up_w, L0_ffn_expert_down_w, L0_ffn_shared_gate_w,
           L0_ffn_shared_up_w, L0_ffn_shared_down_w):
    import numpy as np
    import concourse.bacc as bacc
    from concourse.bass_utils import run_bass_kernel_spmd

    a = np.asarray
    T = x.shape[1]
    E = L0_ffn_lb_bias.shape[0]
    tokens = x.shape[0] * T
    tiles = 2 * tokens // 128 + E
    rows = lambda v: np.broadcast_to(v.astype(np.float32), (128, v.shape[0]))
    cols = lambda v: a(v).reshape(2, 128).T
    halves = lambda w: a(w).reshape(-1, 128, a(w).shape[-1])
    gate = np.concatenate([halves(L0_ffn_shared_gate_w), a(L0_ffn_expert_gate_w)])
    up = np.concatenate([halves(L0_ffn_shared_up_w), a(L0_ffn_expert_up_w)])
    gate_up = np.stack([gate, up], axis=1).reshape(-1, 2, 128, 2, 128).transpose(4, 0, 3, 1, 2).reshape(128, -1)
    shared_down = a(L0_ffn_shared_down_w).T.reshape(2, 128, -1)
    down = np.concatenate([shared_down, a(L0_ffn_expert_down_w).transpose(0, 2, 1)]).transpose(1, 0, 2)
    ins = {
        "x": a(x), "ctx_in": a(ctx_768),
        "wq_t": a(L0_xattn_Wq).T, "wq": a(L0_xattn_Wq), "wk_t": a(L0_xattn_Wk).T, "wk": a(L0_xattn_Wk),
        "wv_t": a(L0_xattn_Wv).T, "wv": a(L0_xattn_Wv), "wo": a(L0_xattn_Wo),
        "g2_rows": np.broadcast_to(a(L0_xattn_ln2_g), (128, 192)),
        "columns": np.stack([cols(v) for v in (L0_xattn_ln1_g, L0_xattn_ln1_b, L0_xattn_bq, L0_xattn_bk,
                                               L0_xattn_bv)], axis=1),
        "b2_columns": a(L0_xattn_ln2_b).reshape(2, 96).T,
        "bo": a(L0_xattn_bo).reshape(1, -1),
        "gate_w_t": a(L0_ffn_gate_w).T,
        "lb_rows": np.broadcast_to(a(L0_ffn_lb_bias), (T, 8)),
        "gate_up_t": gate_up, "down_t": down,
        "region_rows": rows(np.arange(E) * tokens), "expert_ids": rows(np.arange(E)),
        "tile_ids": rows(np.arange(tiles)), "tile_starts": rows(np.arange(0, tokens, 128)),
        "token_ids": np.arange(tokens).reshape(-1, T).T.astype(np.float32),
        "row_ids": np.arange(128).reshape(128, 1).astype(np.float32),
    }
    nc = bacc.Bacc("TRN2", target_bir_lowering=False, num_devices=1)
    arrays, args = {}, {}
    for name, v in ins.items():
        v = np.ascontiguousarray(v)
        arrays[f"in_{name}"] = v
        args[name] = nc.dram_tensor(f"in_{name}", v.shape, mybir.dt.from_np(v.dtype), kind="ExternalInput").ap()
    out = nc.dram_tensor("out_0", x.shape, F32, kind="ExternalOutput").ap()
    token_rows = nc.dram_tensor("token_rows", [E * tokens, x.shape[2] + 2], F32, kind="Internal").ap()
    expert_rows = nc.dram_tensor("expert_rows", [2 * tokens, x.shape[2]], F32, kind="Internal").ap()
    attention_and_experts(nc, **args, expert_rows=expert_rows, token_rows=token_rows, out=out)
    r = run_bass_kernel_spmd(nc, [arrays], core_ids=[0])
    return r.results[0]["out_0"]
```

```python
from contextlib import ExitStack

import concourse.bass as bass
from concourse import mybir

F32 = mybir.dt.float32
F32R = mybir.dt.float32r
BF16 = mybir.dt.bfloat16
I32 = mybir.dt.int32
ALU = mybir.AluOpType
ACT = mybir.ActivationFunctionType
AX = mybir.AxisListType

EPS = 1e-5
NOWHERE = float(2 ** 20)
GROUP = 4
LEAD = 15
TILE = 128


def attention_and_experts(nc, x, ctx_in, wq_t, wq, wk_t, wk, wv_t, wv, wo, g2_rows, columns, b2_columns,
                          bo, gate_w_t, lb_rows, gate_up_t, down_t, region_rows, expert_ids, tile_ids, tile_starts,
                          token_ids, row_ids,
                          expert_rows, token_rows, out):
    B, T, D = x.shape
    K, DC = ctx_in.shape[1:]
    KT = 3
    KP = K // KT
    DT = D // 128
    FA = DC + 2
    FH = FA // 2
    E = lb_rows.shape[1]
    UNITS = down_t.shape[1]
    SHARED = UNITS - E
    BLOCK = GROUP * T
    NB = B // GROUP
    TURNS = NB - 5
    R = B * T
    NT = tile_ids.shape[1]
    NK = tile_starts.shape[1]
    SW = token_rows.shape[1]
    LAST = 39
    SCALE = float(D) ** -0.5
    CHUNKS = 8
    CHUNK = gate_up_t.shape[1] // CHUNKS
    assert T * GROUP == BLOCK and KP * KT == K and LEAD + GROUP * TURNS + 5 <= B

    x_rows = x.rearrange("b t d -> t b d")
    out_rows = out.rearrange("b t d -> t b d")
    ctx_rows = ctx_in.rearrange("b (p t) d -> p b t d", t=KT)

    top = ExitStack()
    with top:
        def sb(name, shape, dt=F32, where=top):
            return where.enter_context(nc.sbuf_tensor(name, shape, dt))

        def sem(name):
            return top.enter_context(nc.semaphore(name))

        X = sb("x_sb", [T, B, D])
        XNT = sb("xn_t_all", [128, DT, B * T])
        GUH = sb("gate_up_hi", [128, 2 * DT * UNITS, 128], F32R)
        GUL = sb("gate_up_lo", [128, 2 * DT * UNITS, 128], F32R)
        ROUTE = sb("route", [T, 2, B, E])
        ID = sb("identity", [128, 128])
        ER = sb("region_first", [128, E])
        BEFORE = sb("before", [128, E, E])
        SEND = sb("send", [128, GROUP, SW])
        TOKEN = sb("token_ids_sb", [T, B])
        SLOT = sb("send_rows", [T, GROUP, 2], I32)
        SEND_LAST = sb("send_last", [128, GROUP, SW])
        SLOT_LAST = sb("send_rows_last", [T, GROUP, 2], I32)
        ONES = sb("ones", [T, 128])

        send_full = [sem(f"send_full{j}") for j in range(GROUP)]
        sent = [sem(f"sent{j}") for j in range(GROUP)]
        slot_ready = sem("slot_ready")
        down_full = sem("down_full")

        def send(j, rows, slots):
            for k in range(2):
                nc.gpsimd.indirect_dma_start(token_rows, bass.IndirectOffsetOnAxis(ap=slots[:, j, k:k + 1], axis=0),
                                             rows[0:T, j, :], None, bounds_check=E * R - 1, oob_is_err=False)\
                    .then_inc(sent[j], 16)

        ONESB = sb("ones_bf", [T, T], BF16)
        TRIB = sb("earlier_bf", [T, T], BF16)
        EX = sb("exp_minus", [T, GROUP, E])
        EX1 = sb("one_plus_exp", [T, GROUP, E])
        SC = sb("route_scores", [T, GROUP, E])
        GT = sb("greater", [T, GROUP, E, E])
        GE = sb("greater_equal", [T, GROUP, E, E])
        GEB = sb("greater_equal_before", [T, GROUP, E, E])
        AHEAD = sb("is_ahead", [T, GROUP, E, E])
        RK = sb("rank", [T, GROUP, E])
        SELB = sb("selected_bf", [T, GROUP, E], BF16)
        BASE = sb("region_next", [T, E])
        ROWS = sb("region_rows_group", [T, GROUP, E])
        CH = sb("chosen_rows", [T, GROUP, E])
        CMAX = sb("chosen_max", [T, GROUP])
        CSUM = sb("chosen_sum", [T, GROUP])
        SS = sb("selected_scores", [T, GROUP, E])
        SM = sb("score_sum", [T, GROUP])
        SE = sb("score_sum_eps", [T, GROUP])
        SI = sb("score_sum_inv", [T, GROUP])
        rows_ready = sem("rows_ready")
        choosing = sem("choosing")
        zeroed = sem("zeroed")
        negexp_ready = sem("negexp_ready")
        denominator = sem("sigmoid_denominator")
        scored = sem("scored")
        compared = sem("compared")
        ranking = sem("ranking")
        ranked = sem("ranked")
        routing = sem("routing")
        route_ready = sem("route_ready")
        off_done = sem("off_done")
        off_ready = sem("off_ready")
        passed = sem("passed_a_wait")

        def need(eng, s, n, r, top_value, per=GROUP, apart=False):
            if isinstance(r, int):
                n = min(n, top_value)
                if n > 0:
                    eng.wait_ge(s, n)
            elif apart:
                assert n > 0
                eng.wait_ge(s, n + per * r)
                eng.sem_inc(passed, 1)
            else:
                assert n > 0
                eng.wait_ge(s, n + per * r)

        def rank(dve, s, r):
            need(dve, compared, 2 * s + 2, r, 2 * NB, 2)
            nc.vector.tensor_tensor(GEB[:, :, :, :], GE[:, :, :, :],
                                    BEFORE[0:T, :, :].unsqueeze(1).broadcast_to([T, GROUP, E, E]),
                                    ALU.mult).then_inc(ranking, 1)
            need(dve, ranking, 2 * s + 1, r, 2 * NB, 2)
            nc.vector.tensor_tensor(AHEAD[:, :, :, :], GT[:, :, :, :], GEB[:, :, :, :], ALU.max)\
                .then_inc(ranking, 1)
            need(dve, ranking, 2 * s + 2, r, 2 * NB, 2)
            nc.vector.tensor_reduce(RK[:, :, :], AHEAD[:, :, :, :], AX.X, ALU.add).then_inc(ranked, 1)

        def score(dve, s, r):
            need(dve, negexp_ready, s + 2, r, NB + 1, 1)
            nc.vector.tensor_scalar(EX1[:, :, :], EX[:, :, :], 1.0, None, ALU.add).then_inc(denominator, 1)
            need(dve, denominator, s + 1, r, NB, 1)
            need(dve, ranked, s + 1, r, NB + 1, 1)
            nc.vector.reciprocal(SC[:, :, :], EX1[:, :, :]).then_inc(scored, 1)
            need(dve, scored, s + 1, r, NB, 1)
            of_j = SC[:, :, :].unsqueeze(2).broadcast_to([T, GROUP, E, E])
            of_e = SC[:, :, :].unsqueeze(3).broadcast_to([T, GROUP, E, E])
            nc.vector.tensor_tensor(GT[:, :, :, :], of_j, of_e, ALU.is_gt).then_inc(compared, 1)
            nc.vector.tensor_tensor(GE[:, :, :, :], of_j, of_e, ALU.is_ge).then_inc(compared, 1)

        RC = 3

        def route(dve, s, r):
            def then(k):
                need(dve, routing, RC * s + k, r, 10 ** 6, RC)

            need(dve, ranked, s + 2, r, NB + 1, 1)
            need(dve, off_done, s + 1, r, NB + 1, 1)
            blk = bass.ds(s * GROUP + r * GROUP, GROUP)
            nc.vector.tensor_scalar(SELB[:, :, :], RK[:, :, :], 1.5, None, ALU.is_lt)\
                .then_inc(route_ready, 1)
            nc.vector.scalar_tensor_tensor(out=SS[:, :, :], in0=RK[:, :, :], scalar=1.5, in1=SC[:, :, :],
                                           op0=ALU.is_lt, op1=ALU.mult).then_inc(routing, 1)
            nc.vector.tensor_scalar(ROUTE[:, 1, blk, :], RK[:, :, :], 1.5, None, ALU.is_lt)\
                .then_inc(route_ready, 1)
            then(1)
            nc.vector.tensor_reduce(SM[:, :], SS[:, :, :], AX.X, ALU.add).then_inc(routing, 1)
            then(2)
            nc.vector.tensor_scalar(SE[:, :], SM[:, :], 1e-8, None, ALU.add).then_inc(routing, 1)
            then(3)
            nc.vector.reciprocal(SI[:, :], SE[:, :]).then_inc(route_ready, 1)
            need(dve, route_ready, 4 * s + 3, r, 10 ** 6, 4)
            nc.vector.tensor_tensor(ROUTE[:, 0, blk, :], SS[:, :, :],
                                    SI[:, :].unsqueeze(2).broadcast_to([T, GROUP, E]), ALU.mult)\
                .then_inc(route_ready, 1)

        def place(dve, s, r, ps, rows, slots):
            need(dve, off_done, s + 2, r, NB + 1, 1)
            need(dve, off_ready, s + 1, r, NB + 1, 1)
            blk = bass.ds(s * GROUP + r * GROUP, GROUP)
            nc.vector.tensor_tensor(ROWS[:, :, :],
                                    ps[:, 0:GROUP * E].rearrange("p (a e) -> p a e", e=E),
                                    BASE[:, :].unsqueeze(1).broadcast_to([T, GROUP, E]), ALU.add)\
                .then_inc(rows_ready, 1)
            need(dve, rows_ready, s + 1, r, NB, 1)
            nc.vector.tensor_tensor(BASE[:, :], ps[:, GROUP * E:(GROUP + 1) * E], BASE[:, :], ALU.add)\
                .then_inc(off_ready, 1)
            nc.vector.tensor_tensor(CH[:, :, :], ROWS[:, :, :], ROUTE[:, 1, blk, :], ALU.mult)\
                .then_inc(choosing, 1)
            need(dve, choosing, 3 * s + 1, r, 10 ** 6, 3)
            need(dve, slot_ready, 4 * s, r, 4 * NB, 4)
            nc.vector.tensor_reduce(CMAX[:, :], CH[:, :, :], AX.X, ALU.max).then_inc(choosing, 1)
            nc.vector.tensor_reduce(CSUM[:, :], CH[:, :, :], AX.X, ALU.add).then_inc(choosing, 1)
            need(dve, choosing, 3 * s + 3, r, 10 ** 6, 3)
            if s == 0:
                dve.wait_ge(zeroed, 16 * E)
            for j in range(GROUP):
                if slots is SLOT:
                    need(dve, sent[j], 32 * s, r, 10 ** 6, 32)
            nc.vector.tensor_copy(slots[:, :, 0], CMAX[:, :]).then_inc(slot_ready, 1)
            nc.vector.tensor_copy(rows[0:T, :, D], TOKEN[:, blk]).then_inc(slot_ready, 1)
            nc.vector.tensor_copy(rows[0:T, :, D + 1], CMAX[:, :]).then_inc(slot_ready, 1)
            nc.vector.tensor_tensor(slots[:, :, 1], CSUM[:, :], CMAX[:, :], ALU.subtract)\
                .then_inc(slot_ready, 1)

        def count_rows(ps):
            for to in range(GROUP + 1):
                parts = [(ONESB, jj) for jj in range(to)] + [(TRIB, to)] * (to < GROUP)
                for k, (w, jj) in enumerate(parts):
                    last = nc.tensor.matmul(ps[:, to * E:(to + 1) * E], w[:, :], SELB[:, jj, :],
                                            start=k == 0, stop=k == len(parts) - 1)
            return last


        one = ExitStack()
        with one:
            def s1(name, shape, dt=F32):
                return sb(name, shape, dt, one)

            G2 = s1("g2_sb", [128, DC])
            COL = s1("columns_sb", [128, 5, DT])
            B2C = s1("b2_columns_sb", [DC // 2, 2])
            LBR = s1("lb_rows_sb", [T, E])
            GW = s1("gate_w_sb", [128, DT, E])
            WKA = s1("wk_aug", [128, DT, FA])
            WVA = s1("wv_aug", [128, DT, FA])
            G1S = s1("g1_scaled", [128, DT])
            TQ = s1("q_bias", [128, DT])
            A = s1("a_sb", [128, DT, FA])
            C = s1("c_sb", [FH, 2])
            VO = s1("vo_sb", [FH, 2, D])
            HALF = s1("minus_half", [128, 5])
            STG = s1("stage", [128, 2, CHUNK])

            RAW = s1("ctx_raw", [KP, 4, KT, DC])
            X2N = s1("ctx_norm", [KP, 4, KT, FA])
            N1 = s1("x_norm", [T, 4, D])
            X1T = s1("x_norm_t", [128, DT, 2 * T])
            QT = s1("q_t", [FH, 2, 2, 2 * T])
            X2T = s1("ctx_norm_t", [FH, 2, 2, K])
            P = s1("probs", [T, 2, K])
            PT = s1("probs_t", [KP, 2, KT, T])
            CT = s1("context_t", [FH, 2, 2, T])
            XN = s1("x2_norm", [T, 2, D])
            XNS = s1("xn_t", [128, DT, BLOCK])
            XNA = s1("x2_norm_all", [T, B - GROUP, D])
            ST = s1("stats", [128, 5, 6])
            MV = s1("mean_var", [128, 4, 5, 2])
            VE = s1("var_eps", [128, 4, 5])
            RS = s1("rstd", [128, 4, 5])
            NM = s1("minus_mean_rstd", [128, 4, 5])
            NMAX = s1("minus_max", [T, 4])
            L = s1("row_sum", [T, 4])
            RL = s1("row_sum_inv", [T, 4])
            LG = s1("logits_sb", [T, GROUP, E])

            spare = XNS[:, :, :].rearrange("p a b -> p (a b)")
            WQT = spare[:, 0:DT * D].rearrange("p (t n) -> p t n", t=DT)
            WKT = spare[:, DT * D:DT * (D + DC)].rearrange("p (t n) -> p t n", t=DT)
            WVT = X1T[:, :, :].rearrange("p a b -> p (a b)")[:, 0:DT * DC].rearrange("p (t n) -> p t n", t=DT)
            WQ = STG[:, 0, 0:DT * D].rearrange("p (t n) -> p t n", t=DT)
            WO = STG[:, 1, 0:DT * D].rearrange("p (t n) -> p t n", t=DT)
            WK = N1[0:DC // 2, 0:2, :]
            WV = N1[0:DC // 2, 2:4, :]

            x2t_ps = one.enter_context(nc.psum_tensor("x2t_ps", [128, 2, 512], F32))
            s_ps = one.enter_context(nc.psum_tensor("s_ps", [128, 512], F32))
            pt_ps = one.enter_context(nc.psum_tensor("pt_ps", [128, 512], F32))
            ct_ps = one.enter_context(nc.psum_tensor("ct_ps", [128, 512], F32))
            o_ps = one.enter_context(nc.psum_tensor("o_ps", [128, 512], F32))
            tr_ps = one.enter_context(nc.psum_tensor("tr_ps", [128, 512], F32))
            q_ps = one.enter_context(nc.psum_tensor("q_ps", [128, 512], F32))
            LOGITS = 2 * 2 * T

            setup_full = sem("setup_full")
            bo_full = sem("bo_full")
            x_first = sem("x_first")
            x_rest = sem("x_rest")
            raw_full = [sem(f"raw_full{j}") for j in range(4)]
            stage_full = [sem(f"stage_full{j}") for j in range(2)]
            made = sem("made_by_pool")
            cleared = sem("cleared")
            bias_done = sem("bias_done")
            aug_done = sem("aug_done")
            fold_done = sem("fold_done")
            folded = sem("folded")
            vo_ready = sem("vo_ready")
            vec_made = sem("made_by_vector")
            ctx_stats = sem("ctx_stats")
            ctx_mv = sem("ctx_mv")
            x_stats = sem("x_stats")
            x_mv = sem("x_mv")
            x2_stats = sem("x2_stats")
            x2_mv = sem("x2_mv")
            var_ready = sem("var_ready")
            rstd_ready = sem("rstd_ready")
            nm_ready = sem("nm_ready")
            ctx_ready = sem("ctx_norm_ready")
            n1_ready = sem("n1_ready")
            x1t_done = sem("x1t_done")
            x1t_ready = sem("x1t_ready")
            q_done = sem("q_done")
            q_ready = sem("q_ready")
            x2t_done = sem("x2t_done")
            x2t_ready = sem("x2t_ready")
            s_done = sem("s_done")
            max_ready = sem("max_ready")
            exp_ready = sem("exp_ready")
            inv_ready = sem("inv_ready")
            pt_done = sem("pt_done")
            pt_ready = sem("pt_ready")
            ct_done = sem("ct_done")
            ct_ready = sem("ct_ready")
            o_done = sem("o_done")
            xmid_ready = sem("xmid_ready")
            xn_ready = sem("xn_ready")
            xnt_done = sem("xnt_done")
            xnt_ready = sem("xnt_ready")
            xna_full = [sem(f"xna_full{j}") for j in range(2)]
            base_ready = sem("base_ready")
            lg_done = sem("lg_done")
            lg_ready = sem("lg_ready")
            whi_ready = sem("whi_ready")
            wlo_ready = sem("wlo_ready")

            def valid(b):
                return 0 <= b < B

            def steps(eng, step, first=-5):
                for i in range(first, LEAD):
                    step(i, 0)
                with eng.Fori(0, TURNS) as r:
                    for i in range(LEAD, LEAD + GROUP):
                        step(i, r)
                for i in range(LEAD + GROUP * TURNS, LAST):
                    step(i, 0)

            N_SETUP = 14
            block = one.enter_context(nc.Block())

            @block.sync
            def _(sp):
                two = lambda a: a.rearrange("(t p) n -> p t n", t=2)
                for dst, src in ((WKT[:, :, :], two(wk_t)), (G2[:, :], g2_rows), (COL[:, :, :], columns),
                                 (WQ[:, :, :], two(wq)), (B2C[:, :], b2_columns), (WK[:, :, :], two(wk)),
                                 (WV[:, :, :], two(wv))):
                    sp.dma_start(dst, src).then_inc(setup_full, 16)
                sp.dma_start(X[:, 0:GROUP, :], x_rows[:, 0:GROUP, :]).then_inc(x_first, 16)
                for j in range(4):
                    sp.dma_start(RAW[:, j, :, :], ctx_rows[:, j, :, :]).then_inc(raw_full[j], 16)
                sp.dma_start(X[:, GROUP:B, :], x_rows[:, GROUP:B, :]).then_inc(x_rest, 16)
                sp.wait_ge(vo_ready, 2)
                sp.dma_start(VO[FH - 1:FH, 1, :], bo).then_inc(bo_full, 16)
                sp.wait_ge(cleared, 5)
                for e in range(E):
                    sp.dma_start(token_rows[e * R:e * R + TILE, :], SEND[:, 0, :]).then_inc(zeroed, 16)

                def step(i, r):
                    if valid(i + 5) and i + 5 >= GROUP:
                        b = i + 5
                        need(sp, ctx_ready, KT * (b - 3), r, KT * B, KT * GROUP)
                        sp.dma_start(RAW[:, b % 4, :, :], ctx_rows[:, b + GROUP * r, :, :])\
                            .then_inc(raw_full[b % 4], 16)
                    if isinstance(r, int) and 0 <= i + 2 < CHUNKS:
                        k = i + 2
                        if k >= 2:
                            sp.wait_ge(wlo_ready, k - 1)
                        sp.dma_start(STG[:, k % 2, :], gate_up_t[:, k * CHUNK:(k + 1) * CHUNK])\
                            .then_inc(stage_full[k % 2], 16)
                    if valid(i - 3):
                        b = i - 3
                        need(sp, xn_ready, b + 1, r, B)
                        last_ones = isinstance(r, int) and b >= B - GROUP
                        sp.dma_start(SEND_LAST[0:T, b % 4, 0:D] if last_ones else XNA[:, b + GROUP * r, :],
                                     XN[:, b % 2, :]).then_inc(xna_full[b % 2], 16)
                    if valid(i - 11):
                        b = i - 11
                        need(sp, xna_full[b % 2], 16 * (b // 2 + 1), r, 16 * B // 2, 32, apart=True)
                        if b < GROUP and isinstance(r, int):
                            sp.wait_ge(zeroed, 16 * E)
                        need(sp, sent[b % 4], 32 * (b // 4), r, 10 ** 6, 32)
                        sp.dma_start(SEND[0:T, b % 4, 0:D], XNA[:, b + GROUP * r, :]).then_inc(send_full[b % 4], 16)

                steps(sp, step)
                sp.wait_ge(bo_full, 16)
                for j in range(2):
                    sp.wait_ge(xna_full[j], 16 * B // 2)

            @block.gpsimd
            def _(pool):
                nc.gpsimd.memset(ID[:, :], 0.0).then_inc(cleared, 1)
                nc.gpsimd.memset(BEFORE[:, :, :], 1.0).then_inc(cleared, 1)
                nc.gpsimd.memset(SEND[:, 0, 0:D], 0.0).then_inc(cleared, 1)
                nc.gpsimd.memset(SEND[:, 0, D:SW], NOWHERE).then_inc(cleared, 1)
                nc.gpsimd.memset(P[:, 0, 0:T], 1.0).then_inc(cleared, 1)
                nc.gpsimd.memset(HALF[:, :], -0.5).then_inc(made, 1)
                pool.wait_ge(cleared, 5)
                nc.gpsimd.affine_select(out=ID[:, :], in_=ID[:, :], compare_op=ALU.not_equal, fill=1.0, base=0,
                                        pattern=[[-1, 128]], channel_multiplier=1).then_inc(made, 1)
                nc.gpsimd.affine_select(out=BEFORE[:, :, :], in_=BEFORE[:, :, :], compare_op=ALU.is_gt, fill=0.0,
                                        base=0, pattern=[[1, E], [-1, E]], channel_multiplier=0).then_inc(made, 1)
                nc.gpsimd.affine_select(out=P[:, 0, 0:T], in_=P[:, 0, 0:T], compare_op=ALU.is_gt, fill=0.0,
                                        base=0, pattern=[[1, T]], channel_multiplier=-1).then_inc(made, 1)
                pool.wait_ge(made, 4)


                def step(i, r):
                    j = i % 4
                    if -4 <= i <= B + 2:
                        need(pool, var_ready, 2 * (i + 5), r, 10 ** 6, 2 * GROUP)
                        need(pool, n1_ready, i + 1, r, B)
                        need(pool, xn_ready, i - 6, r, B)
                        nc.gpsimd.tensor_tensor(RS[:, j, :], VE[:, j, :], HALF[:, :], ALU.pow).then_inc(rstd_ready, 1)
                    if valid(i + 3):
                        need(pool, nm_ready, i + 5, r, 10 ** 6)
                        need(pool, ct_done, i, r, B)
                        need(pool, raw_full[(i + 3) % 4], 16 * ((i + 3) // 4 + 1), r, 10 ** 6, 16, apart=True)
                        for t in range(KT):
                            nc.gpsimd.tensor_scalar(X2N[:, (i + 3) % 4, t, 0:DC], RAW[:, (i + 3) % 4, t, :],
                                                    RS[0:KP, j, t:t + 1], NM[0:KP, j, t:t + 1],
                                                    ALU.mult, ALU.add).then_inc(ctx_ready, 1)
                    if isinstance(r, int) and 0 <= i < CHUNKS:
                        pool.wait_ge(whi_ready, i + 1)
                        n = CHUNK // 128
                        nc.gpsimd.tensor_tensor(GUL[:, i * n:(i + 1) * n, :],
                                                STG[:, i % 2, :].rearrange("p (a b) -> p a b", b=128),
                                                GUH[:, i * n:(i + 1) * n, :].bitcast(F32),
                                                ALU.subtract).then_inc(wlo_ready, 1)
                    for first, js in ((14, (0, 1)), (15, (2,)), (16, (3,))):
                        s = (i - first) // 4
                        if i % 4 == first % 4 and 0 <= s < NB - 2:
                            for j in js:
                                need(pool, slot_ready, 4 * (s + 1), r, 4 * NB, 4, apart=True)
                                need(pool, send_full[j], 16 * (s + 1), r, 16 * NB, 16, apart=True)
                                send(j, SEND, SLOT)

                steps(pool, step)

            @block.vector
            def _(dve):
                nc.vector.memset(ONES[:, :], 1.0).then_inc(vec_made, 1)
                nc.vector.memset(MV[:, :, :, :], 1.0).then_inc(vec_made, 1)
                nc.vector.memset(WVA[:, :, FA - 1:FA], 0.0).then_inc(vec_made, 1)
                nc.vector.memset(WKA[:, :, FA - 1:FA], 0.0).then_inc(vec_made, 1)
                nc.vector.memset(X2N[:, :, :, DC:FA], 1.0).then_inc(vec_made, 1)
                dve.wait_ge(made, 4)
                nc.vector.tensor_copy(TRIB[:, :], P[:, 0, 0:T]).then_inc(vec_made, 1)
                nc.vector.memset(ONESB[:, :], 1.0).then_inc(vec_made, 1)
                dve.wait_ge(vec_made, 7)

                def norms(i, r):
                    m = (i + 1) % 4
                    if valid(i + 4):
                        need(dve, raw_full[(i + 4) % 4], 16 * ((i + 4) // 4 + 1), r, 10 ** 6, 16)
                        for t in range(KT):
                            nc.vector.bn_stats(ST[0:KP, t, :], RAW[:, (i + 4) % 4, t, :]).then_inc(ctx_stats, 1)
                    if valid(i + 5):
                        if i + 5 < GROUP:
                            dve.wait_ge(x_first, 16)
                        else:
                            dve.wait_ge(x_rest, 16)
                        nc.vector.bn_stats(ST[0:T, 4, :], X[:, i + 5 + GROUP * r, :]).then_inc(x_stats, 1)
                    if valid(i - 2):
                        need(dve, xmid_ready, i - 1, r, B, apart=True)
                        nc.vector.bn_stats(ST[0:T, 3, :], X[:, i - 2 + GROUP * r, :]).then_inc(x2_stats, 1)
                    if valid(i + 4):
                        need(dve, ctx_stats, KT * (i + 5), r, KT * B, KT * GROUP, apart=True)
                        for t in range(KT):
                            nc.vector.bn_aggr(MV[0:KP, m, t, :], ST[0:KP, t, :]).then_inc(ctx_mv, 1)
                    if valid(i + 5):
                        need(dve, x_stats, i + 6, r, B, apart=True)
                        nc.vector.bn_aggr(MV[0:T, m, 4, :], ST[0:T, 4, :]).then_inc(x_mv, 1)
                    if valid(i - 2):
                        need(dve, x2_stats, i - 1, r, B, apart=True)
                        nc.vector.bn_aggr(MV[0:T, m, 3, :], ST[0:T, 3, :]).then_inc(x2_mv, 1)
                    if -4 <= i + 1 <= B + 2:
                        need(dve, ctx_mv, KT * (i + 5), r, KT * B, KT * GROUP)
                        need(dve, x_mv, i + 6, r, B)
                        need(dve, x2_mv, i - 1, r, B)
                        need(dve, rstd_ready, i + 2, r, 10 ** 6)
                        nc.vector.tensor_scalar(VE[:, m, 0:4], MV[:, m, 0:4, 1], EPS, None, ALU.add)\
                            .then_inc(var_ready, 1)
                        nc.vector.tensor_scalar(VE[:, m, 4:5], MV[:, m, 4:5, 1], 1.0 + EPS, EPS * EPS, ALU.mult,
                                                ALU.add).then_inc(var_ready, 1)

                dve.sem_inc(off_ready, 1)
                dve.sem_inc(ranked, 1)
                def step(i, r):
                    if i % 2 == 0 and valid(i - 8):
                        p = (i - 8) // 2
                        need(dve, lg_done, p + 1, r, B // 2, 2)
                        need(dve, negexp_ready, p // 2 + 1, r, NB + 1, 1)
                        nc.vector.tensor_tensor(LG[:, 2 * (p % 2):2 * (p % 2) + 2, :],
                                                q_ps[0:T, LOGITS:LOGITS + 2 * E].rearrange("p (a e) -> p a e", e=E),
                                                LBR[:, :].unsqueeze(1).broadcast_to([T, 2, E]), ALU.add)\
                            .then_inc(lg_ready, 1)
                    if valid(i - 2):
                        need(dve, exp_ready, i - 1, r, B)
                        nc.vector.reciprocal(RL[:, (i - 2) % 4:(i - 2) % 4 + 1], L[:, (i - 2) % 4:(i - 2) % 4 + 1])\
                            .then_inc(inv_ready, 1)
                    if valid(i + 1):
                        need(dve, s_done, i + 2, r, B)
                        nc.vector.tensor_reduce(NMAX[:, (i + 1) % 4:(i + 1) % 4 + 1], s_ps[0:T, 0:K], AX.X, ALU.max,
                                                negate=True).then_inc(max_ready, 1)
                    if -4 <= i <= B + 2:
                        need(dve, rstd_ready, i + 5, r, 10 ** 6)
                        need(dve, n1_ready, i + 1, r, B)
                        need(dve, xn_ready, i - 6, r, B)
                        need(dve, ctx_ready, KT * i, r, KT * B, KT * GROUP)
                        nc.vector.scalar_tensor_tensor(out=NM[:, i % 4, :], in0=MV[:, i % 4, :, 0], scalar=-1.0,
                                                       in1=RS[:, i % 4, :], op0=ALU.mult, op1=ALU.mult)\
                            .then_inc(nm_ready, 1)
                    if valid(i):
                        need(dve, pt_done, i + 1, r, B)
                        need(dve, ct_done, i - 1, r, B)
                        nc.vector.tensor_copy(PT[:, i % 2, :, :].rearrange("p a b -> p (a b)"), pt_ps[0:KP, 0:KT * T])\
                            .then_inc(pt_ready, 1)
                    if valid(i - 2):
                        b = i - 2
                        need(dve, inv_ready, b + 1, r, B)
                        need(dve, o_done, b + 1, r, B)
                        nc.vector.scalar_tensor_tensor(out=X[:, b + GROUP * r, :], in0=o_ps[0:T, 0:D],
                                                       scalar=RL[:, b % 4:b % 4 + 1], in1=X[:, b + GROUP * r, :],
                                                       op0=ALU.mult, op1=ALU.add).then_inc(xmid_ready, 1)
                    norms(i, r)
                    if i % 4 == 2 and 10 <= i < 6 + B:
                        score(dve, (i - 10) // 4, r)
                    if i % 4 == 3 and 11 <= i < 3 + B:
                        rank(dve, (i - 11) // 4, r)
                    if i % 4 == 0 and 12 <= i < 4 + B:
                        route(dve, (i - 12) // 4, r)
                    if i % 4 == 1 and 13 <= i < 5 + B:
                        s = (i - 13) // 4
                        place(dve, s, r, q_ps[0:T, 0:(GROUP + 1) * E], SEND, SLOT)

                dve.wait_ge(setup_full, 16 * N_SETUP)
                g2b = G2[:, :].unsqueeze(1).broadcast_to([128, DT, DC])
                nc.vector.tensor_tensor(WKA[:, :, 0:DC], WKT[:, :, :], g2b, ALU.mult).then_inc(aug_done, 1)
                nc.vector.tensor_tensor(WVA[:, :, 0:DC], WVT[:, :, :], g2b, ALU.mult).then_inc(aug_done, 1)
                nc.vector.tensor_scalar(G1S[:, :], COL[:, 0, :], SCALE, None, ALU.mult).then_inc(aug_done, 1)
                nc.vector.tensor_copy(BASE[:, :], ER[0:T, :]).then_inc(base_ready, 1)
                dve.wait_ge(bias_done, 1)
                nc.vector.tensor_tensor(TQ[:, :], tr_ps[:, 0:2], COL[:, 2, :], ALU.add).then_inc(aug_done, 1)
                nc.vector.tensor_tensor(WKA[:, :, DC], tr_ps[:, 2:4], COL[:, 3, :], ALU.add).then_inc(aug_done, 1)
                nc.vector.tensor_tensor(WVA[:, :, DC], tr_ps[:, 4:6], COL[:, 4, :], ALU.add).then_inc(aug_done, 1)
                for i in (-5, -4, -3):
                    step(i, 0)
                dve.wait_ge(fold_done, 1)
                dve.wait_ge(aug_done, 6)
                for dt in range(DT):
                    nc.vector.tensor_scalar(A[:, dt, :], x2t_ps[:, dt, 0:FA], G1S[:, dt:dt + 1], None, ALU.mult)\
                        .then_inc(folded, 1)
                nc.vector.tensor_scalar(C[:, :], q_ps[0:FH, 0:2], SCALE, None, ALU.mult).then_inc(folded, 1)
                nc.vector.tensor_copy(VO[:, 0, :], ct_ps[0:FH, 0:D]).then_inc(vo_ready, 1)
                nc.vector.tensor_copy(VO[:, 1, :], o_ps[0:FH, 0:D]).then_inc(vo_ready, 1)
                dve.wait_ge(base_ready, 1)

                steps(dve, step, -2)

            @block.scalar
            def _(act):
                def step(i, r):
                    j = i % 4
                    if i % 2 == 0 and valid(i + 2):
                        p = (i + 2) // 2
                        need(act, x1t_done, p + 1, r, B // 2, 2)
                        need(act, q_done, p, r, B // 2, 2)
                        nc.scalar.activation(X1T[:, :, :].rearrange("p a b -> p (a b)"), tr_ps[:, 0:4 * T], ACT.Copy)\
                            .then_inc(x1t_ready, 1)
                    if valid(i + 2):
                        need(act, x2t_done, i + 3, r, B)
                        need(act, s_done, i + 1, r, B)
                        nc.scalar.activation(X2T[:, i % 2, :, :], x2t_ps[0:FH, :, 0:K], ACT.Copy)\
                            .then_inc(x2t_ready, 1)
                    if i % 2 == 0 and valid(i + 2):
                        p = (i + 2) // 2
                        need(act, q_done, p + 1, r, B // 2, 2)
                        need(act, s_done, i, r, B)
                        for h in range(2):
                            nc.scalar.activation(QT[:, p % 2, h, :], q_ps[0:FH, h * 2 * T:(h + 1) * 2 * T],
                                                 ACT.Identity, bias=C[:, h:h + 1]).then_inc(q_ready, 1)
                    if valid(i - 4):
                        b = i - 4
                        need(act, xnt_done, b + 1, r, B)
                        need(act, lg_done, (b - 4) // 2 + 1, r, B // 2, 2)
                        nc.scalar.activation(XNT[:, :, bass.ds(b * T + r * BLOCK, T)],
                                             tr_ps[:, 0:2 * T].rearrange("p (a b) -> p a b", b=T), ACT.Copy)\
                            .then_inc(xnt_ready, 1)
                        nc.scalar.activation(XNS[:, :, (b % 4) * T:(b % 4 + 1) * T],
                                             tr_ps[:, 0:2 * T].rearrange("p (a b) -> p a b", b=T), ACT.Copy)\
                            .then_inc(xnt_ready, 1)
                    if valid(i + 1):
                        need(act, max_ready, i + 2, r, B)
                        need(act, pt_done, i, r, B)
                        need(act, inv_ready, i - 2, r, B)
                        nc.scalar.activation(P[:, (i + 1) % 2, :], s_ps[0:T, 0:K], ACT.Exp,
                                             bias=NMAX[:, (i + 1) % 4:(i + 1) % 4 + 1],
                                             accum_out=L[:, (i + 1) % 4:(i + 1) % 4 + 1]).then_inc(exp_ready, 1)
                    if i % 4 == 2 and 10 <= i < 10 + B:
                        s = (i - 10) // 4
                        need(act, lg_ready, 2 * s + 2, r, B // 2, 2)
                        nc.scalar.activation(EX[:, :, :], LG[:, :, :], ACT.Exp, scale=-1.0).then_inc(negexp_ready, 1)
                    if valid(i + 4):
                        b = i + 4
                        need(act, nm_ready, i + 5, r, 10 ** 6)
                        need(act, x1t_done, b // 2 - 1, r, B // 2, 2)
                        nc.scalar.activation(N1[:, b % 4, :], X[:, b + GROUP * r, :], ACT.Identity,
                                             bias=NM[0:T, j, 4:5], scale=RS[0:T, j, 4:5]).then_inc(n1_ready, 1)
                    if valid(i - 3):
                        b = i - 3
                        need(act, nm_ready, i + 5, r, 10 ** 6)
                        need(act, xnt_done, b - 1, r, B)
                        need(act, xna_full[b % 2], 16 * (b // 2), r, 16 * B // 2, 32)
                        nc.scalar.activation(XN[:, b % 2, :], X[:, b + GROUP * r, :], ACT.Identity,
                                             bias=NM[0:T, j, 3:4], scale=RS[0:T, j, 3:4]).then_inc(xn_ready, 1)
                    if isinstance(r, int) and 0 <= i < CHUNKS:
                        act.wait_ge(stage_full[i % 2], 16 * (i // 2 + 1))
                        n = CHUNK // 128
                        nc.scalar.activation(GUH[:, i * n:(i + 1) * n, :],
                                             STG[:, i % 2, :].rearrange("p (a b) -> p a b", b=128), ACT.Copy)\
                            .then_inc(whi_ready, 1)
                    if valid(i - 1):
                        b = i - 1
                        need(act, ct_done, b + 1, r, B)
                        need(act, o_done, b - 1, r, B)
                        nc.scalar.activation(CT[:, b % 2, :, :].rearrange("p a b -> p (a b)"), ct_ps[0:FH, 0:2 * T],
                                             ACT.Copy).then_inc(ct_ready, 1)

                two = lambda a: a.rearrange("(t p) n -> p t n", t=2)
                for dst, src in ((WVT[:, :, :], two(wv_t)), (WQT[:, :, :], two(wq_t)), (WO[:, :, :], two(wo)),
                                 (LBR[:, :], lb_rows), (GW[:, :, :], two(gate_w_t)), (ER[:, :], region_rows),
                                 (TOKEN[:, :], token_ids)):
                    act.dma_start(dst, src).then_inc(setup_full, 16)
                act.sem_inc(negexp_ready, 1)
                act.wait_ge(bias_done, 1)
                steps(act, step)

            @block.tensor
            def _(pe):
                pe.sem_inc(off_done, 1)
                pe.wait_ge(setup_full, 16 * N_SETUP)
                for et in range(DT):
                    for dt in range(DT):
                        nc.tensor.matmul(tr_ps[:, et:et + 1], WQ[:, dt, et * 128:(et + 1) * 128], COL[:, 1, dt:dt + 1],
                                         start=dt == 0, stop=dt == DT - 1)
                for at, w in ((2, WK), (4, WV)):
                    for et in range(DT):
                        for ft in range(2):
                            last = nc.tensor.matmul(tr_ps[:, at + et:at + et + 1], w[:, ft, et * 128:(et + 1) * 128],
                                                    B2C[:, ft:ft + 1], start=ft == 0, stop=ft == 1)
                last.then_inc(bias_done, 1)
                pe.wait_ge(aug_done, 6)
                pe.wait_ge(vec_made, 7)
                for dt in range(DT):
                    for et in range(DT):
                        nc.tensor.matmul(x2t_ps[:, dt, 0:FA], WQT[:, et, dt * 128:(dt + 1) * 128], WKA[:, et, :],
                                         start=et == 0, stop=et == DT - 1)
                for h, ps in ((0, ct_ps), (1, o_ps)):
                    for et in range(DT):
                        nc.tensor.matmul(q_ps[0:FH, h:h + 1], WKA[:, et, h * FH:(h + 1) * FH], TQ[:, et:et + 1],
                                         start=et == 0, stop=et == DT - 1)
                    for et in range(DT):
                        last = nc.tensor.matmul(ps[0:FH, 0:D], WVA[:, et, h * FH:(h + 1) * FH], WO[:, et, :],
                                                start=et == 0, stop=et == DT - 1)
                last.then_inc(fold_done, 1)
                pe.wait_ge(folded, 3)
                pe.wait_ge(vo_ready, 2)
                pe.wait_ge(made, 4)

                def step(i, r):
                    if i % 2 == 0 and valid(i + 2):
                        need(pe, n1_ready, i + 4, r, B)
                        need(pe, xnt_ready, 2 * (i - 4), r, 2 * B, 2 * GROUP)
                        for kt in range(DT):
                            for jj in range(2):
                                last = nc.tensor.transpose(tr_ps[:, (2 * kt + jj) * T:(2 * kt + jj + 1) * T],
                                                           N1[:, (i + 2 + jj) % 4, kt * 128:(kt + 1) * 128],
                                                           ID[0:T, 0:T])
                        last.then_inc(x1t_done, 1)
                    if valid(i + 1):
                        b = i + 1
                        need(pe, x2t_ready, b + 1, r, B)
                        need(pe, q_ready, 2 * (b // 2 + 1), r, B, GROUP)
                        need(pe, exp_ready, b, r, B)
                        for h in range(2):
                            last = nc.tensor.matmul(s_ps[0:T, 0:K], QT[:, (b // 2) % 2, h, (b % 2) * T:(b % 2 + 1) * T],
                                                    X2T[:, b % 2, h, :], start=h == 0, stop=h == 1)
                        last.then_inc(s_done, 1)
                    if valid(i + 2):
                        b = i + 2
                        need(pe, ctx_ready, KT * (b + 1), r, KT * B, KT * GROUP)
                        need(pe, x2t_ready, b, r, B)
                        for h in range(2):
                            for t in range(KT):
                                last = nc.tensor.transpose(x2t_ps[0:FH, h, t * KP:(t + 1) * KP],
                                                           X2N[:, b % 4, t, h * FH:(h + 1) * FH], ID[0:KP, 0:KP])
                        last.then_inc(x2t_done, 1)
                    if i % 2 == 0 and valid(i + 2):
                        p = (i + 2) // 2
                        need(pe, x1t_ready, p + 1, r, B // 2, 2)
                        need(pe, q_ready, 2 * p, r, B, GROUP)
                        need(pe, lg_ready, (i - 8) // 2 + 1, r, B // 2, 2)
                        need(pe, off_ready, (i - 10) // 4 + 1, r, NB + 1, 1)
                        for h in range(2):
                            for kt in range(DT):
                                last = nc.tensor.matmul(q_ps[0:FH, h * 2 * T:(h + 1) * 2 * T],
                                                        A[:, kt, h * FH:(h + 1) * FH], X1T[:, kt, :],
                                                        start=kt == 0, stop=kt == DT - 1)
                        last.then_inc(q_done, 1)
                    if valid(i - 4):
                        b = i - 4
                        need(pe, xn_ready, b + 1, r, B)
                        need(pe, xnt_ready, 2 * b, r, 2 * B, 2 * GROUP)
                        if i % 2 == 0:
                            need(pe, x1t_ready, (i + 2) // 2 + 1, r, B // 2, 2)
                        for kt in range(DT):
                            last = nc.tensor.transpose(tr_ps[:, kt * T:(kt + 1) * T],
                                                       XN[:, b % 2, kt * 128:(kt + 1) * 128], ID[0:T, 0:T])
                        last.then_inc(xnt_done, 1)
                    if valid(i):
                        need(pe, exp_ready, i + 1, r, B)
                        need(pe, pt_ready, i, r, B)
                        for t in range(KT):
                            last = nc.tensor.transpose(pt_ps[0:KP, t * T:(t + 1) * T],
                                                       P[:, i % 2, t * KP:(t + 1) * KP], ID[0:T, 0:T])
                        last.then_inc(pt_done, 1)
                    if valid(i - 1):
                        b = i - 1
                        need(pe, pt_ready, b + 1, r, B)
                        need(pe, ct_ready, b, r, B)
                        for h in range(2):
                            for t in range(KT):
                                last = nc.tensor.matmul(ct_ps[0:FH, h * T:(h + 1) * T],
                                                        X2N[:, b % 4, t, h * FH:(h + 1) * FH], PT[:, b % 2, t, :],
                                                        start=t == 0, stop=t == KT - 1)
                        last.then_inc(ct_done, 1)
                    if valid(i - 2):
                        b = i - 2
                        need(pe, ct_ready, b + 1, r, B)
                        need(pe, xmid_ready, b, r, B)
                        if b == 0:
                            pe.wait_ge(bo_full, 16)
                        for h in range(2):
                            last = nc.tensor.matmul(o_ps[0:T, 0:D], CT[:, b % 2, h, :], VO[:, h, :],
                                                    start=h == 0, stop=h == 1)
                        last.then_inc(o_done, 1)
                    if i % 2 == 1 and valid(i - 7):
                        p = (i - 7) // 2
                        need(pe, xnt_ready, 2 * (i - 5), r, 2 * B, 2 * GROUP)
                        need(pe, q_ready, 2 * ((i + 1) // 2 + 1), r, B, GROUP)
                        need(pe, lg_ready, p, r, B // 2, 2)
                        need(pe, off_ready, (i - 10) // 4 + 1, r, NB + 1, 1)
                        for jj in range(2):
                            b = i - 7 + jj
                            for kt in range(DT):
                                last = nc.tensor.matmul(q_ps[0:T, LOGITS + jj * E:LOGITS + (jj + 1) * E],
                                                        XNS[:, kt, (b % 4) * T:(b % 4 + 1) * T], GW[:, kt, :],
                                                        start=kt == 0, stop=kt == DT - 1)
                        last.then_inc(lg_done, 1)
                    if i % 4 == 1 and 13 <= i < 5 + B:
                        s = (i - 13) // 4
                        need(pe, route_ready, 4 * s + 1, r, 10 ** 6, 4)
                        need(pe, q_ready, 2 * ((i + 1) // 2 + 1), r, B, GROUP)
                        need(pe, off_ready, s + 1, r, NB, 1)
                        count_rows(q_ps[0:T, 0:(GROUP + 1) * E]).then_inc(off_done, 1)

                steps(pe, step)

        two = ExitStack()
        with two:
            def s2(name, shape, dt=F32):
                return sb(name, shape, dt, two)

            PAIRS = NT // 2
            FIELD = 4
            GATE_UP = DT * 2 * 128
            DEPTH = 4

            WDH = s2("down_hi", [128, UNITS, D], F32R)
            WDL = s2("down_lo", [128, UNITS, D], F32R)
            WD = s2("down", [128, UNITS, D])
            XSH = s2("xn_hi", [128, 2, DT, BLOCK], F32R)
            XSL = s2("xn_lo", [128, 2, DT, BLOCK], F32R)
            SG = s2("silu", [128, 2, BLOCK])
            HF = s2("hidden", [128, 2, BLOCK])
            HH = s2("hidden_hi", [128, 2, BLOCK], F32R)
            HL = s2("hidden_lo", [128, 2, BLOCK], F32R)
            XTH = s2("tile_t_hi", [128, 2, 4 * TILE], F32R)
            XTL = s2("tile_t_lo", [128, 2, 4 * TILE], F32R)
            TH = s2("tile_hidden", [TILE, 2, 2, TILE])
            THH = s2("tile_hidden_t_hi", [128, 2, 2 * TILE], F32R)
            THL = s2("tile_hidden_t_lo", [128, 2, 2 * TILE], F32R)
            YR = s2("returned", [128, 2, 2, GROUP, D])
            PART = s2("totals_parts", [T, 2, E])
            TOT = s2("totals", [128, 2, E])
            CNT = s2("counts", [128, E])
            INV = s2("counts_inv", [128, E])
            WM = s2("mean_weight", [128, E])
            TC = s2("tile_counts", [128, E])
            TF = s2("tile_first", [128, E])
            TE = s2("tile_end", [128, E])
            FL = s2("full_start", [128, E])
            TROW = s2("tile_row", [128, NT], I32)
            TAB = s2("tile_table", [128, PAIRS + 3], I32)

            ROWI = s2("row_ids_sb", [128, 1])
            DEST = s2("row_to", [128, 4, 2], I32)

            flat = YR[:, :, :, :, :].rearrange("p n w a d -> p (n w a d)")
            at_yo, at_sg = 8 * SW, 8 * SW + 4 * D
            XT = flat[:, 0:at_yo].rearrange("p (s k d) -> p s k d", s=4, k=2)
            YO = flat[:, at_yo:at_sg].rearrange("p (s k d) -> p s k d", s=2, k=2)
            TSG = flat[:, at_sg:at_sg + 4 * TILE].rearrange("p (s k n) -> p s k n", s=2, k=2)
            PAST = TSG.rearrange("p s k (j e) -> p (s k j) e", e=E)
            HAS = flat[:, 0:E * NK].rearrange("p (e k) -> p e k", k=NK)
            TCB = flat[:, E * NK:E * (NK + E)].rearrange("p (e j) -> p e j", j=E)
            at = E * (NK + E)
            TI, TS, EI = flat[:, at:at + NT], flat[:, at + NT:at + NT + NK], flat[:, at + NT + NK:at + NT + NK + E]
            behind = at_sg + 4 * TILE
            OVER = flat[:, behind:behind + NT]
            ROWF = flat[:, behind + NT:behind + 2 * NT]
            PK = flat[:, behind + 2 * NT:behind + 2 * NT + PAIRS]
            TABF = flat[:, behind + 3 * NT:behind + 3 * NT + PAIRS + 3]
            TX = flat[:, behind + 4 * NT:behind + 5 * NT]
            MINE = flat[:, behind + 5 * NT:behind + 6 * NT]
            SKIP = flat[:, behind + 6 * NT:behind + 7 * NT]
            SECOND, DESTF = (flat[:, behind + 7 * NT + 4 * a:behind + 7 * NT + 4 * a + 4]
                             .rearrange("p (s k) -> p s k", k=2) for a in range(2))
            A1, A2 = (YO[:, a, :, :].rearrange("p k (j e) -> p (k j) e", e=E) for a in range(2))
            OH = TH[:, :, :, :].rearrange("p s k (j e) -> p (s k j) e", e=E)

            g_ps = two.enter_context(nc.psum_tensor("g_ps", [128, 2, 512], F32))
            u_ps = two.enter_context(nc.psum_tensor("u_ps", [128, 2, 512], F32))
            d_ps = two.enter_context(nc.psum_tensor("d_ps", [128, GROUP, 512], F32))
            COUNTS = d_ps[0:T, 2, 0:(GROUP + 1) * E]
            TOTALS = d_ps[:, 3, 0:2 * E]

            consts_full = sem("consts_full")
            shared_full = sem("shared_full")
            part_ready = sem("part_ready")
            tot_done = sem("tot_done")
            tot_ready = sem("tot_ready")
            mean_chain = sem("mean_chain")
            mean_ready = sem("mean_ready")
            plan = sem("plan")
            table_ready = sem("table_ready")
            dhi_ready = sem("dhi_ready")
            dlo_ready = sem("dlo_ready")
            xhi_ready = sem("xhi_ready")
            xlo_ready = sem("xlo_ready")
            g_done = sem("g_done")
            u_done = sem("u_done")
            silu_ready = sem("silu_ready")
            h_ready = sem("h_ready")
            hhi_ready = sem("hhi_ready")
            hlo_ready = sem("hlo_ready")
            d_done = sem("d_done")
            fin_ready = sem("fin_ready")
            tile_full = [sem(f"tile_full{j}") for j in range(4)]
            tt_done = sem("tile_t_done")
            tthi_ready = sem("tile_t_hi_ready")
            ttlo_ready = sem("tile_t_lo_ready")
            tg_done = sem("tile_gate_up_done")
            tsilu_ready = sem("tile_silu_ready")
            th_ready = sem("tile_hidden_ready")
            tht_done = sem("tile_hidden_t_done")
            thhi_ready = sem("tile_hidden_hi_ready")
            thlo_ready = sem("tile_hidden_lo_ready")
            ty_done = sem("tile_out_done")
            ty_ready = sem("tile_out_ready")
            ty_sent = [sem(f"tile_out_sent{j}") for j in range(2)]
            second_ready = sem("second_ready")
            destf_ready = sem("destf_ready")
            dest_ready = sem("dest_ready")
            returned = [sem(f"returned{j}") for j in range(2)]
            summed = sem("summed_returned")
            added = sem("added_returned")
            stored = sem("stored")
            passed2 = sem("passed_a_wait2")

            def reach(eng, s, n, r, per, apart=False):
                if isinstance(r, int):
                    if n > 0:
                        eng.wait_ge(s, n)
                else:
                    assert n > 0
                    eng.wait_ge(s, n + per * r)
                    if apart:
                        eng.sem_inc(passed2, 1)

            def tiles(eng, step):
                first = 6
                turns = (PAIRS - 2 - first) // 4
                for i in range(first):
                    step(i, 0)
                with eng.Fori(0, turns) as r:
                    for i in range(first, first + 4):
                        step(i, r)
                for i in range(first + 4 * turns, PAIRS + DEPTH):
                    step(i, 0)

            def pair(p):
                return 0 <= p < PAIRS

            FIRST = 4

            block2 = two.enter_context(nc.Block())

            @block2.sync
            def _(sp):
                sp.dma_start(WD[:, 0:SHARED, :], down_t[:, 0:SHARED, :]).then_inc(shared_full, 16)
                sp.dma_start(WD[:, SHARED:UNITS, :], down_t[:, SHARED:UNITS, :]).then_inc(down_full, 16)
                for j in range(GROUP):
                    sp.wait_ge(send_full[j], 16 * (NB - 1))
                for dst, src in ((EI, expert_ids), (TI, tile_ids), (TS, tile_starts), (ROWI, row_ids)):
                    sp.dma_start(dst[:, :], src).then_inc(consts_full, 16)
                for j in range(GROUP):
                    sp.wait_ge(sent[j], 32 * NB)
                sp.wait_ge(table_ready, 1)

                def load(p, r):
                    reach(sp, tt_done, p - 3, r, 4, apart=True)
                    reach(sp, destf_ready, p - 3, r, 4, apart=True)
                    for k in range(2):
                        row = sp.value_load(TROW[0:1, bass.ds(2 * p + k + 8 * r, 1)], min_val=0,
                                            max_val=E * R - TILE)
                        sp.dma_start(XT[:, p % 4, k, :], token_rows[bass.ds(row, TILE), :])\
                            .then_inc(tile_full[p % 4], 16)

                def step(i, r):
                    if pair(i + 2):
                        load(i + 2, r)

                load(0, 0)
                load(1, 0)
                tiles(sp, step)
                for j in range(2):
                    sp.wait_ge(ty_sent[j], 32 * PAIRS // 2)
                back = expert_rows.rearrange("(w b t) d -> t w b d", w=2, t=T)

                def fetch(n, r):
                    reach(sp, added, n - 1, r, 2)
                    for w in range(2):
                        sp.dma_start(YR[0:T, n % 2, w, :, :], back[:, w, bass.ds(GROUP * n + 2 * GROUP * r, GROUP), :])\
                            .then_inc(returned[n % 2], 16)

                def store(n, r):
                    reach(sp, added, n + 1, r, 2, apart=True)
                    rows = bass.ds(GROUP * n + 2 * GROUP * r, GROUP)
                    sp.dma_start(out_rows[:, rows, :], X[:, rows, :]).then_inc(stored, 16)

                fetch(0, 0)
                fetch(1, 0)
                with sp.Fori(0, (NB - 2) // 2) as r:
                    for n in range(2):
                        store(n, r)
                        fetch(n + 2, r)
                store(NB - 2, 0)
                store(NB - 1, 0)
                sp.wait_ge(stored, 16 * NB)

            @block2.gpsimd
            def _(pool):
                pool.wait_ge(slot_ready, 4 * (NB - 1))
                for j in range(GROUP):
                    send(j, SEND, SLOT)
                pool.wait_ge(slot_ready, 4 * NB)
                for j in range(GROUP):
                    send(j, SEND_LAST, SLOT_LAST)

                def step(i, r):
                    if pair(i - 4):
                        p = i - 4
                        reach(pool, ty_ready, p + 1, r, 4, apart=True)
                        reach(pool, dest_ready, p + 1, r, 4, apart=True)
                        for k in range(2):
                            nc.gpsimd.indirect_dma_start(
                                expert_rows, bass.IndirectOffsetOnAxis(ap=DEST[:, p % 4, k:k + 1], axis=0),
                                YO[:, p % 2, k, :], None, bounds_check=2 * R - 1, oob_is_err=False)\
                                .then_inc(ty_sent[p % 2], 16)

                tiles(pool, step)

                def sum_returned(n, r):
                    reach(pool, returned[n % 2], 32 * (n // 2 + 1), r, 32)
                    nc.gpsimd.tensor_tensor(YR[0:T, n % 2, 0, :, :], YR[0:T, n % 2, 0, :, :], YR[0:T, n % 2, 1, :, :],
                                            ALU.add).then_inc(summed, 1)

                with pool.Fori(0, NB // 2) as r:
                    for n in range(2):
                        sum_returned(n, r)

            @block2.scalar
            def _(act):
                def halves(n, r):
                    reach(act, g_done, 2 * (n - 1), r, 4)
                    reach(act, u_done, 2 * (n - 1), r, 4)
                    nc.scalar.activation(XSH[:, n % 2, :, :], XNT[:, :, bass.ds(n * BLOCK + 2 * BLOCK * r, BLOCK)],
                                         ACT.Copy).then_inc(xhi_ready, 1)

                def silu(n, u):
                    q = SHARED * n + u
                    reach(act, g_done, q + 1, 0, 0)
                    reach(act, h_ready, q - 1, 0, 0)
                    nc.scalar.activation(SG[:, u, :], g_ps[:, u, 0:BLOCK], ACT.Silu).then_inc(silu_ready, 1)

                def hidden_upper(n, u):
                    q = SHARED * n + u
                    reach(act, h_ready, q + 1, 0, 0)
                    reach(act, d_done, n, 0, 0)
                    nc.scalar.activation(HH[:, u, :], HF[:, u, :], ACT.Copy).then_inc(hhi_ready, 1)

                def block_step(n):
                    silu(n, 0)
                    if n < NB - 1:
                        halves(n + 1, 0)
                    hidden_upper(n, 0)
                    silu(n, 1)
                    hidden_upper(n, 1)

                def step(i, r):
                    if pair(i):
                        reach(act, tt_done, i + 1, r, 4)
                        reach(act, tg_done, i - 1, r, 4)
                        nc.scalar.activation(XTH[:, i % 2, :], d_ps[:, i % 2, :], ACT.Copy).then_inc(tthi_ready, 1)
                    if pair(i - 2):
                        p = i - 2
                        reach(act, tht_done, p + 1, r, 4)
                        reach(act, ty_done, p - 1, r, 4)
                        nc.scalar.activation(THH[:, p % 2, :], d_ps[:, 2 + p % 2, 0:2 * TILE], ACT.Copy)\
                            .then_inc(thhi_ready, 1)
                    if pair(i - 1):
                        p = i - 1
                        reach(act, tg_done, p + 1, r, 4)
                        reach(act, th_ready, p - 1, r, 4)
                        nc.scalar.activation(TSG[:, p % 2, :, :],
                                             g_ps[:, p % 2, :].rearrange("p (k g n) -> p k g n", k=2, g=2)[:, :, 0, :],
                                             ACT.Silu).then_inc(tsilu_ready, 1)
                    if pair(i - 3):
                        p = i - 3
                        reach(act, ty_done, p + 1, r, 4)
                        reach(act, ty_sent[p % 2], 32 * (p // 2), r, 64)
                        nc.scalar.activation(YO[:, p % 2, :, :].rearrange("p k d -> p (k d)"), u_ps[:, p % 2, :],
                                             ACT.Copy).then_inc(ty_ready, 1)

                halves(0, 0)
                act.wait_ge(shared_full, 16)
                for u in range(SHARED):
                    nc.scalar.activation(WDH[:, u, :], WD[:, u, :], ACT.Copy).then_inc(dhi_ready, 1)
                for n in range(FIRST):
                    block_step(n)
                    if n == 2:
                        act.wait_ge(down_full, 16)
                        act.wait_ge(mean_ready, 1)
                        for e in range(E):
                            nc.scalar.activation(WDH[:, SHARED + e, :], WD[:, SHARED + e, :], ACT.Copy,
                                                 scale=WM[:, e:e + 1]).then_inc(dhi_ready, 1)
                tiles(act, step)
                for n in range(FIRST, NB):
                    block_step(n)

            @block2.vector
            def _(dve):
                def halves(n, r):
                    reach(dve, xhi_ready, n + 1, r, 2)
                    nc.vector.tensor_tensor(XSL[:, n % 2, :, :], XNT[:, :, bass.ds(n * BLOCK + 2 * BLOCK * r, BLOCK)],
                                            XSH[:, n % 2, :, :].bitcast(F32), ALU.subtract).then_inc(xlo_ready, 1)

                def hidden(n, u):
                    q = SHARED * n + u
                    reach(dve, u_done, q + 1, 0, 0)
                    reach(dve, silu_ready, q + 1, 0, 0)
                    reach(dve, hlo_ready, q - 1, 0, 0)
                    reach(dve, hhi_ready, q - 1, 0, 0)
                    nc.vector.tensor_tensor(HF[:, u, :], u_ps[:, u, 0:BLOCK], SG[:, u, :], ALU.mult)\
                        .then_inc(h_ready, 1)

                def hidden_lower(n, u):
                    q = SHARED * n + u
                    reach(dve, hhi_ready, q + 1, 0, 0)
                    reach(dve, d_done, n, 0, 0)
                    nc.vector.tensor_tensor(HL[:, u, :], HF[:, u, :], HH[:, u, :].bitcast(F32), ALU.subtract)\
                        .then_inc(hlo_ready, 1)

                def finish(n, r):
                    reach(dve, d_done, n + 1, r, 2)
                    for j in range(2):
                        rows = bass.ds(GROUP * n + 2 * j + 2 * GROUP * r, 2)
                        nc.vector.tensor_tensor(X[:, rows, :], d_ps[0:T, j, :].rearrange("p (a d) -> p a d", d=D),
                                                X[:, rows, :], ALU.add).then_inc(fin_ready, 1)

                def add_returned(n):
                    dve.wait_ge(fin_ready, 2 * (n + 1))
                    dve.wait_ge(summed, n + 1)
                    rows = slice(GROUP * n, GROUP * (n + 1))
                    nc.vector.tensor_tensor(X[:, rows, :], YR[0:T, n % 2, 0, :, :], X[:, rows, :], ALU.add)\
                        .then_inc(added, 1)

                def block_step(n):
                    hidden(n, 0)
                    if n < NB - 1:
                        halves(n + 1, 0)
                    hidden_lower(n, 0)
                    hidden(n, 1)
                    if n > 0 and n != FIRST:
                        finish(n - 1, 0)
                    hidden_lower(n, 1)
                    if n >= FIRST:
                        add_returned(2 * (n - FIRST))
                    if FIRST <= n < NB - 1:
                        add_returned(2 * (n - FIRST) + 1)

                def step(i, r):
                    if pair(i):
                        reach(dve, tthi_ready, i + 1, r, 4)
                        reach(dve, tg_done, i - 1, r, 4)
                        nc.vector.tensor_tensor(XTL[:, i % 2, :], d_ps[:, i % 2, :], XTH[:, i % 2, :].bitcast(F32),
                                                ALU.subtract).then_inc(ttlo_ready, 1)
                    if pair(i - 2):
                        p = i - 2
                        reach(dve, thhi_ready, p + 1, r, 4)
                        reach(dve, ty_done, p - 1, r, 4)
                        nc.vector.tensor_tensor(THL[:, p % 2, :], d_ps[:, 2 + p % 2, 0:2 * TILE],
                                                THH[:, p % 2, :].bitcast(F32), ALU.subtract).then_inc(thlo_ready, 1)
                    if pair(i - 1):
                        p = i - 1
                        reach(dve, tsilu_ready, p + 1, r, 4)
                        reach(dve, tht_done, p - 1, r, 4)
                        nc.vector.tensor_tensor(TH[:, p % 2, :, :],
                                                g_ps[:, p % 2, :].rearrange("p (k g n) -> p k g n", k=2, g=2)[:, :, 1, :],
                                                TSG[:, p % 2, :, :], ALU.mult).then_inc(th_ready, 1)
                    if pair(i):
                        at = bass.ds(2 * i + 8 * r, 2)
                        reach(dve, tile_full[i % 4], 32 * (i // 4 + 1), r, 32)
                        reach(dve, destf_ready, i - 1, r, 4)
                        nc.vector.tensor_tensor(SECOND[:, i % 2, :], XT[:, i % 4, :, D + 1], MINE[:, at], ALU.is_gt)\
                            .then_inc(second_ready, 1)
                    if pair(i - 1):
                        p = i - 1
                        reach(dve, second_ready, p + 1, r, 4)
                        reach(dve, dest_ready, p - 1, r, 4)
                        nc.vector.scalar_tensor_tensor(out=DESTF[:, p % 2, :], in0=SECOND[:, p % 2, :],
                                                       scalar=float(R), in1=XT[:, p % 4, :, D], op0=ALU.mult,
                                                       op1=ALU.add).then_inc(destf_ready, 1)
                    if pair(i - 2):
                        p = i - 2
                        reach(dve, destf_ready, p + 1, r, 4)
                        reach(dve, ty_sent[p % 2], 32 * (p // 2 - 1), r, 64)
                        nc.vector.tensor_tensor(DEST[:, p % 4, :], DESTF[:, p % 2, :],
                                                SKIP[:, bass.ds(2 * p + 8 * r, 2)], ALU.add).then_inc(dest_ready, 1)

                halves(0, 0)
                for u in range(SHARED):
                    dve.wait_ge(dhi_ready, u + 1)
                    nc.vector.tensor_tensor(WDL[:, u, :], WD[:, u, :], WDH[:, u, :].bitcast(F32),
                                            ALU.subtract).then_inc(dlo_ready, 1)
                rank(dve, NB - 2, 0)
                route(dve, NB - 2, 0)
                score(dve, NB - 1, 0)
                rank(dve, NB - 1, 0)
                block_step(0)
                place(dve, NB - 2, 0, COUNTS, SEND, SLOT)
                route(dve, NB - 1, 0)
                dve.wait_ge(route_ready, 4 * NB)
                nc.vector.tensor_reduce(PART[:, :, :], ROUTE[:, :, :, :].rearrange("p w b e -> p w e b"), AX.X,
                                        ALU.add).then_inc(part_ready, 1)
                block_step(1)
                place(dve, NB - 1, 0, COUNTS, SEND_LAST, SLOT_LAST)
                dve.wait_ge(tot_done, 1)
                nc.vector.tensor_copy(TOT[:, :, :], TOTALS.rearrange("p (w e) -> p w e", w=2)).then_inc(tot_ready, 1)
                dve.wait_ge(tot_ready, 1)
                nc.vector.tensor_scalar(CNT[:, :], TOT[:, 1, :], 1.0, None, ALU.max).then_inc(mean_chain, 1)
                dve.wait_ge(mean_chain, 1)
                nc.vector.reciprocal(INV[:, :], CNT[:, :]).then_inc(mean_chain, 1)
                dve.wait_ge(mean_chain, 2)
                nc.vector.tensor_tensor(WM[:, :], TOT[:, 0, :], INV[:, :], ALU.mult).then_inc(mean_ready, 1)

                def over_tiles(a):
                    return a.unsqueeze(1).broadcast_to([128, NT, E])

                count = TOT[:, 1, :]
                tile = TI[:, :].unsqueeze(2).broadcast_to([128, NT, E])
                dve.wait_ge(consts_full, 64)
                nc.vector.tensor_tensor(HAS[:, :, :], count.unsqueeze(2).broadcast_to([128, E, NK]),
                                        TS[:, :].unsqueeze(1).broadcast_to([128, E, NK]), ALU.is_gt).then_inc(plan, 1)
                nc.vector.tensor_scalar(FL[:, :], count, -float(TILE), None, ALU.add).then_inc(plan, 1)
                dve.wait_ge(plan, 2)
                nc.vector.tensor_reduce(TC[:, :], HAS[:, :, :], AX.X, ALU.add).then_inc(plan, 1)
                dve.wait_ge(plan, 3)
                nc.vector.tensor_tensor(TCB[:, :, :], BEFORE[:, :, :], TC[:, :].unsqueeze(1).broadcast_to([128, E, E]),
                                        ALU.mult).then_inc(plan, 1)
                dve.wait_ge(plan, 4)
                nc.vector.tensor_reduce(TF[:, :], TCB[:, :, :], AX.X, ALU.add).then_inc(plan, 1)
                dve.wait_ge(plan, 5)
                nc.vector.tensor_tensor(TE[:, :], TF[:, :], TC[:, :], ALU.add).then_inc(plan, 1)
                nc.vector.tensor_scalar(FL[:, :], FL[:, :], 0.0, None, ALU.max).then_inc(plan, 1)
                dve.wait_ge(plan, 7)
                nc.vector.tensor_tensor(PAST[:, :, :], over_tiles(TE[:, :]), tile, ALU.is_le).then_inc(plan, 1)
                dve.wait_ge(plan, 8)
                nc.vector.tensor_reduce(TX[:, :], PAST[:, :, :], AX.X, ALU.add).then_inc(plan, 1)
                dve.wait_ge(plan, 9)
                nc.vector.tensor_scalar(TX[:, :], TX[:, :], float(E - 1), None, ALU.min).then_inc(plan, 1)
                block_step(2)
                dve.wait_ge(plan, 10)
                nc.vector.tensor_tensor(OH[:, :, :], TX[:, :].unsqueeze(2).broadcast_to([128, NT, E]),
                                        over_tiles(EI[:, :]), ALU.is_equal).then_inc(plan, 1)
                dve.wait_ge(plan, 11)
                nc.vector.tensor_tensor(A1[:, :, :], OH[:, :, :], over_tiles(TF[:, :]), ALU.mult).then_inc(plan, 1)
                nc.vector.tensor_tensor(A2[:, :, :], OH[:, :, :], over_tiles(FL[:, :]), ALU.mult).then_inc(plan, 1)
                dve.wait_ge(plan, 13)
                nc.vector.tensor_reduce(ROWF[:, :], A1[:, :, :], AX.X, ALU.add).then_inc(plan, 1)
                nc.vector.tensor_reduce(OVER[:, :], A2[:, :, :], AX.X, ALU.add).then_inc(plan, 1)
                dve.wait_ge(plan, 15)
                nc.vector.tensor_tensor(ROWF[:, :], TI[:, :], ROWF[:, :], ALU.subtract).then_inc(plan, 1)
                dve.wait_ge(plan, 16)
                nc.vector.tensor_scalar(ROWF[:, :], ROWF[:, :], float(TILE), None, ALU.mult).then_inc(plan, 1)
                dve.wait_ge(plan, 17)
                nc.vector.tensor_tensor(MINE[:, :], ROWF[:, :], OVER[:, :], ALU.min).then_inc(plan, 1)
                dve.wait_ge(plan, 18)
                nc.vector.tensor_tensor(OVER[:, :], ROWF[:, :], MINE[:, :], ALU.subtract).then_inc(plan, 1)
                dve.wait_ge(plan, 19)
                nc.vector.scalar_tensor_tensor(out=ROWF[:, :], in0=TX[:, :], scalar=float(R), in1=MINE[:, :],
                                               op0=ALU.mult, op1=ALU.add).then_inc(plan, 1)
                dve.wait_ge(plan, 20)
                nc.vector.tensor_copy(TROW[:, :], ROWF[:, :]).then_inc(table_ready, 1)
                nc.vector.tensor_scalar(MINE[:, :], ROWF[:, :], ROWI[:, 0:1], None, ALU.add).then_inc(table_ready, 1)
                nc.vector.tensor_scalar(SKIP[:, :], OVER[:, :], ROWI[:, 0:1], NOWHERE, ALU.is_gt, ALU.mult)\
                    .then_inc(plan, 1)
                nc.vector.memset(TABF[:, :], 0.0).then_inc(plan, 1)
                pairs = TX[:, :].rearrange("p (i k) -> p i k", k=2)
                nc.vector.scalar_tensor_tensor(out=PK[:, :], in0=pairs[:, :, 1], scalar=float(1 << FIELD),
                                               in1=pairs[:, :, 0], op0=ALU.mult, op1=ALU.add).then_inc(plan, 1)
                dve.wait_ge(plan, 23)
                nc.vector.tensor_scalar(PK[:, :], PK[:, :], float(SHARED + (SHARED << FIELD)), None, ALU.add)\
                    .then_inc(plan, 1)
                dve.wait_ge(plan, 24)
                nc.vector.tensor_scalar(TABF[:, 1:PAIRS + 1], PK[:, :], float(GATE_UP), None, ALU.mult)\
                    .then_inc(plan, 1)
                dve.wait_ge(plan, 25)
                nc.vector.scalar_tensor_tensor(out=TABF[:, 3:PAIRS + 3], in0=PK[:, :],
                                               scalar=float(GATE_UP << 2 * FIELD), in1=TABF[:, 3:PAIRS + 3],
                                               op0=ALU.mult, op1=ALU.add).then_inc(plan, 1)
                dve.wait_ge(plan, 26)
                nc.vector.tensor_copy(TAB[:, :], TABF[:, :]).then_inc(table_ready, 1)

                dve.wait_ge(mean_ready, 1)
                for e in range(E):
                    u = SHARED + e
                    dve.wait_ge(dhi_ready, u + 1)
                    nc.vector.scalar_tensor_tensor(out=WDL[:, u, :], in0=WD[:, u, :],
                                                   scalar=WM[:, e:e + 1], in1=WDH[:, u, :].bitcast(F32),
                                                   op0=ALU.mult, op1=ALU.subtract).then_inc(dlo_ready, 1)
                block_step(3)
                finish(FIRST - 1, 0)
                dve.wait_ge(table_ready, 3)
                dve.wait_ge(plan, 26)
                tiles(dve, step)

                for n in range(FIRST, NB):
                    block_step(n)
                finish(NB - 1, 0)
                add_returned(NB - 1)

            @block2.tensor
            def _(pe):
                def gate_up(n, u, r):
                    q = SHARED * n + u
                    if u == 0:
                        reach(pe, xhi_ready, n + 1, r, 2)
                        reach(pe, xlo_ready, n + 1, r, 2)
                    for g, ps, free, done in ((0, g_ps, silu_ready, g_done), (1, u_ps, h_ready, u_done)):
                        reach(pe, free, q - 1, r, 4)
                        k = 0
                        for kt in range(DT):
                            at = (u * DT + kt) * 2 + g
                            for w, v in ((GUH, XSH), (GUH, XSL), (GUL, XSH)):
                                last = nc.tensor.matmul(ps[:, u, 0:BLOCK], w[:, at, :], v[:, n % 2, kt, :],
                                                        start=k == 0, stop=k == 3 * DT - 1)
                                k += 1
                        last.then_inc(done, 1)

                def down(n, r):
                    reach(pe, hlo_ready, SHARED * (n + 1), r, 4)
                    reach(pe, hhi_ready, SHARED * (n + 1), r, 4)
                    reach(pe, fin_ready, 2 * n, r, 4)
                    for j in range(GROUP):
                        k = 0
                        for u in range(SHARED):
                            for h, w in ((HH, WDH), (HH, WDL), (HL, WDH)):
                                last = nc.tensor.matmul(d_ps[0:T, j // 2, (j % 2) * D:(j % 2 + 1) * D],
                                                        h[:, u, j * T:(j + 1) * T], w[:, u, :],
                                                        start=k == 0, stop=k == 3 * SHARED - 1)
                                k += 1
                    last.then_inc(d_done, 1)

                guh, gul, wdh, wdl = (w.rearrange("p a n -> p (a n)") for w in
                                      (GUH[:, :, :], GUL[:, :, :], WDH[:, :, :], WDL[:, :, :]))

                def offset(table, field, size):
                    shift = field * FIELD + (GATE_UP.bit_length() - size.bit_length())
                    return nc.s_assert_within((table >> shift if shift else table) & (15 * size), 0,
                                              (UNITS - 1) * size,
                                              skip_runtime_bounds_check_because="the table is made of units")

                def step(i, r):
                    if pair(i - 1) or pair(i - 3):
                        table = nc.values_load(TAB[0:1, bass.ds(i + 4 * r, 1)], engines=(pe.engine,), min_val=0,
                                               max_val=(GATE_UP << 4 * FIELD) - 1,
                                               skip_runtime_bounds_check_because="it has four fields")
                    if pair(i):
                        reach(pe, tile_full[i % 4], 32 * (i // 4 + 1), r, 32)
                        reach(pe, ttlo_ready, i - 1, r, 4)
                        for k in range(2):
                            for kt in range(DT):
                                last = nc.tensor.transpose(d_ps[:, i % 2, (k * DT + kt) * TILE:(k * DT + kt + 1) * TILE],
                                                           XT[:, i % 4, k, kt * 128:(kt + 1) * 128], ID[:, :])
                        last.then_inc(tt_done, 1)
                    if pair(i - 2):
                        p = i - 2
                        reach(pe, th_ready, p + 1, r, 4)
                        reach(pe, thlo_ready, p - 1, r, 4)
                        for k in range(2):
                            last = nc.tensor.transpose(d_ps[:, 2 + p % 2, k * TILE:(k + 1) * TILE],
                                                       TH[:, p % 2, k, :], ID[:, :])
                        last.then_inc(tht_done, 1)
                    if pair(i - 1):
                        p = i - 1
                        reach(pe, tthi_ready, p + 1, r, 4)
                        reach(pe, ttlo_ready, p + 1, r, 4)
                        reach(pe, th_ready, p - 1, r, 4)
                        for k in range(2):
                            at = offset(table, k, GATE_UP)
                            n = 0
                            for kt in range(DT):
                                cols = slice((k * DT + kt) * TILE, (k * DT + kt + 1) * TILE)
                                for w, v in ((guh, XTH), (gul, XTH), (guh, XTL)):
                                    last = nc.tensor.matmul(g_ps[:, p % 2, k * 256:(k + 1) * 256], v[:, p % 2, cols],
                                                            w[:, bass.ds(at + kt * 2 * TILE, 2 * TILE)],
                                                            start=n == 0, stop=n == 3 * DT - 1)
                                    n += 1
                        last.then_inc(tg_done, 1)
                    if pair(i - 3):
                        p = i - 3
                        if p == 0:
                            pe.wait_ge(dlo_ready, UNITS)
                        reach(pe, thhi_ready, p + 1, r, 4)
                        reach(pe, thlo_ready, p + 1, r, 4)
                        reach(pe, ty_ready, p - 1, r, 4)
                        for k in range(2):
                            at = offset(table, 2 + k, D)
                            for n, (w, v) in enumerate(((wdh, THH), (wdl, THH), (wdh, THL))):
                                last = nc.tensor.matmul(u_ps[:, p % 2, k * D:(k + 1) * D],
                                                        v[:, p % 2, k * TILE:(k + 1) * TILE],
                                                        w[:, bass.ds(at, D)],
                                                        start=n == 0, stop=n == 2)
                        last.then_inc(ty_done, 1)

                def block_step(n):
                    gate_up(n, 0, 0)
                    if n == 1:
                        pe.wait_ge(dlo_ready, SHARED)
                    if n > 0 and n != FIRST:
                        down(n - 1, 0)
                    gate_up(n, 1, 0)
                    if n < 2:
                        pe.wait_ge(route_ready, 4 * (NB - 2 + n) + 1)
                        pe.wait_ge(off_ready, NB - 1 + n)
                        count_rows(COUNTS).then_inc(off_done, 1)
                    if n == 1:
                        pe.wait_ge(part_ready, 1)
                        nc.tensor.matmul(TOTALS, ONES[:, :], PART[:, :, :].rearrange("p w e -> p (w e)"),
                                         start=True, stop=True).then_inc(tot_done, 1)

                for n in range(FIRST):
                    block_step(n)
                down(FIRST - 1, 0)

                pe.wait_ge(fin_ready, 2 * FIRST)
                pe.wait_ge(off_ready, NB + 1)
                pe.wait_ge(tot_ready, 1)
                pe.wait_ge(h_ready, SHARED * FIRST)
                pe.wait_ge(table_ready, 3)
                tiles(pe, step)

                pe.wait_ge(th_ready, PAIRS)
                pe.wait_ge(ty_ready, PAIRS)
                for n in range(FIRST, NB):
                    block_step(n)
                down(NB - 1, 0)


def kernel(x, ctx_768, L0_xattn_ln1_g, L0_xattn_ln1_b, L0_xattn_ln2_g, L0_xattn_ln2_b, L0_xattn_Wq, L0_xattn_bq,
           L0_xattn_Wk, L0_xattn_bk, L0_xattn_Wv, L0_xattn_bv, L0_xattn_Wo, L0_xattn_bo, L0_ffn_gate_w,
           L0_ffn_lb_bias, L0_ffn_expert_gate_w, L0_ffn_expert_up_w, L0_ffn_expert_down_w, L0_ffn_shared_gate_w,
           L0_ffn_shared_up_w, L0_ffn_shared_down_w):
    import numpy as np
    import concourse.bacc as bacc
    from concourse.bass_utils import run_bass_kernel_spmd

    a = np.asarray
    T = x.shape[1]
    E = L0_ffn_lb_bias.shape[0]
    tokens = x.shape[0] * T
    tiles = 2 * tokens // 128 + E
    rows = lambda v: np.broadcast_to(v.astype(np.float32), (128, v.shape[0]))
    cols = lambda v: a(v).reshape(2, 128).T
    halves = lambda w: a(w).reshape(-1, 128, a(w).shape[-1])
    gate = np.concatenate([halves(L0_ffn_shared_gate_w), a(L0_ffn_expert_gate_w)])
    up = np.concatenate([halves(L0_ffn_shared_up_w), a(L0_ffn_expert_up_w)])
    gate_up = np.stack([gate, up], axis=1).reshape(-1, 2, 128, 2, 128).transpose(4, 0, 3, 1, 2).reshape(128, -1)
    shared_down = a(L0_ffn_shared_down_w).T.reshape(2, 128, -1)
    down = np.concatenate([shared_down, a(L0_ffn_expert_down_w).transpose(0, 2, 1)]).transpose(1, 0, 2)
    ins = {
        "x": a(x), "ctx_in": a(ctx_768),
        "wq_t": a(L0_xattn_Wq).T, "wq": a(L0_xattn_Wq), "wk_t": a(L0_xattn_Wk).T, "wk": a(L0_xattn_Wk),
        "wv_t": a(L0_xattn_Wv).T, "wv": a(L0_xattn_Wv), "wo": a(L0_xattn_Wo),
        "g2_rows": np.broadcast_to(a(L0_xattn_ln2_g), (128, 192)),
        "columns": np.stack([cols(v) for v in (L0_xattn_ln1_g, L0_xattn_ln1_b, L0_xattn_bq, L0_xattn_bk,
                                               L0_xattn_bv)], axis=1),
        "b2_columns": a(L0_xattn_ln2_b).reshape(2, 96).T,
        "bo": a(L0_xattn_bo).reshape(1, -1),
        "gate_w_t": a(L0_ffn_gate_w).T,
        "lb_rows": np.broadcast_to(a(L0_ffn_lb_bias), (T, 8)),
        "gate_up_t": gate_up, "down_t": down,
        "region_rows": rows(np.arange(E) * tokens), "expert_ids": rows(np.arange(E)),
        "tile_ids": rows(np.arange(tiles)), "tile_starts": rows(np.arange(0, tokens, 128)),
        "token_ids": np.arange(tokens).reshape(-1, T).T.astype(np.float32),
        "row_ids": np.arange(128).reshape(128, 1).astype(np.float32),
    }
    nc = bacc.Bacc("TRN2", target_bir_lowering=False, num_devices=1)
    arrays, args = {}, {}
    for name, v in ins.items():
        v = np.ascontiguousarray(v)
        arrays[f"in_{name}"] = v
        args[name] = nc.dram_tensor(f"in_{name}", v.shape, mybir.dt.from_np(v.dtype), kind="ExternalInput").ap()
    out = nc.dram_tensor("out_0", x.shape, F32, kind="ExternalOutput").ap()
    token_rows = nc.dram_tensor("token_rows", [E * tokens, x.shape[2] + 2], F32, kind="Internal").ap()
    expert_rows = nc.dram_tensor("expert_rows", [2 * tokens, x.shape[2]], F32, kind="Internal").ap()
    attention_and_experts(nc, **args, expert_rows=expert_rows, token_rows=token_rows, out=out)
    r = run_bass_kernel_spmd(nc, [arrays], core_ids=[0])
    return r.results[0]["out_0"]
```
